# Optimizing a Trainium2 kernel written in Bass

```python
import numpy as np
import jax
import jax.numpy as jnp

def _softmax(x, axis=-1):
    return jax.nn.softmax(x, axis=axis)

def _gelu(x):
    return jax.nn.gelu(x, approximate=True)

def _silu(x):
    return jax.nn.silu(x)

def _sigmoid(x):
    return jax.nn.sigmoid(x)

def _layernorm(x, axis=-1, eps=1e-05):
    m = jnp.mean(x, axis=axis, keepdims=True)
    v = jnp.var(x, axis=axis, keepdims=True)
    return (x - m) / jnp.sqrt(v + eps)

def _scatter_add(tgt, idx, src, axis=0):
    return tgt.at[idx].add(src)

def _segment_sum(src, seg, n):
    return jax.ops.segment_sum(src, seg, n)
kernel_name = 'mk_xattn_ffn_d2_seqx_r8_c159d5'

def setup_inputs(seed: int=0):
    np.random.seed(seed)
    _w = jnp.asarray

    def _rec_inputs():
        import jax
        import jax.numpy as jnp
        _rk = jax.random.key(seed)
        x = 7.22e-05 + 1 * jax.random.normal(jax.random.fold_in(_rk, 1), (32, 64, 512), jnp.float32)
        _lenS = 64 - jax.random.randint(jax.random.fold_in(_rk, 7), (32,), 0, max(1, 64 // 4) + 1, jnp.int32)
        _lenS2 = 64 - jax.random.randint(jax.random.fold_in(_rk, 8), (32,), 0, max(1, 64 // 4) + 1, jnp.int32)
        _ctx_4096P = jax.random.normal(jax.random.fold_in(_rk, 11), (32, 16, 512), jnp.float32)
        _ctx_4096c = jax.random.dirichlet(jax.random.fold_in(_rk, 511), 0.3 * jnp.ones((16,), jnp.float32), (32, 64))
        _ctx_4096t = jnp.einsum('bsk,bkd->bsd', _ctx_4096c, _ctx_4096P)
        _ctx_4096t = _ctx_4096t * jax.lax.rsqrt(jnp.mean(jnp.square(_ctx_4096t)) + 1e-12) * 0.953939
        ctx_4096 = 4.13588e-05 + 0.999923 * (_ctx_4096t + 0.3 * jax.random.normal(jax.random.fold_in(_rk, 611), (32, 64, 512), jnp.float32))
        _validS = jnp.arange(64)[None, :] < _lenS[:, None]
        _validS2 = jnp.arange(64)[None, :] < _lenS2[:, None]
        _causal = jnp.tril(jnp.ones((64, 64), dtype=bool))
        mask_BxSxS2_ff1 = jnp.where(jnp.ones((32, 64, 64), dtype=bool), 1.0, 0.0).astype(jnp.float32)
        mask_1x1xSxS2_ff0 = jnp.where(jnp.ones((1, 1, 64, 64), dtype=bool), 0.0, -1000000000.0).astype(jnp.float32)
        return (x, ctx_4096, mask_BxSxS2_ff1, mask_1x1xSxS2_ff0)
    x, ctx_4096, mask_BxSxS2_ff1, mask_1x1xSxS2_ff0 = _rec_inputs()

    def _L0_xattn_setup():
        import jax, jax.numpy as jnp
        import numpy as np
        N_Q_HEADS = 32
        N_KV_HEADS = 8
        D_MODEL = 512
        D_K = 128
        D_V = 128
        ROPE_BASE = 10000.0

        def _rope(x):
            d = x.shape[-1]
            s = x.shape[2]
            inv_freq = 1.0 / ROPE_BASE ** (jnp.arange(0, d, 2, dtype=jnp.float32) / d)
            ang = jnp.arange(s, dtype=jnp.float32)[:, None] * inv_freq[None, :]
            cos = jnp.concatenate([jnp.cos(ang), jnp.cos(ang)], axis=-1)[None, None]
            sin = jnp.concatenate([jnp.sin(ang), jnp.sin(ang)], axis=-1)[None, None]
            x1, x2 = (x[..., :d // 2], x[..., d // 2:])
            rot = jnp.concatenate([-x2, x1], axis=-1)
            return x * cos + rot * sin
        key = jax.random.key(seed)
        ks = jax.random.split(key, 8)
        bs, s = (2, 128)
        inp = {'query': jax.random.normal(ks[0], (bs, s, D_MODEL), dtype=jnp.float32), 'key': jax.random.normal(ks[1], (bs, s, D_MODEL), dtype=jnp.float32), 'value': jax.random.normal(ks[2], (bs, s, D_MODEL), dtype=jnp.float32), 'mask': jnp.ones((bs, s, s), dtype=jnp.float32), 'wq': jax.random.normal(ks[3], (D_MODEL, N_Q_HEADS * D_K), dtype=jnp.float32) * 0.02, 'wk': jax.random.normal(ks[4], (D_MODEL, N_KV_HEADS * D_K), dtype=jnp.float32) * 0.02, 'wv': jax.random.normal(ks[5], (D_MODEL, N_KV_HEADS * D_V), dtype=jnp.float32) * 0.02, 'wo': jax.random.normal(ks[6], (N_Q_HEADS * D_V, D_MODEL), dtype=jnp.float32) * 0.02}
        return inp
    _L0_xattn_all = _L0_xattn_setup()
    _L0_xattn_in = {k: v for k, v in _L0_xattn_all.items() if k in ('wq', 'wk', 'wv', 'wo')}
    del _L0_xattn_all

    def _L0_ffn_setup():
        import jax, jax.numpy as jnp
        import numpy as np
        HIDDEN = 512
        INTER = 1376
        GROUP = 128
        B, S = (4, 256)
        NIB = jnp.uint32(15)

        def _pack_rows(nib):
            r = nib.reshape(-1, 8, nib.shape[-1])
            shifts = (jnp.arange(8, dtype=jnp.uint32) * 4)[None, :, None]
            return jnp.sum(r << shifts, axis=1, dtype=jnp.uint32)

        def _pack_cols(nib):
            r = nib.reshape(nib.shape[0], -1, 8)
            shifts = (jnp.arange(8, dtype=jnp.uint32) * 4)[None, None, :]
            return jnp.sum(r << shifts, axis=2, dtype=jnp.uint32)

        def _dequant(qw, qz, sc, g_idx):
            shifts = jnp.arange(8, dtype=jnp.uint32) * 4
            wq = qw[:, None, :] >> shifts[None, :, None] & NIB
            wq = wq.reshape(-1, qw.shape[1]).astype(jnp.float32)
            zq = qz[:, :, None] >> shifts[None, None, :] & NIB
            zq = zq.reshape(qz.shape[0], -1).astype(jnp.float32) + 1.0
            return sc[g_idx] * (wq - zq[g_idx])
        key = jax.random.key(seed)
        ks = jax.random.split(key, 7)
        n_groups = HIDDEN // GROUP
        n_groups_d = INTER // GROUP
        x = jax.random.normal(ks[0], (B, S, HIDDEN), jnp.float32)
        nib_w_gu = jax.random.randint(ks[1], (HIDDEN, 2 * INTER), 0, 16).astype(jnp.uint32)
        nib_z_gu = jax.random.randint(ks[2], (n_groups, 2 * INTER), 0, 15).astype(jnp.uint32)
        qweight_gu = _pack_rows(nib_w_gu)
        qzeros_gu = _pack_cols(nib_z_gu)
        scales_gu = jax.random.uniform(ks[3], (n_groups, 2 * INTER), jnp.float32, 0.005, 0.02)
        g_idx_gu = jnp.arange(HIDDEN, dtype=jnp.int32) // GROUP
        nib_w_d = jax.random.randint(ks[4], (INTER, HIDDEN), 0, 16).astype(jnp.uint32)
        nib_z_d = jax.random.randint(ks[5], (n_groups_d, HIDDEN), 0, 15).astype(jnp.uint32)
        qweight_down = _pack_rows(nib_w_d)
        qzeros_down = _pack_cols(nib_z_d)
        scales_down = jax.random.uniform(ks[6], (n_groups_d, HIDDEN), jnp.float32, 0.005, 0.02)
        g_idx_down = jnp.arange(INTER, dtype=jnp.int32) // GROUP
        return {'x': x, 'qweight_gu': qweight_gu, 'qzeros_gu': qzeros_gu, 'scales_gu': scales_gu, 'g_idx_gu': g_idx_gu, 'qweight_down': qweight_down, 'qzeros_down': qzeros_down, 'scales_down': scales_down, 'g_idx_down': g_idx_down}
    _L0_ffn_all = _L0_ffn_setup()
    _L0_ffn_in = {k: v for k, v in _L0_ffn_all.items() if k in ('qweight_gu', 'qzeros_gu', 'scales_gu', 'g_idx_gu', 'qweight_down', 'qzeros_down', 'scales_down', 'g_idx_down')}
    del _L0_ffn_all

    def _L1_xattn_setup():
        import jax, jax.numpy as jnp
        import numpy as np
        NUM_HEADS = 32
        NUM_KV_HEADS = 8
        HEAD_DIM = 128
        HIDDEN = 512
        EPS = 1e-05

        def rmsnorm(x, w, eps=EPS):
            xf = x.astype(jnp.float32)
            var = jnp.mean(xf * xf, axis=-1, keepdims=True)
            return w * (xf * jax.lax.rsqrt(var + eps)).astype(x.dtype)
        key = jax.random.key(seed)
        ks = jax.random.split(key, 10)
        B, Q, KV = (1, 128, 6404)
        s = 1.0 / np.sqrt(HIDDEN)
        return {'hidden_states': jax.random.normal(ks[0], (B, Q, HIDDEN), jnp.float32), 'cross_attention_states': jax.random.normal(ks[1], (B, KV, HIDDEN), jnp.float32), 'attention_mask': jnp.zeros((B, 1, Q, KV), jnp.float32), 'q_proj_w': jax.random.normal(ks[2], (NUM_HEADS * HEAD_DIM, HIDDEN), jnp.float32) * s, 'k_proj_w': jax.random.normal(ks[3], (NUM_KV_HEADS * HEAD_DIM, HIDDEN), jnp.float32) * s, 'v_proj_w': jax.random.normal(ks[4], (NUM_KV_HEADS * HEAD_DIM, HIDDEN), jnp.float32) * s, 'o_proj_w': jax.random.normal(ks[5], (HIDDEN, NUM_HEADS * HEAD_DIM), jnp.float32) * s, 'q_norm_w': jnp.ones((HEAD_DIM,), jnp.float32), 'k_norm_w': jnp.ones((HEAD_DIM,), jnp.float32)}
    _L1_xattn_all = _L1_xattn_setup()
    _L1_xattn_in = {k: v for k, v in _L1_xattn_all.items() if k in ('q_proj_w', 'k_proj_w', 'v_proj_w', 'o_proj_w', 'q_norm_w', 'k_norm_w')}
    del _L1_xattn_all

    def _L1_ffn_setup():
        import jax, jax.numpy as jnp
        import numpy as np
        HID, BOT, RDIM, NSLOT, K, VB = (512, 64, 48, 128, 8, 32)
        TAU_LOW, TAU_HIGH, EARLY_EXIT = (0.5, 2.0, 0.05)

        def _uncertainty(h, Wu1, bu1, Wu2, bu2):
            var = jnp.var(h, axis=-1)
            log_var = jnp.log1p(var)
            norm_var = log_var / (jnp.mean(log_var) + 1e-06)
            learned = (jax.nn.gelu(h @ Wu1.T + bu1) @ Wu2.T + bu2)[..., 0]
            return jnp.clip(norm_var * 0.5 + jax.nn.sigmoid(learned) * 2.5, 0.0, 5.0)
        key = jax.random.key(seed)
        ks = jax.random.split(key, 12)
        B, S = (2, 256)
        return {'hidden_states': jax.random.normal(ks[0], (B, S, HID), dtype=jnp.float32), 'Wq': jax.random.normal(ks[1], (BOT, HID), dtype=jnp.float32) / np.sqrt(HID), 'Wr': jax.random.normal(ks[2], (RDIM, BOT), dtype=jnp.float32) / np.sqrt(BOT), 'aux_keys': jax.random.normal(ks[3], (NSLOT, BOT), dtype=jnp.float32) * 0.01, 'aux_values': jax.random.normal(ks[4], (NSLOT, HID), dtype=jnp.float32) * 0.02, 'Wvd': jax.random.normal(ks[5], (VB, HID), dtype=jnp.float32) * 0.1 / np.sqrt(HID), 'Wvu': jax.random.normal(ks[6], (HID, VB), dtype=jnp.float32) * 0.1 / np.sqrt(VB), 'Wu1': jax.random.normal(ks[7], (HID // 4, HID), dtype=jnp.float32) / np.sqrt(HID), 'bu1': jnp.zeros((HID // 4,), dtype=jnp.float32), 'Wu2': jax.random.normal(ks[8], (1, HID // 4), dtype=jnp.float32) * 0.01, 'bu2': jnp.zeros((1,), dtype=jnp.float32), 'gate_w1': jnp.float32(0.5), 'gate_bias': jnp.float32(-1.0), 'log_rel': jnp.zeros((NSLOT,), dtype=jnp.float32)}
    _L1_ffn_all = _L1_ffn_setup()
    _L1_ffn_in = {k: v for k, v in _L1_ffn_all.items() if k in ('Wq', 'Wr', 'aux_keys', 'aux_values', 'Wvd', 'Wvu', 'Wu1', 'bu1', 'Wu2', 'bu2', 'gate_w1', 'gate_bias', 'log_rel')}
    del _L1_ffn_all
    return {'x': x, 'ctx_4096': ctx_4096, 'mask_BxSxS2_ff1': mask_BxSxS2_ff1, 'mask_1x1xSxS2_ff0': mask_1x1xSxS2_ff0, 'L0_xattn_wq': _L0_xattn_in['wq'], 'L0_xattn_wk': _L0_xattn_in['wk'], 'L0_xattn_wv': _L0_xattn_in['wv'], 'L0_xattn_wo': _L0_xattn_in['wo'], 'L0_ffn_qweight_gu': _L0_ffn_in['qweight_gu'], 'L0_ffn_qzeros_gu': _L0_ffn_in['qzeros_gu'], 'L0_ffn_scales_gu': _L0_ffn_in['scales_gu'], 'L0_ffn_g_idx_gu': _L0_ffn_in['g_idx_gu'], 'L0_ffn_qweight_down': _L0_ffn_in['qweight_down'], 'L0_ffn_qzeros_down': _L0_ffn_in['qzeros_down'], 'L0_ffn_scales_down': _L0_ffn_in['scales_down'], 'L0_ffn_g_idx_down': _L0_ffn_in['g_idx_down'], 'L1_xattn_q_proj_w': _L1_xattn_in['q_proj_w'], 'L1_xattn_k_proj_w': _L1_xattn_in['k_proj_w'], 'L1_xattn_v_proj_w': _L1_xattn_in['v_proj_w'], 'L1_xattn_o_proj_w': _L1_xattn_in['o_proj_w'], 'L1_xattn_q_norm_w': _L1_xattn_in['q_norm_w'], 'L1_xattn_k_norm_w': _L1_xattn_in['k_norm_w'], 'L1_ffn_Wq': _L1_ffn_in['Wq'], 'L1_ffn_Wr': _L1_ffn_in['Wr'], 'L1_ffn_aux_keys': _L1_ffn_in['aux_keys'], 'L1_ffn_aux_values': _L1_ffn_in['aux_values'], 'L1_ffn_Wvd': _L1_ffn_in['Wvd'], 'L1_ffn_Wvu': _L1_ffn_in['Wvu'], 'L1_ffn_Wu1': _L1_ffn_in['Wu1'], 'L1_ffn_bu1': _L1_ffn_in['bu1'], 'L1_ffn_Wu2': _L1_ffn_in['Wu2'], 'L1_ffn_bu2': _L1_ffn_in['bu2'], 'L1_ffn_gate_w1': _L1_ffn_in['gate_w1'], 'L1_ffn_gate_bias': _L1_ffn_in['gate_bias'], 'L1_ffn_log_rel': _L1_ffn_in['log_rel']}

def reference(x, ctx_4096, mask_BxSxS2_ff1, mask_1x1xSxS2_ff0, L0_xattn_wq, L0_xattn_wk, L0_xattn_wv, L0_xattn_wo, L0_ffn_qweight_gu, L0_ffn_qzeros_gu, L0_ffn_scales_gu, L0_ffn_g_idx_gu, L0_ffn_qweight_down, L0_ffn_qzeros_down, L0_ffn_scales_down, L0_ffn_g_idx_down, L1_xattn_q_proj_w, L1_xattn_k_proj_w, L1_xattn_v_proj_w, L1_xattn_o_proj_w, L1_xattn_q_norm_w, L1_xattn_k_norm_w, L1_ffn_Wq, L1_ffn_Wr, L1_ffn_aux_keys, L1_ffn_aux_values, L1_ffn_Wvd, L1_ffn_Wvu, L1_ffn_Wu1, L1_ffn_bu1, L1_ffn_Wu2, L1_ffn_bu2, L1_ffn_gate_w1, L1_ffn_gate_bias, L1_ffn_log_rel):
    import jax
    import jax.numpy as jnp

    def _L0_xattn_ref(query, key, value, mask, wq, wk, wv, wo):
        import jax, jax.numpy as jnp
        import numpy as np
        N_Q_HEADS = 32
        N_KV_HEADS = 8
        D_MODEL = 512
        D_K = 128
        D_V = 128
        ROPE_BASE = 10000.0

        def _rope(x):
            d = x.shape[-1]
            s = x.shape[2]
            inv_freq = 1.0 / ROPE_BASE ** (jnp.arange(0, d, 2, dtype=jnp.float32) / d)
            ang = jnp.arange(s, dtype=jnp.float32)[:, None] * inv_freq[None, :]
            cos = jnp.concatenate([jnp.cos(ang), jnp.cos(ang)], axis=-1)[None, None]
            sin = jnp.concatenate([jnp.sin(ang), jnp.sin(ang)], axis=-1)[None, None]
            x1, x2 = (x[..., :d // 2], x[..., d // 2:])
            rot = jnp.concatenate([-x2, x1], axis=-1)
            return x * cos + rot * sin
        bs, s, _ = query.shape
        g = N_Q_HEADS // N_KV_HEADS
        q = (query @ wq).reshape(bs, s, N_Q_HEADS, D_K).transpose(0, 2, 1, 3)
        k = (key @ wk).reshape(bs, s, N_KV_HEADS, D_K).transpose(0, 2, 1, 3)
        v = (value @ wv).reshape(bs, s, N_KV_HEADS, D_V).transpose(0, 2, 1, 3)
        q = _rope(q)
        k = _rope(k)
        scale = jnp.sqrt(jnp.float32(D_K))
        qg = q.reshape(bs, N_KV_HEADS, g, s, D_K)
        scores = jnp.einsum('bhgqd,bhkd->bhgqk', qg, k) / scale
        masked = jnp.where(mask[:, None, None].astype(bool), scores, -1000000000.0)
        w = jax.nn.softmax(masked, axis=-1)
        out = jnp.einsum('bhgqk,bhkd->bhgqd', w, v)
        out = out.reshape(bs, N_Q_HEADS, s, D_V).transpose(0, 2, 1, 3).reshape(bs, s, N_Q_HEADS * D_V)
        return out @ wo

    def _L0_ffn_ref(x, qweight_gu, qzeros_gu, scales_gu, g_idx_gu, qweight_down, qzeros_down, scales_down, g_idx_down):
        import jax, jax.numpy as jnp
        import numpy as np
        HIDDEN = 512
        INTER = 1376
        GROUP = 128
        B, S = (4, 256)
        NIB = jnp.uint32(15)

        def _pack_rows(nib):
            r = nib.reshape(-1, 8, nib.shape[-1])
            shifts = (jnp.arange(8, dtype=jnp.uint32) * 4)[None, :, None]
            return jnp.sum(r << shifts, axis=1, dtype=jnp.uint32)

        def _pack_cols(nib):
            r = nib.reshape(nib.shape[0], -1, 8)
            shifts = (jnp.arange(8, dtype=jnp.uint32) * 4)[None, None, :]
            return jnp.sum(r << shifts, axis=2, dtype=jnp.uint32)

        def _dequant(qw, qz, sc, g_idx):
            shifts = jnp.arange(8, dtype=jnp.uint32) * 4
            wq = qw[:, None, :] >> shifts[None, :, None] & NIB
            wq = wq.reshape(-1, qw.shape[1]).astype(jnp.float32)
            zq = qz[:, :, None] >> shifts[None, None, :] & NIB
            zq = zq.reshape(qz.shape[0], -1).astype(jnp.float32) + 1.0
            return sc[g_idx] * (wq - zq[g_idx])
        w_gu = _dequant(qweight_gu, qzeros_gu, scales_gu, g_idx_gu)
        inter = jnp.einsum('bsh,hf->bsf', x, w_gu)
        gate, up = (inter[..., :INTER], inter[..., INTER:])
        h = jax.nn.silu(gate) * up
        w_d = _dequant(qweight_down, qzeros_down, scales_down, g_idx_down)
        return jnp.einsum('bsf,fh->bsh', h, w_d)

    def _L1_xattn_ref(hidden_states, cross_attention_states, attention_mask, q_proj_w, k_proj_w, v_proj_w, o_proj_w, q_norm_w, k_norm_w):
        import jax, jax.numpy as jnp
        import numpy as np
        NUM_HEADS = 32
        NUM_KV_HEADS = 8
        HEAD_DIM = 128
        HIDDEN = 512
        EPS = 1e-05

        def rmsnorm(x, w, eps=EPS):
            xf = x.astype(jnp.float32)
            var = jnp.mean(xf * xf, axis=-1, keepdims=True)
            return w * (xf * jax.lax.rsqrt(var + eps)).astype(x.dtype)
        B, Q, _ = hidden_states.shape
        KV = cross_attention_states.shape[1]
        n_rep = NUM_HEADS // NUM_KV_HEADS
        q = (hidden_states @ q_proj_w.T).reshape(B, Q, NUM_HEADS, HEAD_DIM).transpose(0, 2, 1, 3)
        k = (cross_attention_states @ k_proj_w.T).reshape(B, KV, NUM_KV_HEADS, HEAD_DIM).transpose(0, 2, 1, 3)
        v = (cross_attention_states @ v_proj_w.T).reshape(B, KV, NUM_KV_HEADS, HEAD_DIM).transpose(0, 2, 1, 3)
        q = rmsnorm(q, q_norm_w)
        k = jnp.repeat(k, n_rep, axis=1)
        v = jnp.repeat(v, n_rep, axis=1)
        k = rmsnorm(k, k_norm_w)
        scale = 1.0 / np.sqrt(HEAD_DIM)
        scores = jnp.einsum('bhqd,bhkd->bhqk', q, k) * scale + attention_mask
        attn = jax.nn.softmax(scores.astype(jnp.float32), axis=-1).astype(q.dtype)
        out = jnp.einsum('bhqk,bhkd->bhqd', attn, v)
        out = out.transpose(0, 2, 1, 3).reshape(B, Q, NUM_HEADS * HEAD_DIM)
        return out @ o_proj_w.T

    def _L1_ffn_ref(hidden_states, Wq, Wr, aux_keys, aux_values, Wvd, Wvu, Wu1, bu1, Wu2, bu2, gate_w1, gate_bias, log_rel):
        import jax, jax.numpy as jnp
        import numpy as np
        HID, BOT, RDIM, NSLOT, K, VB = (512, 64, 48, 128, 8, 32)
        TAU_LOW, TAU_HIGH, EARLY_EXIT = (0.5, 2.0, 0.05)

        def _uncertainty(h, Wu1, bu1, Wu2, bu2):
            var = jnp.var(h, axis=-1)
            log_var = jnp.log1p(var)
            norm_var = log_var / (jnp.mean(log_var) + 1e-06)
            learned = (jax.nn.gelu(h @ Wu1.T + bu1) @ Wu2.T + bu2)[..., 0]
            return jnp.clip(norm_var * 0.5 + jax.nn.sigmoid(learned) * 2.5, 0.0, 5.0)
        query = hidden_states @ Wq.T
        rq = query @ Wr.T
        rk = aux_keys @ Wr.T
        router_scores = jnp.einsum('bsr,nr->bsn', rq, rk) / np.sqrt(RDIM) + log_rel
        top_scores, top_idx = jax.lax.top_k(router_scores, K)
        sel_keys = aux_keys[top_idx]
        attn = jnp.einsum('bsd,bskd->bsk', query, sel_keys) / np.sqrt(BOT) + log_rel[top_idx]
        w = jax.nn.softmax(attn, axis=-1)
        sel_vals = aux_values[top_idx]
        aux_out = jnp.einsum('bsk,bskh->bsh', w, sel_vals)
        aux_out = aux_out @ Wvd.T @ Wvu.T
        u = _uncertainty(hidden_states, Wu1, bu1, Wu2, bu2)
        u_norm = jnp.clip((u - TAU_LOW) / (TAU_HIGH - TAU_LOW), 0.0, 1.0)
        gate = jax.nn.sigmoid(gate_w1 * u_norm + gate_bias)
        gate = jnp.where(gate < EARLY_EXIT, 0.0, gate)
        return hidden_states + gate[..., None] * aux_out
    x = x + _L0_xattn_ref(_layernorm(x, axis=-1), ctx_4096, ctx_4096, mask_BxSxS2_ff1, L0_xattn_wq, L0_xattn_wk, L0_xattn_wv, L0_xattn_wo)
    x = x + _L0_ffn_ref(_layernorm(x, axis=-1), L0_ffn_qweight_gu, L0_ffn_qzeros_gu, L0_ffn_scales_gu, L0_ffn_g_idx_gu, L0_ffn_qweight_down, L0_ffn_qzeros_down, L0_ffn_scales_down, L0_ffn_g_idx_down)
    x = x + _L1_xattn_ref(_layernorm(x, axis=-1), ctx_4096, mask_1x1xSxS2_ff0, L1_xattn_q_proj_w, L1_xattn_k_proj_w, L1_xattn_v_proj_w, L1_xattn_o_proj_w, L1_xattn_q_norm_w, L1_xattn_k_norm_w)
    x = x + _L1_ffn_ref(_layernorm(x, axis=-1), L1_ffn_Wq, L1_ffn_Wr, L1_ffn_aux_keys, L1_ffn_aux_values, L1_ffn_Wvd, L1_ffn_Wvu, L1_ffn_Wu1, L1_ffn_bu1, L1_ffn_Wu2, L1_ffn_bu2, L1_ffn_gate_w1, L1_ffn_gate_bias, L1_ffn_log_rel)
    return x

_drawn_inputs = setup_inputs


def setup_inputs(seed=0):
    import zlib

    import numpy as np

    out = dict(_drawn_inputs(seed))
    spreads = {'L1_xattn_q_norm_w': (1.0, 0.6),
     'L1_xattn_k_norm_w': (1.0, 0.6),
     'L1_ffn_bu1': (0.0, 2.0),
     'L1_ffn_log_rel': (0.0, 2.0)}
    factors = {'L1_ffn_Wq': 64.0,
     'L1_ffn_Wr': 64.0,
     'L1_ffn_aux_keys': 64.0,
     'L1_ffn_aux_values': 64.0,
     'L1_ffn_Wvd': 64.0,
     'L1_ffn_Wvu': 64.0,
     'L1_ffn_Wu1': 64.0,
     'L1_ffn_Wu2': 64.0}
    for name, (base, spread) in spreads.items():
        noise = np.random.default_rng([zlib.crc32(name.encode()), seed]).standard_normal(out[name].shape)
        drawn = base * np.exp(spread * noise) if base else spread * noise
        out[name] = jnp.asarray(drawn.astype(out[name].dtype))
    for name, factor in factors.items():
        out[name] = (out[name] * factor).astype(out[name].dtype)
    return out
```

```python
from contextlib import ExitStack

import numpy as np

import concourse.bass as bass
from concourse import mybir

F32 = mybir.dt.float32
F16 = mybir.dt.float16
BF16 = mybir.dt.bfloat16
U32 = mybir.dt.uint32
I32 = mybir.dt.int32
U8 = mybir.dt.uint8
ALU = mybir.AluOpType
ACTF = mybir.ActivationFunctionType
AX = mybir.AxisListType.X
RMAX = bass.bass_isa.ReduceOp.max

NB, SQ, D = 32, 64, 512
T = NB * SQ
NH, NKV, DH = 32, 8, 128
KT = D // 128
TC = 512
NC = T // TC
BC = TC // SQ
INTER = 1376
FT = 11
NSLOT, BOT, RDIM, VB = 128, 64, 48, 32
LN_EPS = 1e-5
ISQ = float(1.0 / np.sqrt(np.float32(DH)))
BIG = 1e30
STAGES = 4


class Sem:

    def __init__(self, handle):
        self.handle, self.count = handle, 0


class Queue:

    def __init__(self):
        self.ops, self.seen = [], {}

    def wait(self, *marks):
        for sem, n in marks:
            if self.seen.get(id(sem), 0) < n:
                self.seen[id(sem)] = n
                self.ops.append((None, sem.handle, n))

    def put(self, fn, sem=None, n=1):
        self.ops.append((fn, sem.handle if sem else None, n))
        if sem:
            sem.count += n
            return (sem, sem.count)
        return None

    def run(self, eng):
        for fn, handle, n in self.ops:
            if fn is None:
                eng.wait_ge(handle, n)
            elif handle is None:
                fn(eng)
            else:
                fn(eng).then_inc(handle, n)


def build(nc, din, out):
    ctx = ExitStack()
    with ctx:
        def sb(name, shape, dt):
            return ctx.enter_context(nc.sbuf_tensor(name, shape, dt))

        sems = {}

        def S(name):
            if name not in sems:
                sems[name] = Sem(ctx.enter_context(nc.semaphore("s_" + name)))
            return sems[name]

        PE, ACT, DVE, POOL, SP = Queue(), Queue(), Queue(), Queue(), Queue()

        def mm(o, l, r, start, stop, sem=None, w=()):
            PE.wait(*w)
            return PE.put(lambda e: e.matmul(o, l, r, start=start, stop=stop), sem)

        def tp(o, i, ident, sem=None, w=()):
            PE.wait(*w)
            return PE.put(lambda e: e.transpose(o, i, ident), sem)

        def act(o, i, f, sem=None, w=(), **kw):
            ACT.wait(*w)
            return ACT.put(lambda e: e.activation(o, i, f, **kw), sem)

        def tt(o, a, b, op, sem=None, w=(), q=None):
            q = q or DVE
            q.wait(*w)
            return q.put(lambda e: e.tensor_tensor(o, a, b, op), sem)

        def ts(o, a, s1, s2, op0, op1, sem=None, w=(), q=None):
            q = q or DVE
            q.wait(*w)
            if op1 is None:
                return q.put(lambda e: e.tensor_scalar(o, a, s1, None, op0), sem)
            return q.put(lambda e: e.tensor_scalar(o, a, s1, s2, op0, op1), sem)

        def stt(o, a, s, b, op0, op1, sem=None, w=()):
            DVE.wait(*w)
            return DVE.put(lambda e: e.scalar_tensor_tensor(o, a, s, b, op0, op1), sem)

        def red(o, i, op, sem=None, w=(), absv=False):
            DVE.wait(*w)
            if absv:
                return DVE.put(lambda e: e.tensor_reduce(o, i, AX, op, apply_absolute_value=True), sem)
            return DVE.put(lambda e: e.tensor_reduce(o, i, AX, op), sem)

        def recip(o, i, sem=None, w=()):
            DVE.wait(*w)
            return DVE.put(lambda e: e.reciprocal(o, i), sem)

        def fill(o, v, sem=None, w=(), q=None):
            q = q or DVE
            q.wait(*w)
            return q.put(lambda e: e.memset(o, v), sem)

        def dma(o, i, sem, w=(), q=None):
            q = q or SP
            q.wait(*w)
            return q.put(lambda e: e.dma_start(o, i), sem, 16)

        def allmax(o, i, sem, w=()):
            POOL.wait(*w)
            return POOL.put(lambda e: e.partition_all_reduce(o, i, 128, RMAX), sem)

        X = sb("X", [128, T // 128, D], F32)
        CT = [sb(f"CT{i}", [128, KT, T], F16) for i in range(2)]
        XT = [sb(f"XT{i}", [128, KT, T], F16) for i in range(2)]
        WB = [sb(f"WB{i}", [128, 10240], F16) for i in range(2)]
        STG = sb("STG", [128, 4096], F32)
        AR = sb("AR", [128, 11776], F32)
        LNB = sb("LNB", [128, 2, D], F32)
        CST = sb("CST", [128, 516], F32)
        SHC = sb("SHC", [128, 1], U32)
        SML = sb("SML", [128, 256], F32)
        ONEB = sb("ONEB", [128, 2], BF16)
        PB = [ctx.enter_context(nc.psum_tensor(f"PB{i}", [128, 512], F32)) for i in range(8)]

        IDN = CST[:, 0:128]
        COST, SINT = CST[:, 128:192], CST[:, 192:256]
        COSK, SINK = CST[:, 256:384], CST[:, 384:512]
        IDXG, IDXD = CST[:, 512:513], CST[:, 513:514]
        ONEF = CST[:, 514:515]

        small = [0]

        def sm(n):
            a = small[0]
            small[0] += n
            assert small[0] <= 256
            return SML[:, a:a + n]

        arena = [0]

        def view(words, dt, **dims):
            a = arena[0]
            arena[0] += words
            assert arena[0] <= 11776, arena[0]
            v = AR[:, a:a + words]
            return v if dt == F32 else v.bitcast(dt)

        def wset(i):
            w = WB[i]
            q = [w[:, n * 2048:(n + 1) * 2048].rearrange("p (k n) -> p k n", k=4) for n in range(2)]
            kv = [w[:, 4096 + n * 1024:4096 + (n + 1) * 1024].rearrange("p (k n) -> p k n", k=4) for n in range(2)]
            o = [w[:, 6144 + n * 2048:6144 + (n + 1) * 2048].rearrange("p (k n) -> p k n", k=4) for n in range(2)]
            return q, kv, o

        WSET = [wset(0), wset(1)]

        bank_free = [()] * 8

        class Ring:

            def __init__(self, banks):
                self.banks, self.n = banks, 0

            def take(self):
                i = self.banks[self.n % len(self.banks)]
                self.n += 1
                PE.wait(*bank_free[i])
                return i, PB[i]

            def release(self, i, *marks):
                bank_free[i] = marks

        c_cst = dma(CST[:, :], din["const_f"], S("cst"))
        c_sh = dma(SHC[:, :], din["const_u"], S("cst2"))
        XM = [None] * 16
        xv = din["x"].rearrange("(t p) d -> p t d", p=128)
        for c in range(NC):
            m = dma(X[:, 4 * c:4 * c + 4, :], xv[:, 4 * c:4 * c + 4, :], S(f"x{c}"))
            for t in range(4):
                XM[4 * c + t] = m
        c_one = fill(ONEB[:, :], 1.0, S("one"))

        NRM = sm(4)

        def norm_scale(p, r, am, mark, mul=1.0):
            a = allmax(NRM[:, 0:1], am, S("ns_all"), [mark] + norm_scale.last)
            a = ts(NRM[:, 1:2], NRM[:, 0:1], 2.0 ** -100, 2.0 ** 100, ALU.max, ALU.min, S("ns"), [a])
            a = ts(NRM[:, 2:3].bitcast(U32), NRM[:, 1:2].bitcast(U32), 0x7F800000, None, ALU.bitwise_and, None,
                   S("ns"), [a])
            a = ts(p, NRM[:, 2:3], mul, None, ALU.mult, None, S("ns"), [a])
            b = recip(r, p, S("ns"), [a])
            norm_scale.last = [b]
            return b

        norm_scale.last = []

        class Stage:
            free = [(), ()]
            n = 0

        def stage():
            i = Stage.n % 2
            Stage.n += 1
            SP.wait(*Stage.free[i])
            return i, STG[:, i * 2048:(i + 1) * 2048]

        CTP, CTR, AMX = sm(4), sm(4), sm(2)
        CT_ready = [None] * NC
        CT_scaled = [None] * NC
        am_free = [()]

        def load_ctx(c):
            i, st = stage()
            m = dma(st.rearrange("p (k t) -> p k t", k=4),
                    din["ctxT"].rearrange("(k p) t -> p k t", p=128)[:, :, c * TC:(c + 1) * TC], S(f"stg{i}"))
            a = red(AMX[:, 0:1], st, ALU.max, S("amx"), [m] + list(am_free[0]), absv=True)
            b = norm_scale(CTP[:, c:c + 1], CTR[:, c:c + 1], AMX[:, 0:1], a)
            am_free[0] = [b]
            marks = []
            for k in range(KT):
                hi, lo = [CT[n][:, k, c * TC:(c + 1) * TC] for n in range(2)]
                src = st[:, k * TC:(k + 1) * TC]
                h = act(hi, src, ACTF.Copy, S("ct_hi"), [b], scale=CTR[:, c:c + 1])
                l = stt(lo, src, CTR[:, c:c + 1], hi, ALU.mult, ALU.subtract, S("ct_lo"), [h, b])
                marks += [h, l]
            Stage.free[i] = marks[-2:]
            CT_ready[c], CT_scaled[c] = marks[-2:], b

        LNS, LNM, LNV, LNR, LNC = sm(24), sm(8), sm(4), sm(4), sm(4)
        ln_free = [[], []]
        XT_ready = [None] * NC
        XT_used = [[] for _ in range(NC)]
        c_half = fill(LNC[:, :], -0.5, S("one"))
        lns_free = [[]]

        def ln_stats(c):
            for t in range(4):
                a = DVE_bn(LNS[:, 6 * t:6 * t + 6], X[:, 4 * c + t, :], [XM[4 * c + t]] + lns_free[0])
            for t in range(4):
                a = DVE_agg(LNM[:, 2 * t:2 * t + 2], LNS[:, 6 * t:6 * t + 6], [a])
            a = ts(LNV[:, :], LNM[:, 1:8:2], LN_EPS, None, ALU.add, None, S("ln"), [a])
            return tt(LNR[:, :], LNV[:, :], LNC[:, :], ALU.pow, S("ln_pow"), [a, c_half], q=POOL)

        def DVE_bn(o, i, w):
            DVE.wait(*w)
            return DVE.put(lambda e: e.bn_stats(o, i), S("ln"))

        def DVE_agg(o, i, w):
            DVE.wait(*w)
            return DVE.put(lambda e: e.bn_aggr(o, i), S("ln"))

        def ln_chunk(c, ring):
            r = ln_stats(c)
            marks = []
            for t in range(4):
                b = LNB[:, t % 2, :]
                n = ts(b, X[:, 4 * c + t, :], LNM[:, 2 * t:2 * t + 1], LNR[:, t:t + 1], ALU.subtract, ALU.mult,
                       S("ln_x"), [r] + ln_free[t % 2])
                lns_free[0] = [n]
                i, bank = ring.take()
                for k in range(KT):
                    m = tp(bank[:, k * 128:(k + 1) * 128], b[:, k * 128:(k + 1) * 128], IDN, S("ln_t"), [n, c_cst])
                ln_free[t % 2] = [m]
                src = bank[:, :].rearrange("p (k t) -> p k t", k=4)
                hi, lo = [XT[n][:, :, (4 * c + t) * 128:(4 * c + t + 1) * 128] for n in range(2)]
                h = act(hi, src, ACTF.Copy, S("xt_hi"), [m] + XT_used[c])
                l = tt(lo, src, hi, ALU.subtract, S("xt_lo"), [h])
                ring.release(i, l)
                marks = [h, l]
            XT_ready[c] = marks

        QT = [view(1024, F16) for _ in range(2)]
        KTT = [view(256, F16) for _ in range(2)]
        V = [[view(256, F16).rearrange("p (t d) -> p t d", t=4) for _ in range(2)] for _ in range(2)]
        KF = view(512, F32).rearrange("p (t d) -> p t d", t=4)
        KR = view(512, F32).rearrange("p (t d) -> p t d", t=4)
        M1 = [view(512, F32) for _ in range(2)]
        RT_all = view(1024, F32)
        RT = [RT_all[:, 0:512], RT_all[:, 512:1024]]
        SS = view(1024, F32).rearrange("p (a n) -> p a n", a=2)
        PT = [view(512, F16).rearrange("p (a b n) -> p a b n", a=2, b=4) for _ in range(2)]
        AT = [view(1024, F16).rearrange("p (h t) -> p h t", h=4) for _ in range(2)]
        MK = view(1024, F32)
        M01 = MK[:, 0:512].bitcast(U8).rearrange("p (b k) -> p b k", b=NB)
        MNO = MK[:, 512:1024].bitcast(U8).rearrange("p (b k) -> p b k", b=NB)
        SQH = MK.bitcast(BF16)
        SQL = RT_all.bitcast(BF16)
        MASK1, WQK = KR[:, 0, 0:64], KR[:, 1, :]
        MXT, SMT, RCT, RSQ, KSS, RSK = sm(16), sm(16), sm(16), sm(16), sm(4), sm(4)
        HLF = sm(16)
        WSC = sm(24)
        CO = sm(16)
        c_hlf = fill(HLF, -0.5, S("one"))
        pr, sr, br = Ring([0, 1]), Ring([2, 3]), Ring([4, 5, 6, 7])

        def rows_of(t, pair, b):
            return t[:, (pair * BC + b) * 128:(pair * BC + b + 1) * 128]

        def head_of(t, h):
            return t.rearrange("p (a b h q) -> p a b h q", a=2, b=BC, h=2)[:, h // 2, :, h % 2, :]

        def by_batch(t):
            return t.rearrange("p (b s) -> p b s", s=SQ)

        class G:
            w_used = [[], [], [], [], [], []]
            qt_used, kt_used, v_used = [], [], [[], []]
            kf_free, m1_free, rt_free = [], [[], []], [[], []]
            ss_free, pt_used, at_used = [], [], []
            sml_free, sq_used = [], []
            late = []

        def flush():
            todo, G.late = G.late, []
            for f in todo:
                f()

        W_ready = {}

        def prep_weight(L, g, kind):
            par = (g + L) % 2
            q, kv, o = WSET[par]
            i, st = stage()
            s4 = st.rearrange("p (k n) -> p k n", k=4)
            if kind == 0:
                m = dma(s4, din[f"wq{L}"].rearrange("(k p) n -> p k n", p=128)[:, :, g * 512:(g + 1) * 512], S(f"stg{i}"))
                n, dst = 512, q
            elif kind == 1:
                s4 = st[:, 0:1024].rearrange("p (k n) -> p k n", k=4)
                for j, nm in enumerate(("wk", "wv")):
                    m = dma(s4[:, :, j * 128:(j + 1) * 128],
                            din[f"{nm}{L}"].rearrange("(k p) n -> p k n", p=128)[:, :, g * 128:(g + 1) * 128],
                            S(f"stg{i}"))
                n, dst = 256, kv
            else:
                m = dma(s4, din[f"wo{L}"].rearrange("(h p) n -> p h n", p=128)[:, 4 * g:4 * g + 4, :], S(f"stg{i}"))
                n, dst = 512, o
            a = red(AMX[:, 0:1], st[:, 0:4 * n], ALU.max, S("amx"), [m] + list(am_free[0]), absv=True)
            col = par * 12 + kind * 4
            b = norm_scale(WSC[:, col:col + 1], WSC[:, col + 1:col + 2], AMX[:, 0:1], a)
            am_free[0] = [b]
            r = WSC[:, col + 1:col + 2]
            used = G.w_used[par * 3 + kind]
            hs = [act(dst[0][:, k, :], s4[:, k, :], ACTF.Copy, S("w_hi"), [b] + used, scale=r) for k in range(4)]
            ls = [stt(dst[1][:, k, :], s4[:, k, :], r, dst[0][:, k, :], ALU.mult, ALU.subtract, S("w_lo"), [hs[k]])
                  for k in range(4)]
            Stage.free[i] = [ls[-1]]
            W_ready[(L, g, kind)] = [hs[-1], ls[-1]]
            if kind == 2:
                p_q, p_kv = [WSC[:, par * 12 + 4 * k:par * 12 + 4 * k + 1] for k in range(2)]
                r_q, r_kv = [WSC[:, par * 12 + 4 * k + 1:par * 12 + 4 * k + 2] for k in range(2)]
                e_q, e_kv = WSC[:, par * 12 + 2:par * 12 + 3], WSC[:, par * 12 + 3:par * 12 + 4]
                if L == 0:
                    a = ts(e_q, p_q, p_kv, ISQ, ALU.mult, ALU.mult, S("co"), [b] + G.co_used[par])
                else:
                    a = ts(e_q, r_q, r_q, LN_EPS, ALU.mult, ALU.mult, S("co"), [b] + G.co_used[par])
                    a = ts(e_kv, r_kv, r_kv, LN_EPS, ALU.mult, ALU.mult, S("co"), [b])
                W_ready[(L, g, 3)] = [a]

        def unit_scales(L, g, c):
            par = (g + L) % 2
            co, w = CO[:, par * 8:par * 8 + 8], [CT_scaled[c]] + W_ready[(L, g, 3)] + G.co_used[par]
            p_kv, p_o = [WSC[:, par * 12 + 4 * k:par * 12 + 4 * k + 1] for k in (1, 2)]
            a = ts(co[:, c:c + 1], CTP[:, c:c + 1], p_kv, p_o, ALU.mult, ALU.mult, S("co"), w)
            if L == 0:
                a = ts(co[:, 4 + c:5 + c], CTP[:, c:c + 1], WSC[:, par * 12 + 2:par * 12 + 3], None, ALU.mult, None, S("co"))
            else:
                a = ts(co[:, 4 + c:5 + c], CTR[:, c:c + 1], WSC[:, par * 12 + 3:par * 12 + 4], CTR[:, c:c + 1],
                       ALU.mult, ALU.mult, S("co"))
            G.co_ready = [a]

        G.co_used = [[], []]
        PWN = sm(4)

        def kv_proj(L, g, c, uv, co_ready):
            par = (g + L) % 2
            wkv = WSET[par][1]
            ready = W_ready[(L, g, 1)] + CT_ready[c]
            vd, vmarks = V[uv], []
            banks = []
            for half in range(2):
                i, bank = pr.take()
                PE.wait(*ready)
                for t2 in range(2):
                    tok = slice((4 * c + 2 * half + t2) * 128, (4 * c + 2 * half + t2 + 1) * 128)
                    o = bank[:, t2 * 256:(t2 + 1) * 256]
                    n = 0
                    for k in range(KT):
                        for a, b in ((0, 0), (0, 1), (1, 0)):
                            m = mm(o, CT[a][:, k, tok], wkv[b][:, k, :], n == 0, n == 11,
                                   S("kv") if n == 11 else None)
                            n += 1
                src = bank[:, :].rearrange("p (t n) -> p t n", t=2)
                tsl = slice(2 * half, 2 * half + 2)
                h = act(vd[0][:, tsl, :], src[:, :, 128:256], ACTF.Copy, S("v_hi"), [m] + G.v_used[uv])
                if L == 0:
                    def bc(x):
                        return x.unsqueeze(1).to_broadcast([128, 2, x.shape[1]])
                    k1 = tt(KF[:, tsl, :], src[:, :, 0:128], bc(COSK), ALU.mult, S("k_e"), [h, c_cst] + G.kf_free)
                    tt(KR[:, tsl, 0:64], src[:, :, 64:128], bc(SINK[:, 0:64]), ALU.mult, S("k_e"), G.kf_free)
                    k2 = tt(KR[:, tsl, 64:128], src[:, :, 0:64], bc(SINK[:, 64:128]), ALU.mult, S("k_e"))
                else:
                    for t2 in range(2):
                        t = 2 * half + t2
                        k1 = act(M1[0][:, 0:128], src[:, t2, 0:128], ACTF.Square, S("k_sq"),
                                 [m] + G.m1_free[0] + G.kss_used, accum_out=KSS[:, t:t + 1])
                        G.m1_free[0] = [k1]
                    k2 = tt(KF[:, tsl, :], src[:, :, 0:128], WQK.unsqueeze(1).to_broadcast([128, 2, 128]), ALU.mult,
                            S("k_e"), [k1] + G.kf_free + G.wqk)
                l = tt(vd[1][:, tsl, :], src[:, :, 128:256], vd[0][:, tsl, :], ALU.subtract, S("v_lo"), [h])
                pr.release(i, h, l, k1, k2)
                vmarks = [h, l]
            kk = [k1, k2]
            G.w_used[par * 3 + 1] = [m]
            if L == 0:
                k = tt(KF[:, :, :], KF[:, :, :], KR[:, :, :], ALU.add, S("k_add"), kk, q=POOL)
            else:
                a = ts(KSS[:, :], KSS[:, :], 1.0 / DH, CO[:, par * 8 + 4 + c:par * 8 + 5 + c], ALU.mult, ALU.add,
                       S("k_ms"), [k1] + co_ready)
                a = tt(RSK[:, :], KSS[:, :], HLF[:, 0:4], ALU.pow, S("k_pow"), [a, c_hlf] + G.kss_used, q=POOL)
                k = tt(KF[:, :, :], KF[:, :, :], RSK[:, :].unsqueeze(2).to_broadcast([128, 4, 128]), ALU.mult,
                       S("k_add"), [a, k2], q=POOL)
                G.kss_used = [k]
            return k, vmarks

        G.kss_used, G.wqk = [], []

        def k_turn(k):
            i, bank = pr.take()
            for t in range(4):
                m = tp(bank[:, t * 128:(t + 1) * 128], KF[:, t, :], IDN, S("k_t"), [k])
            G.kf_free = [m]
            h = act(KTT[0], bank[:, :], ACTF.Copy, S("kt_hi"), [m] + G.kt_used)
            l = tt(KTT[1], bank[:, :], KTT[0], ALU.subtract, S("kt_lo"), [h])
            pr.release(i, h, l)
            return [h, l]

        def q_proj(L, g, c, h, marks):
            par = (g + L) % 2
            wq = WSET[par][0]
            i, bank = pr.take()
            PE.wait(*W_ready[(L, g, 0)], *XT_ready[c])
            n = 0
            for k in range(KT):
                for a, b in ((0, 0), (0, 1), (1, 0)):
                    m = mm(bank[:, :], wq[a][:, k, h * 128:(h + 1) * 128], XT[b][:, k, c * TC:(c + 1) * TC],
                           n == 0, n == 11, S("q") if n == 11 else None)
                    n += 1
            if h == 3:
                G.w_used[par * 3] = [m]
                XT_used[c] = [m]
            m1, rt = M1[h % 2], RT[h % 2]
            v3 = bank[:, :].rearrange("p (b s) -> p b s", s=SQ)
            if L == 0:
                r1 = act(rt[0:64, :], bank[64:128, :], ACTF.Copy, S("q_rot"), [m] + G.rt_free[h % 2])
                r2 = act(rt[64:128, :], bank[0:64, :], ACTF.Copy, S("q_rot"))
                c1 = tt(m1.rearrange("p (b s) -> p b s", s=SQ), v3, COST.unsqueeze(1).to_broadcast([128, BC, SQ]),
                        ALU.mult, S("q_cos"), [r2, c_cst] + G.m1_free[h % 2])
                pr.release(i, r2, c1)
                r3v = rt.rearrange("p (b s) -> p b s", s=SQ)
                r3 = tt(r3v, r3v, SINT.unsqueeze(1).to_broadcast([128, BC, SQ]), ALU.mult, S("q_sin"), [r2], q=POOL)

                def finish():
                    a = tt(m1, m1, rt, ALU.add, S("q_add"), [c1, r3])
                    G.rt_free[h % 2] = [a]
                    hi = act(head_of(QT[0], h), by_batch(m1), ACTF.Copy, S("qt_hi"), [a] + G.qt_used)
                    lo = tt(head_of(QT[1], h), by_batch(m1), head_of(QT[0], h), ALU.subtract, S("qt_lo"), [hi])
                    G.m1_free[h % 2] = [lo]
                    marks.extend([hi, lo])
                G.late.append(finish)
            else:
                hi = act(head_of(QT[0], h), v3, ACTF.Copy, S("qt_hi"), [m] + G.qt_used)
                s1 = act(m1, bank[:, :], ACTF.Square, S("q_sq"), G.m1_free[h % 2])
                s2 = act(head_of(SQH, h), v3, ACTF.Square, S("q_sq"), G.sq_used)
                lo = tt(head_of(QT[1], h), v3, head_of(QT[0], h), ALU.subtract, S("qt_lo"), [s2])
                pr.release(i, s2, lo)
                s3 = tt(head_of(SQL, h), by_batch(m1), head_of(SQH, h), ALU.subtract, S("q_sql"), [s1, s2] + G.sq_used, q=POOL)
                G.m1_free[h % 2] = [s3]
                marks.extend([hi, lo])
                G.sq_ready = [s2, s3]

        def q_norm(L, g):
            par = (g + L) % 2
            i, bank = pr.take()
            PE.wait(*G.sq_ready, c_one)
            for pair in range(2):
                for b in range(BC):
                    o = bank[:, pair * BC + b:pair * BC + b + 1]
                    for n, s in enumerate((SQH, SQL)):
                        m = mm(o, rows_of(s, pair, b), ONEB[:, 0:1], n == 0, n == 1,
                               S("q_ss") if n else None)
            G.sq_used = [m]
            a = ts(RSQ[:, :], bank[:, 0:16], 1.0 / DH, WSC[:, par * 12 + 2:par * 12 + 3], ALU.mult, ALU.add,
                   S("q_ms"), [m] + G.rsq_used + W_ready[(L, g, 3)])
            pr.release(i, a)
            return tt(RSQ[:, :], RSQ[:, :], HLF, ALU.pow, S("q_pow"), [a, c_hlf], q=POOL)

        G.rsq_used = []

        def scores(L, g, c, ready, rsq, co_ready):
            par = (g + L) % 2
            co = CO[:, par * 8:par * 8 + 8]
            es = []
            banks = []
            for pair in range(2):
                i, bank = sr.take()
                PE.wait(*ready)
                for b in range(BC):
                    o = bank[:, b * SQ:(b + 1) * SQ]
                    for n, (x, y) in enumerate(((0, 0), (0, 1), (1, 0))):
                        m = mm(o, rows_of(QT[x], pair, b), KTT[y][:, b * SQ:(b + 1) * SQ],
                               n == 0, n == 2, S("s") if n == 2 else None)
                banks.append((i, bank, m))
            G.qt_used = G.kt_used = [m]
            for pair in range(2):
                i, bank, m = banks[pair]
                s = SS[:, pair, :]
                s3 = s.rearrange("p (b k) -> p b k", b=BC)
                b3 = bank[:, :].rearrange("p (b k) -> p b k", b=BC)
                bsl = slice(c * BC, (c + 1) * BC)
                if L == 0:
                    a = stt(s3, b3, co[:, 4 + c:5 + c], M01[:, bsl, :], ALU.mult, ALU.mult, S("sm"),
                            [m] + G.ss_free + co_ready + G.mask_ready)
                    sr.release(i, a)
                    a = stt(s3, MNO[:, bsl, :], -1e9, s3, ALU.mult, ALU.add, S("sm"), [a])
                else:
                    a = tt(s3, b3, RSQ[:, pair * BC:(pair + 1) * BC].unsqueeze(2).to_broadcast([128, BC, SQ]), ALU.mult,
                           S("sm"), [m, rsq] + G.ss_free)
                    G.rsq_used = [a]
                    sr.release(i, a)
                    a = stt(s3, s3, PWN[:, 2:3], MASK1.unsqueeze(1).to_broadcast([128, BC, SQ]), ALU.mult, ALU.add,
                            S("sm"), [a] + G.wqk)
                mx = MXT[:, pair * BC:(pair + 1) * BC]
                a = red(mx, s3, ALU.max, S("sm"), [a])
                a = tt(s3, s3, mx.unsqueeze(2).to_broadcast([128, BC, SQ]), ALU.subtract, S("sm"), [a])
                es.append(act(s, s, ACTF.Exp, S("exp"), [a]))
            return es

        def soft_norm(es):
            ps = []
            for pair in range(2):
                s3 = SS[:, pair, :].rearrange("p (b k) -> p b k", b=BC)
                cols = slice(pair * BC, (pair + 1) * BC)
                a = red(SMT[:, cols], s3, ALU.add, S("sm"), [es[pair]])
                a = recip(RCT[:, cols], SMT[:, cols], S("sm"), [a] + G.sml_free)
                ps.append(tt(s3, s3, RCT[:, cols].unsqueeze(2).to_broadcast([128, BC, SQ]), ALU.mult, S("p_n"),
                             [a], q=POOL))
            G.sml_free = [ps[-1]]
            return ps

        def p_turn(ps):
            marks = []
            for pair in range(2):
                i, bank = sr.take()
                for b2 in range(4):
                    m = tp(bank[:, b2 * 128:(b2 + 1) * 128], SS[:, pair, b2 * 128:(b2 + 1) * 128], IDN, S("p_t"),
                           [ps[pair]])
                src = bank[:, :].rearrange("p (b n) -> p b n", b=4)
                h = act(PT[0][:, pair, :, :], src, ACTF.Copy, S("pt_hi"), [m] + G.pt_used)
                l = tt(PT[1][:, pair, :, :], src, PT[0][:, pair, :, :], ALU.subtract, S("pt_lo"), [h])
                sr.release(i, h, l)
                marks += [h, l]
            G.ss_free = [m]
            return marks

        def pv(uv, ready):
            vd = V[uv]
            marks = []
            for j in range(2):
                bk = [br.take(), br.take()]
                PE.wait(*ready)
                for jj in range(2):
                    b2 = 2 * j + jj
                    for n, (x, y) in enumerate(((0, 0), (0, 1), (1, 0))):
                        for odd in range(2):
                            rows = slice(64 * odd, 64 * odd + 64)
                            m = mm(bk[odd][1][:, jj * 256:(jj + 1) * 256], vd[x][rows, b2, :], PT[y][rows, :, b2, :],
                                   n == 0, n == 2, S("pv") if n == 2 else None)
                for odd in range(2):
                    i, bank = bk[odd]
                    src = bank[:, :].rearrange("p (b h q) -> p b h q", b=2, h=4)
                    hi, lo = [AT[n].rearrange("p h (b o q) -> p b o h q", o=2, q=SQ)[:, 2 * j:2 * j + 2, odd, :, :]
                              for n in range(2)]
                    h = act(hi, src, ACTF.Copy, S("at_hi"), [m] + G.at_used)
                    l = tt(lo, src, hi, ALU.subtract, S("at_lo"), [h])
                    br.release(i, h, l)
                    marks += [h, l]
            G.pt_used = G.v_used[uv] = [m]
            return marks

        def wo_proj(L, g, c, ready, co_ready):
            par = (g + L) % 2
            wo = WSET[par][2]
            for t in range(4):
                i, bank = br.take()
                PE.wait(*ready, *W_ready[(L, g, 2)])
                n = 0
                for h in range(4):
                    for x, y in ((0, 0), (0, 1), (1, 0)):
                        m = mm(bank[:, :], AT[x][:, h, t * 128:(t + 1) * 128], wo[y][:, h, :], n == 0, n == 11,
                               S("wo") if n == 11 else None)
                        n += 1
                xs = X[:, 4 * c + t, :]
                a = stt(xs, bank[:, :], CO[:, par * 8 + c:par * 8 + c + 1], xs, ALU.mult, ALU.add, S("x_add"),
                        [m, XM[4 * c + t]] + co_ready)
                br.release(i, a)
                XM[4 * c + t] = a
            G.at_used = [m]
            G.w_used[par * 3 + 2] = [m]
            G.co_used[par] = [a]

        def attention(L, before_unit, after_unit):
            units = [(g, c) for g in range(NKV) for c in range(NC)]
            nxt = {}

            def front(u, part):
                g, c = units[u]
                d = nxt.setdefault(u, {"marks": [], "rsq": None})
                if part == "kv":
                    unit_scales(L, g, c)
                    d["co"] = G.co_ready
                    d["k"], d["v"] = kv_proj(L, g, c, u % 2, d["co"])
                elif part == "kt":
                    d["marks"] += k_turn(d["k"])
                elif part == "qn":
                    if L:
                        d["rsq"] = q_norm(L, g)
                else:
                    q_proj(L, g, c, part, d["marks"])

            before_unit(0)
            for p in ("kv", 0, 1, "kt", 2, 3, "qn"):
                front(0, p)
                flush()
            for u, (g, c) in enumerate(units):
                d = nxt.pop(u)
                more = u + 1 < len(units)
                if more:
                    before_unit(u + 1)
                es = scores(L, g, c, d["marks"], d["rsq"], d["co"])
                if more:
                    front(u + 1, "kv")
                ps = soft_norm(es)
                if more:
                    front(u + 1, 0)
                    front(u + 1, 1)
                    flush()
                    front(u + 1, "kt")
                pt = p_turn(ps)
                if more:
                    front(u + 1, 2)
                    flush()
                at = pv(u % 2, pt + d["v"])
                if more:
                    front(u + 1, 3)
                    front(u + 1, "qn")
                    flush()
                wo_proj(L, g, c, at, d["co"])
                after_unit(u)

        def load_masks0():
            st0, st1 = STG[:, 0:2048], STG[:, 2048:4096]
            i, st = stage()
            src = din["mask0"].rearrange("b q k -> q b k")
            for half in range(2):
                m = dma(st[64 * half:64 * half + 64, :].rearrange("p (b k) -> p b k", b=NB), src, S(f"stg{i}"))
            v = st.rearrange("p (b k) -> p b k", b=NB)
            a = ts(M01, v, 0.0, None, ALU.not_equal, None, S("mask"), [m])
            b = ts(MNO, v, 0.0, None, ALU.is_equal, None, S("mask"), [a])
            Stage.free[i] = [b]
            G.mask_ready = [b]

        ln_chunk(0, br)
        load_ctx(0)
        for k in range(3):
            prep_weight(0, 0, k)
        load_masks0()

        TB = WB[0]
        SCT, ZPT = TB[0:64, 0:2752], TB[0:4, 2752:5504]
        OHG, OHD = TB[0:64, 5504:6016], TB[0:64, 6016:7392]
        SCD, ZPD = TB[0:64, 7392:7904], TB[0:10, 7904:8416]
        GUW = [[AR[:, o + n * 1024:o + (n + 1) * 1024].bitcast(F16).rearrange("p (k f) -> p k f", k=4)
                for n in range(2)] for o in (0, 7680)]
        DW = [[AR[:, o + n * 512:o + (n + 1) * 512].bitcast(F16).rearrange("p (j f) -> p j f", j=2)
               for n in range(2)] for o in (2048, 9728)]
        HB = [[AR[:, 5632 + 1024 * i + 512 * n:5632 + 1024 * i + 512 * n + 512].bitcast(F16)
               .rearrange("p (j t) -> p j t", j=2) for n in range(2)] for i in range(2)]
        SG = [AR[:, 10752 + 512 * i:11264 + 512 * i] for i in range(2)]
        PGU, RGU, PD, RD, CH, CY, AMF = sm(1), sm(1), sm(1), sm(1), sm(1), sm(1), sm(2)

        class F:
            tabs, gu_ready, d_ready = [], {}, {}
            gu_used, d_used, h_used, sg_free = [[], []], [[], []], [[], []], [[], []]
            last = []

        def tables_scales(kind):
            name, n, w, dst, p, r = (("scales_gu", 4, 2752, SCT, PGU, RGU), ("scales_d", 10, 512, SCD, PD, RD))[kind]
            SP.wait(*Stage.free[0], *Stage.free[1])
            sf = STG[0:n, 0:w]
            m = dma(sf, din[name], S(f"stg{kind}"))
            z = fill(AMF[:, kind:kind + 1], 0.0, S("tab"))
            a = red(AMF[0:n, kind:kind + 1], sf, ALU.max, S("tab"), [m, z], absv=True)
            b = norm_scale(p, r, AMF[:, kind:kind + 1], a, 16.0)
            z = fill(dst, 0.0, S("tab"), G.w_used[0] + G.w_used[1] + G.w_used[2])
            a = ts(sf, sf, r[0:n, :], None, ALU.mult, None, S("tab"), [b, z])
            h = ts(dst[0:n, :], sf, 1.0, None, ALU.mult, None, S("tab"), [a])
            l = tt(dst[32:32 + n, :], sf, dst[0:n, :], ALU.subtract, S("tab"), [h])
            Stage.free[0] = Stage.free[1] = [l]
            F.tabs.append(l)

        def tables_zeros(kind):
            name, n, w, dst = (("qzeros_gu", 4, 344, ZPT), ("qzeros_d", 10, 64, ZPD))[kind]
            SP.wait(*Stage.free[0], *Stage.free[1])
            qz = STG[0:n, 2752:2752 + w].bitcast(U32)
            uz = STG[0:n, 0:8 * w].bitcast(U32)
            m = dma(qz, din[name], S(f"stg{kind}"))
            for e in range(8):
                a = ts(uz.rearrange("p (c e) -> p e c", e=8)[:, e, :], qz, 4 * e, 15, ALU.logical_shift_right,
                       ALU.bitwise_and, S("tab"), [m])
            a = ts(dst, uz, 1.0, None, ALU.add, None, S("tab"), [a] + G.w_used[0] + G.w_used[1] + G.w_used[2])
            Stage.free[0] = Stage.free[1] = [a]
            F.tabs.append(a)

        def tables_groups(kind):
            name, n, w, dst, idx = (("gidx_gu", 4, 512, OHG, IDXG), ("gidx_d", 10, INTER, OHD, IDXD))[kind]
            SP.wait(*Stage.free[0], *Stage.free[1])
            gi, gf = STG[0:64, 0:w].bitcast(I32), STG[0:64, 2048:2048 + w]
            m = dma(gi, din[name].unsqueeze(0).to_broadcast([64, w]), S(f"stg{kind}"))
            a = ts(gf, gi, 0.0, float(n), ALU.is_lt, ALU.mult, S("tab"), [m])
            a = tt(gf, gf, gi, ALU.add, S("tab"), [a])
            a = ts(gf, gf, 0.0, float(n - 1), ALU.max, ALU.min, S("tab"), [a])
            a = ts(dst, gf, idx[0:64, :], None, ALU.is_equal, None, S("tab"),
                   [a, c_cst] + G.w_used[0] + G.w_used[1] + G.w_used[2])
            Stage.free[0] = Stage.free[1] = [a]
            F.tabs.append(a)

        def tables_factors():
            a = ts(CH, RGU, 1.0 / 32, None, ALU.mult, None, S("tab"), norm_scale.last)
            b = ts(CY, PGU, PGU, 32.0, ALU.mult, ALU.mult, S("tab"), [a])
            b = ts(CY, CY, PD, None, ALU.mult, None, S("tab"), [b])
            F.tabs.append(b)

        def unpack(q, w, n, zp, sc, hi, lo, free, marks):
            a = ts(q.bitcast(U32), q.bitcast(U32), SHC[0:w, :], 15, ALU.logical_shift_right, ALU.bitwise_and, S("uq"), marks)
            iz, bz = pr.take()
            PE.wait(*F.tabs)
            for o, l, r in zp:
                m = mm(bz[0:w, o:o + r.shape[1]], l, r, True, True, S("uq_z"))
            is_, bs = pr.take()
            for o, l, r in sc:
                m2 = mm(bs[0:w, o:o + r.shape[1]], l, r, True, True, S("uq_z"))
            a = tt(q, q.bitcast(U32), bz[0:w, 0:n], ALU.subtract, S("uq"), [a, m])
            pr.release(iz, a)
            a = tt(q, q, bs[0:w, 0:n], ALU.mult, S("uq"), [a, m2])
            pr.release(is_, a)
            h = act(hi, q, ACTF.Copy, S("uq_hi"), [a] + free)
            l = tt(lo, q, hi, ALU.subtract, S("uq_lo"), [h])
            return [h, l], m2

        def step_tiles(s):
            return [128, 128] if s < 5 else [96]

        class Dq:
            pass

        def dequant_load(s):
            n = sum(step_tiles(s))
            i, st = stage()
            q = st[:, 0:8 * n].rearrange("p (k f) -> p k f", k=4)
            for k in range(KT):
                for j in range(2):
                    m = dma(q[:, k, j * n:(j + 1) * n].bitcast(U32),
                            din["qw_gu"][16 * k:16 * k + 16, j * INTER + 256 * s:j * INTER + 256 * s + n]
                            .unsqueeze(1).to_broadcast([16, 8, n]), S(f"stg{i}"))
            Dq.gu = (i, q, m)

        def dequant_load_d(s):
            i, st = stage()
            q = st[:, 0:1024].rearrange("p (j f) -> p j f", j=2)
            for j, w in enumerate(step_tiles(s)):
                m = dma(q[0:w, j, :].bitcast(U32), din["qw_d"][32 * s + 16 * j:32 * s + 16 * j + w // 8, :]
                        .unsqueeze(1).to_broadcast([w // 8, 8, D]), S(f"stg{i}"))
            Dq.d = (i, q, m)

        def dequant(s, k):
            n = sum(step_tiles(s))
            i, q, m = Dq.gu
            cols = [slice(j * INTER + 256 * s, j * INTER + 256 * s + n) for j in range(2)]
            oh = OHG[:, k * 128:(k + 1) * 128]
            marks, last = unpack(q[:, k, :], 128, 2 * n,
                                 [(j * n, oh[0:4, :], ZPT[:, cols[j]]) for j in range(2)],
                                 [(j * n, oh, SCT[:, cols[j]]) for j in range(2)],
                                 GUW[s % 2][0][:, k, 0:2 * n], GUW[s % 2][1][:, k, 0:2 * n], F.gu_used[s % 2], [m, c_sh])
            F.gu_ready[s] = F.gu_ready.get(s, []) + marks
            if k == KT - 1:
                Stage.free[i] = marks

        def dequant_d(s, j):
            i, q, m = Dq.d
            w = step_tiles(s)[j]
            f0 = 256 * s + 128 * j
            marks, last = unpack(q[0:w, j, :], w, 512, [(0, OHD[0:10, f0:f0 + w], ZPD)], [(0, OHD[:, f0:f0 + w], SCD)],
                                 DW[s % 2][0][0:w, j, :], DW[s % 2][1][0:w, j, :], F.d_used[s % 2], [m, c_sh])
            F.d_ready[s] = F.d_ready.get(s, []) + marks
            if j == len(step_tiles(s)) - 1:
                Stage.free[i] = marks
            F.tab_used = [last]

        gr, yr = Ring([2, 3, 4, 5]), Ring([6, 7])

        def ffn_up(s, c):
            n, hb = sum(step_tiles(s)), (4 * s + c) % 2
            hm = []
            for j, w in enumerate(step_tiles(s)):
                bk = []
                for half in range(2):
                    i, bank = gr.take()
                    PE.wait(*F.gu_ready[s], *XT_ready[c])
                    cols = slice(half * n + j * 128, half * n + j * 128 + w)
                    e = 0
                    for k in range(KT):
                        for x, y in ((0, 0), (0, 1), (1, 0)):
                            m = mm(bank[0:w, :], GUW[s % 2][x][:, k, cols], XT[y][:, k, c * TC:(c + 1) * TC],
                                   e == 0, e == 11, S("gu") if e == 11 else None)
                            e += 1
                    bk.append((i, bank, m))
                (ig, bg, mg), (iu, bu, mu) = bk
                sg = SG[j]
                a = act(sg[0:w, :], bg[0:w, :], ACTF.Silu, S("silu"), [mg] + F.sg_free[j] + F.tabs, scale=PGU[0:w, :])
                gr.release(ig, a)
                b = stt(sg[0:w, :], sg[0:w, :], CH[0:w, :], bu[0:w, :], ALU.mult, ALU.mult, S("hf"), [a, mu])
                gr.release(iu, b)
                h = act(HB[hb][0][0:w, j, :], sg[0:w, :], ACTF.Copy, S("h_hi"), [b] + F.h_used[hb])
                l = tt(HB[hb][1][0:w, j, :], sg[0:w, :], HB[hb][0][0:w, j, :], ALU.subtract, S("h_lo"), [h])
                F.sg_free[j] = [l]
                hm += [h, l]
            F.gu_used[s % 2] = [mu]
            if s == 4:
                F.gu0_used = [mu]
            XT_used[c] = [mu]
            return hm

        def ffn_down(s, c, hm):
            hb = (4 * s + c) % 2
            tiles = step_tiles(s)
            for t in range(4):
                i, bank = yr.take()
                PE.wait(*F.d_ready[s], *hm)
                e, last = 0, 3 * len(tiles) - 1
                for j, w in enumerate(tiles):
                    for x, y in ((0, 0), (0, 1), (1, 0)):
                        m = mm(bank[:, :], HB[hb][x][0:w, j, t * 128:(t + 1) * 128], DW[s % 2][y][0:w, j, :],
                               e == 0, e == last, S("y") if e == last else None)
                        e += 1
                xs = X[:, 4 * c + t, :]
                a = stt(xs, bank[:, :], CY[:, :], xs, ALU.mult, ALU.add, S("x_add"), [m, XM[4 * c + t]] + F.tabs)
                yr.release(i, a)
                XM[4 * c + t] = a
            F.h_used[hb] = F.d_used[s % 2] = [m]
            if s == 4:
                F.gu0_used = F.gu0_used + [m]
            F.last = [m, a]

        def ffn(after_chunk):
            prev = None
            for s in range(6):
                for c in range(NC):
                    if s < 5:
                        if c == 0:
                            dequant_load(s + 1)
                            dequant_load_d(s + 1)
                    hm = ffn_up(s, c)
                    if prev:
                        ffn_down(*prev)
                    if s < 5:
                        dequant(s + 1, c)
                        if c < len(step_tiles(s + 1)):
                            dequant_d(s + 1, c)
                    prev = (s, c, hm)
                    after_chunk(s, c)
            ffn_down(*prev)

        def before0(u):
            if 0 < u < NC:
                load_ctx(u)
                ln_chunk(u, br)

        def after0(u):
            g, c = divmod(u, NC)
            if g + 1 < NKV and c < 3:
                prep_weight(0, g + 1, c)
            if STAGES >= 2 and g == NKV - 1:
                if c == 0:
                    tables_scales(0)
                    tables_scales(1)
                    tables_factors()
                if c == 1:
                    tables_zeros(0)
                    tables_zeros(1)
                    ln_chunk(0, br)
                if c == 2:
                    tables_groups(0)
                    tables_groups(1)
                    dequant_load(0)
                    dequant_load_d(0)
                    ln_chunk(1, br)

        if STAGES >= 1:
            attention(0, before0, after0)

        if STAGES >= 2:
            ends = G.qt_used + G.kt_used + G.v_used[0] + G.v_used[1] + G.pt_used + G.at_used + G.ss_free + \
                G.m1_free[0] + G.m1_free[1] + G.rt_free[0] + G.rt_free[1] + G.kf_free
            for i in range(2):
                F.gu_used[i] = F.d_used[i] = F.h_used[i] = F.sg_free[i] = ends
            for k in range(KT):
                dequant(0, k)
            for j in range(2):
                dequant_d(0, j)
            ln_chunk(2, br)
            ln_chunk(3, br)

            def after_ffn(s, c):
                if STAGES >= 3 and s == 4 and c == 3:
                    for k in range(3):
                        prep_weight(1, 0, k)
                if STAGES >= 3 and s == 5 and c >= 2:
                    ln_chunk(c - 2, yr)

            ffn(after_ffn)
            if STAGES >= 3:
                for k in range(3):
                    G.w_used[k] = F.tab_used
                ln_chunk(2, br)
                ln_chunk(3, br)

        TW = WB[1][:, :].bitcast(F32)
        wpos = [0]

        def tw(rows, words):
            o = wpos[0]
            wpos[0] += words
            assert wpos[0] <= 5120
            return TW[0:rows, o:o + words]

        WQM = tw(128, 256).rearrange("p (k n) -> p k n", k=4)
        WU1 = tw(128, 512).rearrange("p (k n) -> p k n", k=4)
        AVT = tw(128, 512).rearrange("p (k n) -> p k n", k=4)
        WVD = tw(128, 128).rearrange("p (k n) -> p k n", k=4)
        WRT, AKT = tw(64, 48), tw(64, 128)
        WVU, AV3 = tw(32, 512), tw(128, 512)
        T1T, RKT = tw(32, 128), tw(48, 128)
        WU2, BU1, LREL, BU2, GWT, GBT = tw(128, 2), tw(128, 1), tw(128, 128), tw(128, 1), tw(128, 1), tw(128, 1)
        ALL1 = tw(128, 128)
        VAR, LGT, GATE = sm(16), sm(16), sm(16)
        TOT = sm(4)

        class R4:
            ready = []

        def tail_loads():
            used = G.w_used[3] + G.w_used[4] + G.w_used[5]
            for dst, src in (
                (WQM, din["wqm"].rearrange("(k p) n -> p k n", p=128)),
                (WU1, din["wu1"].rearrange("(k p) n -> p k n", p=128)),
                (AVT, din["avT"].rearrange("(k p) n -> p k n", p=128)),
                (WVD, din["wvd"].rearrange("(k p) n -> p k n", p=128)),
                (WRT, din["wrT"]), (AKT, din["akT"]), (WVU, din["wvu"]),
                (WU2[:, 0:1], din["wu2"]), (BU1, din["bu1"]),
                (LREL, din["log_rel"].to_broadcast([128, NSLOT])),
                (BU2, din["bu2"].to_broadcast([128, 1])),
                (GWT, din["gate_w1"].to_broadcast([128, 1])),
                (GBT, din["gate_bias"].to_broadcast([128, 1])),
            ):
                R4.ready = [dma(dst, src, S("tail_w"), used)]
            R4.ones = fill(ALL1, 1.0, S("tail_one"), used)

        def tail_setup():
            i, bank = pr.take()
            PE.wait(*R4.ready)
            m = mm(bank[0:48, 0:128], WRT, AKT, True, True, S("t_pe"))
            a = act(RKT, bank[0:48, 0:128], ACTF.Copy, S("t_act"), [m])
            pr.release(i, a)
            i, bank = pr.take()
            for k in range(KT):
                m = mm(bank[0:32, 0:128], WVD[:, k, :], AVT[:, k, :], k == 0, k == 3, S("t_pe") if k == 3 else None)
            b = act(T1T, bank[0:32, 0:128], ACTF.Copy, S("t_act"), [m])
            pr.release(i, b)
            i, bank = pr.take()
            m = mm(bank[:, :], T1T, WVU, True, True, S("t_pe"), [b])
            b = act(AV3, bank[:, :], ACTF.Copy, S("t_act"), [m])
            pr.release(i, b)
            R4.setup = [a, b]

        def AO(t):
            return CT[t // 8][:, :, :].rearrange("p k t -> p (k t)")[:, (t % 8) * 1024:(t % 8) * 1024 + 1024].bitcast(F32)

        tv = [0]

        def tv_view(words):
            o = tv[0]
            tv[0] += words
            assert tv[0] <= 11776
            return AR[:, o:o + words]

        QY, RQ, UG = [[tv_view(512) for _ in range(2)] for _ in range(3)]
        RS_, AS_, SE_, R2_ = [[tv_view(512).rearrange("p (t n) -> p t n", t=4) for _ in range(2)] for _ in range(4)]
        WT = [tv_view(512) for _ in range(2)]
        M8, MX4, SM4, RC4 = tv_view(32), tv_view(4), tv_view(4), tv_view(4)
        LNS2, LNM2 = tv_view(24), tv_view(8)

        def tail_front(c, used):
            r = ln_stats(c)
            i0, ht = stage()
            ht = ht.rearrange("p (k t) -> p k t", k=4)
            for t in range(4):
                b = LNB[:, t % 2, :]
                n = ts(b, X[:, 4 * c + t, :], LNM[:, 2 * t:2 * t + 1], LNR[:, t:t + 1], ALU.subtract, ALU.mult,
                       S("ln_x"), [r] + ln_free[t % 2])
                lns_free[0] = [n]
                v = DVE_bn(LNS2[:, 6 * t:6 * t + 6], b, [n] + used)
                xs = X[:, 4 * c + t, :]
                XM[4 * c + t] = tt(xs, xs, b, ALU.add, S("x_add2"), [n], q=POOL)
                i, bank = br.take()
                for k in range(KT):
                    m = tp(bank[:, k * 128:(k + 1) * 128], b[:, k * 128:(k + 1) * 128], IDN, S("ln_t"), [n])
                ln_free[t % 2] = [m, v, XM[4 * c + t]]
                h = act(ht[:, :, t * 128:(t + 1) * 128], bank[:, :].rearrange("p (k t) -> p k t", k=4), ACTF.Copy,
                        S("t_act"), [m] + list(Stage.free[i0]))
                br.release(i, h)
            for t in range(4):
                v = DVE_agg(LNM2[:, 2 * t:2 * t + 2], LNS2[:, 6 * t:6 * t + 6], [v])
            v = ts(VAR[:, 4 * c:4 * c + 4], LNM2[:, 1:8:2], 1.0, None, ALU.mult, None, S("t_dve"), [v])
            i, bq = pr.take()
            PE.wait(*R4.ready, h)
            for k in range(KT):
                m = mm(bq[0:64, :], WQM[:, k, :], ht[:, k, :], k == 0, k == 3, S("t_pe") if k == 3 else None)
            q = act(QY[c % 2][0:64, :], bq[0:64, :], ACTF.Copy, S("t_act"), [m] + used)
            pr.release(i, q)
            i, bu = pr.take()
            for k in range(KT):
                m = mm(bu[:, :], WU1[:, k, :], ht[:, k, :], k == 0, k == 3, S("t_pe") if k == 3 else None)
            Stage.free[i0] = [m]
            u = act(UG[c % 2], bu[:, :], ACTF.Gelu_apprx_tanh, S("t_act"), [m], bias=BU1)
            pr.release(i, u)
            i, br_ = pr.take()
            m = mm(br_[0:48, :], WRT, QY[c % 2][0:64, :], True, True, S("t_pe"), [q])
            q2 = act(RQ[c % 2][0:48, :], br_[0:48, :], ACTF.Copy, S("t_act"), [m])
            pr.release(i, q2)
            return q, u, q2, v

        def tail_back(c, q, u, q2):
            p = c % 2
            r_, a_, s_, r2_ = RS_[p], AS_[p], SE_[p], R2_[p]
            ir, b_r = sr.take()
            ia, b_a = sr.take()
            PE.wait(q, q2, *R4.setup)
            for t in range(4):
                tok = slice(t * 128, (t + 1) * 128)
                m1 = mm(b_r[:, tok], RQ[p][0:48, tok], RKT, True, True, S("t_pe"))
            for t in range(4):
                tok = slice(t * 128, (t + 1) * 128)
                m2 = mm(b_a[:, tok], QY[p][0:64, tok], AKT, True, True, S("t_pe"))
            il, b_l = pr.take()
            PE.wait(u)
            for t in range(4):
                m3 = mm(b_l[:, t:t + 1], UG[p][:, t * 128:(t + 1) * 128], WU2[:, 0:1], True, True, S("t_pe"))
            lg = ts(LGT[:, 4 * c:4 * c + 4], b_l[:, 0:4], BU2, None, ALU.add, None, S("t_dve"), [m3])
            pr.release(il, lg)
            lrel = LREL.unsqueeze(1).to_broadcast([128, 4, NSLOT])
            a = stt(r_, b_r[:, :].rearrange("p (t n) -> p t n", t=4), float(1.0 / np.sqrt(np.float32(RDIM))), lrel,
                    ALU.mult, ALU.add, S("t_dve"), [m1])
            sr.release(ir, a)
            b = stt(a_, b_a[:, :].rearrange("p (t n) -> p t n", t=4), 0.125, lrel, ALU.mult, ALU.add, S("t_dve"), [m2])
            sr.release(ia, b)
            for t in range(4):
                x = top8(M8[:, 8 * t:8 * t + 8], r_[:, t, :], [a])
            for t in range(4):
                x = strike(r2_[:, t, :], M8[:, 8 * t:8 * t + 8], r_[:, t, :], [x])
            x = tt(s_, r2_, r_, ALU.not_equal, S("t_dve"), [x])
            y = ts(r2_, s_, 1.0, BIG, ALU.subtract, ALU.mult, S("t_dve"), [x])
            x = tt(a_, a_, s_, ALU.mult, S("t_dve"), [b, x])
            x = tt(a_, a_, r2_, ALU.add, S("t_dve"), [x, y])
            x = red(MX4, a_, ALU.max, S("t_dve"), [x])
            x = tt(a_, a_, MX4.unsqueeze(2).to_broadcast([128, 4, NSLOT]), ALU.subtract, S("t_dve"), [x])
            x = act(a_, a_, ACTF.Exp, S("t_act"), [x])
            x = red(SM4, a_, ALU.add, S("t_dve"), [x])
            x = recip(RC4, SM4, S("t_dve"), [x])
            x = tt(a_, a_, RC4.unsqueeze(2).to_broadcast([128, 4, NSLOT]), ALU.mult, S("t_dve"), [x])
            i, bank = sr.take()
            for t in range(4):
                m = tp(bank[:, t * 128:(t + 1) * 128], a_[:, t, :], IDN, S("t_pe"), [x])
            w = act(WT[p], bank[:, :], ACTF.Copy, S("t_act"), [m])
            sr.release(i, w)
            for t in range(4):
                i, bank = br.take()
                m = mm(bank[:, :], WT[p][:, t * 128:(t + 1) * 128], AV3, True, True, S("t_pe"), [w])
                h = act(AO(4 * c + t), bank[:, :], ACTF.Copy, S("t_act"), [m] + R4.ct_used)
                br.release(i, h)
                R4.ao.append(h)
            return m

        def top8(o, i, w):
            DVE.wait(*w)
            return DVE.put(lambda e: e.max(o, i), S("t_dve"))

        def strike(o, v, i, w):
            DVE.wait(*w)
            return DVE.put(lambda e: e.match_replace(o, v, i, -3e38), S("t_dve"))

        def gates(v):
            x = act(GATE, VAR[:, :], ACTF.Ln, S("t_act"), v, bias=1.0, accum_out=TOT[:, 0:1])
            i, bank = pr.take()
            m = mm(bank[:, 0:1], ALL1, TOT[:, 0:1], True, True, S("t_pe"), [x, R4.ones])
            y = ts(TOT[:, 1:2], bank[:, 0:1], 1.0 / T, 1e-6, ALU.mult, ALU.add, S("t_dve"), [m])
            pr.release(i, y)
            y = recip(TOT[:, 2:3], TOT[:, 1:2], S("t_dve"), [y])
            y = ts(GATE, GATE, TOT[:, 2:3], 0.5, ALU.mult, ALU.mult, S("t_dve"), [y, x])
            z = act(VAR, LGT, ACTF.Sigmoid, S("t_act"), [x] + R4.lg)
            y = stt(GATE, VAR, 2.5, GATE, ALU.mult, ALU.add, S("t_dve"), [y, z])
            y = ts(GATE, GATE, 0.0, 5.0, ALU.max, ALU.min, S("t_dve"), [y])
            y = ts(GATE, GATE, 0.5, 1.0 / 1.5, ALU.subtract, ALU.mult, S("t_dve"), [y])
            y = ts(GATE, GATE, 0.0, 1.0, ALU.max, ALU.min, S("t_dve"), [y])
            z = act(VAR, GATE, ACTF.Sigmoid, S("t_act"), [y], scale=GWT, bias=GBT)
            return stt(GATE, VAR, 0.05, VAR, ALU.is_ge, ALU.mult, S("t_dve"), [z])

        def setup_l1():
            i, st = stage()
            m = dma(st[:, 0:128], din["qnw"].to_broadcast([128, 128]), S(f"stg{i}"))
            m = dma(st[:, 128:256], din["knw"].to_broadcast([128, 128]), S(f"stg{i}"))
            for half in range(2):
                mk = dma(MASK1[64 * half:64 * half + 64, :], din["mask1"], S("mask1"), G.kf_free)
            w = st[:, 256:384]
            a = tt(w, st[:, 0:128], st[:, 128:256], ALU.mult, S("l1"), [m])
            a = red(AMX[:, 0:1], w, ALU.max, S("amx"), [a] + list(am_free[0]), absv=True)
            b = norm_scale(PWN[:, 0:1], PWN[:, 1:2], AMX[:, 0:1], a)
            am_free[0] = [b]
            a = ts(WQK, w, PWN[:, 1:2], None, ALU.mult, None, S("l1"), [b] + G.kf_free)
            a = ts(PWN[:, 2:3], PWN[:, 0:1], ISQ, None, ALU.mult, None, S("l1"), [a])
            Stage.free[i] = [a]
            G.wqk = [a, mk]

        if STAGES >= 3:
            setup_l1()
            G.qt_used = G.kt_used = G.v_used[0] = F.gu0_used
            G.rt_free[0] = G.rt_free[1] = G.ss_free = G.sq_used = G.pt_used = G.at_used = F.last

            def after1(u):
                g, c = divmod(u, NC)
                if g + 1 < NKV and c < 3:
                    prep_weight(1, g + 1, c)
                if STAGES >= 4 and g == NKV - 1 and c == 0:
                    tail_loads()

            attention(1, lambda u: None, after1)

        ov = out.rearrange("(t p) d -> p t d", p=128)
        if STAGES >= 4:
            used = G.qt_used + G.kt_used + G.v_used[0] + G.v_used[1] + G.pt_used + G.at_used + G.ss_free + \
                G.m1_free[0] + G.m1_free[1] + G.sq_used + G.kf_free
            R4.ct_used, R4.ao = G.w_used[1], []
            tail_setup()
            R4.lg = []
            vs = []
            prev = None
            for c in range(NC):
                q, u, q2, v = tail_front(c, used)
                vs.append(v)
                if prev:
                    tail_back(*prev)
                prev = (c, q, u, q2)
            tail_back(*prev)
            R4.lg = [(S("t_dve"), S("t_dve").count)]
            gm = gates([vs[-1]])
            for t in range(16):
                xs = X[:, t, :]
                XM[t] = stt(xs, AO(t), GATE[:, t:t + 1], xs, ALU.mult, ALU.add, S("fin"), [gm, R4.ao[t], XM[t]])

        for t in range(16):
            dma(ov[:, t, :], X[:, t, :], S("out"), [XM[t]])
        SP.wait((S("out"), S("out").count))

        block = ctx.enter_context(nc.Block())
        block.sync(SP.run)
        block.tensor(PE.run)
        block.scalar(ACT.run)
        block.vector(DVE.run)
        block.gpsimd(POOL.run)


def _constants():
    f = np.float32
    inv = f(1.0) / np.power(f(10000.0), np.arange(0, DH, 2, dtype=f) / f(DH)).astype(f)
    ang = np.arange(SQ, dtype=f)[:, None] * inv[None, :]
    cos = np.concatenate([np.cos(ang), np.cos(ang)], axis=-1).astype(f)
    sin = np.concatenate([-np.sin(ang), np.sin(ang)], axis=-1).astype(f)
    c = np.zeros((128, 516), f)
    c[:, 0:128] = np.eye(128)
    c[:, 128:192] = cos.T
    c[:, 192:256] = sin.T
    c[:, 256:384] = np.concatenate([cos, cos], axis=0)
    c[:, 384:512] = np.concatenate([sin, sin], axis=0)
    p = np.arange(128)
    c[:, 512] = np.where((p % 32 < 4) & (p < 64), p % 32, -1)
    c[:, 513] = np.where((p % 32 < 10) & (p < 64), p % 32, -1)
    c[:, 514] = 1.0
    return c, (4 * (p % 8)).astype(np.uint32).reshape(128, 1)


def kernel(**inputs):
    import concourse.bacc as bacc
    from concourse.bass_utils import run_bass_kernel_spmd

    a = {k: np.asarray(v) for k, v in inputs.items()}
    cf, cu = _constants()
    arrays = {
        "const_f": cf,
        "const_u": cu,
        "x": a["x"].reshape(T, D),
        "ctxT": a["ctx_4096"].reshape(T, D).T,
        "mask0": a["mask_BxSxS2_ff1"],
        "mask1": a["mask_1x1xSxS2_ff0"].reshape(SQ, SQ),
        "scales_gu": a["L0_ffn_scales_gu"], "scales_d": a["L0_ffn_scales_down"],
        "qzeros_gu": a["L0_ffn_qzeros_gu"], "qzeros_d": a["L0_ffn_qzeros_down"],
        "qw_gu": a["L0_ffn_qweight_gu"], "qw_d": a["L0_ffn_qweight_down"],
        "gidx_gu": a["L0_ffn_g_idx_gu"], "gidx_d": a["L0_ffn_g_idx_down"],
        "wq0": a["L0_xattn_wq"], "wk0": a["L0_xattn_wk"], "wv0": a["L0_xattn_wv"], "wo0": a["L0_xattn_wo"],
        "wq1": a["L1_xattn_q_proj_w"].T, "wk1": a["L1_xattn_k_proj_w"].T, "wv1": a["L1_xattn_v_proj_w"].T,
        "wo1": a["L1_xattn_o_proj_w"].T, "qnw": a["L1_xattn_q_norm_w"].reshape(1, 128),
        "knw": a["L1_xattn_k_norm_w"].reshape(1, 128),
        "wqm": a["L1_ffn_Wq"].T, "wu1": a["L1_ffn_Wu1"].T, "avT": a["L1_ffn_aux_values"].T,
        "wvd": a["L1_ffn_Wvd"].T, "wrT": a["L1_ffn_Wr"].T, "akT": a["L1_ffn_aux_keys"].T,
        "wvu": a["L1_ffn_Wvu"].T, "wu2": a["L1_ffn_Wu2"].T, "bu1": a["L1_ffn_bu1"].reshape(128, 1),
        "log_rel": a["L1_ffn_log_rel"].reshape(1, NSLOT), "bu2": a["L1_ffn_bu2"].reshape(1, 1),
        "gate_w1": a["L1_ffn_gate_w1"].reshape(1, 1), "gate_bias": a["L1_ffn_gate_bias"].reshape(1, 1),
    }
    arrays = {k: np.ascontiguousarray(v) for k, v in arrays.items()}
    nc = bacc.Bacc("TRN2", target_bir_lowering=False, num_devices=1)
    din = {k: nc.dram_tensor("in_" + k, v.shape, mybir.dt.from_np(v.dtype), kind="ExternalInput").ap()
           for k, v in arrays.items()}
    out = nc.dram_tensor("out_x", (T, D), F32, kind="ExternalOutput").ap()
    build(nc, din, out)
    r = run_bass_kernel_spmd(nc, [{"in_" + k: v for k, v in arrays.items()}], core_ids=[0])
    return r.results[0]["out_x"].reshape(NB, SQ, D)
```

```python
from contextlib import ExitStack

import numpy as np

import concourse.bass as bass
from concourse import mybir

F32 = mybir.dt.float32
F16 = mybir.dt.float16
BF16 = mybir.dt.bfloat16
U32 = mybir.dt.uint32
I32 = mybir.dt.int32
U8 = mybir.dt.uint8
ALU = mybir.AluOpType
ACTF = mybir.ActivationFunctionType
AX = mybir.AxisListType.X
RMAX = bass.bass_isa.ReduceOp.max

NB, SQ, D = 32, 64, 512
T = NB * SQ
NH, NKV, DH = 32, 8, 128
KT = D // 128
TC = 512
NC = T // TC
BC = TC // SQ
INTER = 1376
FT = 11
NSLOT, BOT, RDIM, VB = 128, 64, 48, 32
LN_EPS = 1e-5
ISQ = float(1.0 / np.sqrt(np.float32(DH)))
BIG = 1e30
STAGES = 4


class Sem:

    def __init__(self, handle):
        self.handle, self.count = handle, 0


class Queue:

    def __init__(self):
        self.ops, self.seen = [], {}

    def wait(self, *marks):
        for sem, n in marks:
            if self.seen.get(id(sem), 0) < n:
                self.seen[id(sem)] = n
                self.ops.append((None, sem.handle, n))

    def put(self, fn, sem=None, n=1):
        self.ops.append((fn, sem.handle if sem else None, n))
        if sem:
            sem.count += n
            return (sem, sem.count)
        return None

    def run(self, eng):
        for fn, handle, n in self.ops:
            if fn is None:
                eng.wait_ge(handle, n)
            elif handle is None:
                fn(eng)
            else:
                fn(eng).then_inc(handle, n)


def build(nc, din, out):
    ctx = ExitStack()
    with ctx:
        def sb(name, shape, dt):
            return ctx.enter_context(nc.sbuf_tensor(name, shape, dt))

        sems = {}

        def S(name):
            if name not in sems:
                sems[name] = Sem(ctx.enter_context(nc.semaphore("s_" + name)))
            return sems[name]

        PE, ACT, DVE, POOL, SP = Queue(), Queue(), Queue(), Queue(), Queue()

        def mm(o, l, r, start, stop, sem=None, w=()):
            PE.wait(*w)
            return PE.put(lambda e: e.matmul(o, l, r, start=start, stop=stop), sem)

        def tp(o, i, ident, sem=None, w=()):
            PE.wait(*w)
            return PE.put(lambda e: e.transpose(o, i, ident), sem)

        def act(o, i, f, sem=None, w=(), **kw):
            ACT.wait(*w)
            return ACT.put(lambda e: e.activation(o, i, f, **kw), sem)

        def tt(o, a, b, op, sem=None, w=(), q=None):
            q = q or DVE
            q.wait(*w)
            return q.put(lambda e: e.tensor_tensor(o, a, b, op), sem)

        def ts(o, a, s1, s2, op0, op1, sem=None, w=(), q=None):
            q = q or DVE
            q.wait(*w)
            if op1 is None:
                return q.put(lambda e: e.tensor_scalar(o, a, s1, None, op0), sem)
            return q.put(lambda e: e.tensor_scalar(o, a, s1, s2, op0, op1), sem)

        def stt(o, a, s, b, op0, op1, sem=None, w=()):
            DVE.wait(*w)
            return DVE.put(lambda e: e.scalar_tensor_tensor(o, a, s, b, op0, op1), sem)

        def red(o, i, op, sem=None, w=(), absv=False):
            DVE.wait(*w)
            if absv:
                return DVE.put(lambda e: e.tensor_reduce(o, i, AX, op, apply_absolute_value=True), sem)
            return DVE.put(lambda e: e.tensor_reduce(o, i, AX, op), sem)

        def recip(o, i, sem=None, w=()):
            DVE.wait(*w)
            return DVE.put(lambda e: e.reciprocal(o, i), sem)

        def fill(o, v, sem=None, w=(), q=None):
            q = q or DVE
            q.wait(*w)
            return q.put(lambda e: e.memset(o, v), sem)

        def dma(o, i, sem, w=(), q=None):
            q = q or SP
            q.wait(*w)
            return q.put(lambda e: e.dma_start(o, i), sem, 16)

        def allmax(o, i, sem, w=()):
            POOL.wait(*w)
            return POOL.put(lambda e: e.partition_all_reduce(o, i, 128, RMAX), sem)

        X = sb("X", [128, T // 128, D], F32)
        CT = [sb(f"CT{i}", [128, KT, T], F16) for i in range(2)]
        XT = [sb(f"XT{i}", [128, KT, T], F16) for i in range(2)]
        WB = [sb(f"WB{i}", [128, 10240], F16) for i in range(2)]
        STG = sb("STG", [128, 4096], F32)
        AR = sb("AR", [128, 11776], F32)
        LNB = sb("LNB", [128, 2, D], F32)
        CST = sb("CST", [128, 516], F32)
        SHC = sb("SHC", [128, 1], U32)
        SML = sb("SML", [128, 256], F32)
        ONEB = sb("ONEB", [128, 2], BF16)
        PB = [ctx.enter_context(nc.psum_tensor(f"PB{i}", [128, 512], F32)) for i in range(8)]

        IDN = CST[:, 0:128]
        COST, SINT = CST[:, 128:192], CST[:, 192:256]
        COSK, SINK = CST[:, 256:384], CST[:, 384:512]
        IDXG, IDXD = CST[:, 512:513], CST[:, 513:514]
        ONEF = CST[:, 514:515]

        small = [0]

        def sm(n):
            a = small[0]
            small[0] += n
            assert small[0] <= 256
            return SML[:, a:a + n]

        arena = [0]

        def view(words, dt, **dims):
            a = arena[0]
            arena[0] += words
            assert arena[0] <= 11776, arena[0]
            v = AR[:, a:a + words]
            return v if dt == F32 else v.bitcast(dt)

        def wset(i):
            w = WB[i]
            q = [w[:, n * 2048:(n + 1) * 2048].rearrange("p (k n) -> p k n", k=4) for n in range(2)]
            kv = [w[:, 4096 + n * 1024:4096 + (n + 1) * 1024].rearrange("p (k n) -> p k n", k=4) for n in range(2)]
            o = [w[:, 6144 + n * 2048:6144 + (n + 1) * 2048].rearrange("p (k n) -> p k n", k=4) for n in range(2)]
            return q, kv, o

        WSET = [wset(0), wset(1)]

        bank_free = [()] * 8

        class Ring:

            def __init__(self, banks):
                self.banks, self.n = banks, 0

            def take(self):
                i = self.banks[self.n % len(self.banks)]
                self.n += 1
                PE.wait(*bank_free[i])
                return i, PB[i]

            def release(self, i, *marks):
                bank_free[i] = marks

        ring = Ring(list(range(8)))

        c_cst = dma(CST[:, :], din["const_f"], S("cst"))
        c_sh = dma(SHC[:, :], din["const_u"], S("cst2"))
        XM = [None] * 16
        xv = din["x"].rearrange("(t p) d -> p t d", p=128)
        for c in range(NC):
            m = dma(X[:, 4 * c:4 * c + 4, :], xv[:, 4 * c:4 * c + 4, :], S(f"x{c}"))
            for t in range(4):
                XM[4 * c + t] = m
        c_one = fill(ONEB[:, :], 1.0, S("one"))

        NRM = sm(4)

        def norm_scale(p, r, am, mark, mul=1.0):
            a = allmax(NRM[:, 0:1], am, S("ns_all"), [mark] + norm_scale.last)
            a = ts(NRM[:, 1:2], NRM[:, 0:1], 2.0 ** -100, 2.0 ** 100, ALU.max, ALU.min, S("ns"), [a])
            a = ts(NRM[:, 2:3].bitcast(U32), NRM[:, 1:2].bitcast(U32), 0x7F800000, None, ALU.bitwise_and, None,
                   S("ns"), [a])
            a = ts(p, NRM[:, 2:3], mul, None, ALU.mult, None, S("ns"), [a])
            b = recip(r, p, S("ns"), [a])
            norm_scale.last = [b]
            return b

        norm_scale.last = []

        class Stage:
            free = [(), ()]
            n = 0

        def stage():
            i = Stage.n % 2
            Stage.n += 1
            SP.wait(*Stage.free[i])
            return i, STG[:, i * 2048:(i + 1) * 2048]

        CTP, CTR, AMX = sm(4), sm(4), sm(2)
        CT_ready = [None] * NC
        CT_scaled = [None] * NC
        am_free = [()]

        def load_ctx(c):
            i, st = stage()
            m = dma(st.rearrange("p (k t) -> p k t", k=4),
                    din["ctxT"].rearrange("(k p) t -> p k t", p=128)[:, :, c * TC:(c + 1) * TC], S(f"stg{i}"))
            a = red(AMX[:, 0:1], st, ALU.max, S("amx"), [m] + list(am_free[0]), absv=True)
            b = norm_scale(CTP[:, c:c + 1], CTR[:, c:c + 1], AMX[:, 0:1], a)
            am_free[0] = [b]
            marks = []
            for k in range(KT):
                hi, lo = [CT[n][:, k, c * TC:(c + 1) * TC] for n in range(2)]
                src = st[:, k * TC:(k + 1) * TC]
                h = act(hi, src, ACTF.Copy, S("ct_hi"), [b], scale=CTR[:, c:c + 1])
                l = stt(lo, src, CTR[:, c:c + 1], hi, ALU.mult, ALU.subtract, S("ct_lo"), [h, b])
                marks += [h, l]
            Stage.free[i] = marks[-2:]
            CT_ready[c], CT_scaled[c] = marks[-2:], b

        LNS, LNM, LNV, LNR, LNC = sm(24), sm(8), sm(4), sm(4), sm(4)
        ln_free = [[], []]
        XT_ready = [None] * NC
        XT_used = [[] for _ in range(NC)]
        c_half = fill(LNC[:, :], -0.5, S("one"))
        lns_free = [[]]

        def ln_stats(c):
            for t in range(4):
                a = DVE_bn(LNS[:, 6 * t:6 * t + 6], X[:, 4 * c + t, :], [XM[4 * c + t]] + lns_free[0])
            for t in range(4):
                a = DVE_agg(LNM[:, 2 * t:2 * t + 2], LNS[:, 6 * t:6 * t + 6], [a])
            a = ts(LNV[:, :], LNM[:, 1:8:2], LN_EPS, None, ALU.add, None, S("ln"), [a])
            return tt(LNR[:, :], LNV[:, :], LNC[:, :], ALU.pow, S("ln_pow"), [a, c_half], q=POOL)

        def DVE_bn(o, i, w):
            DVE.wait(*w)
            return DVE.put(lambda e: e.bn_stats(o, i), S("ln"))

        def DVE_agg(o, i, w):
            DVE.wait(*w)
            return DVE.put(lambda e: e.bn_aggr(o, i), S("ln"))

        def ln_chunk(c):
            r = ln_stats(c)
            marks = []
            for t in range(4):
                b = LNB[:, t % 2, :]
                n = ts(b, X[:, 4 * c + t, :], LNM[:, 2 * t:2 * t + 1], LNR[:, t:t + 1], ALU.subtract, ALU.mult,
                       S("ln_x"), [r] + ln_free[t % 2])
                lns_free[0] = [n]
                i, bank = ring.take()
                for k in range(KT):
                    m = tp(bank[:, k * 128:(k + 1) * 128], b[:, k * 128:(k + 1) * 128], IDN, S("ln_t"), [n, c_cst])
                ln_free[t % 2] = [m]
                src = bank[:, :].rearrange("p (k t) -> p k t", k=4)
                hi, lo = [XT[n][:, :, (4 * c + t) * 128:(4 * c + t + 1) * 128] for n in range(2)]
                h = act(hi, src, ACTF.Copy, S("xt_hi"), [m] + XT_used[c])
                l = tt(lo, src, hi, ALU.subtract, S("xt_lo"), [h])
                ring.release(i, l)
                marks = [h, l]
            XT_ready[c] = marks

        QT = [view(1024, F16) for _ in range(2)]
        KTT = [view(256, F16) for _ in range(2)]
        V = [[view(256, F16).rearrange("p (t d) -> p t d", t=4) for _ in range(2)] for _ in range(2)]
        KF = view(512, F32).rearrange("p (t d) -> p t d", t=4)
        KR = view(512, F32).rearrange("p (t d) -> p t d", t=4)
        M1 = [view(512, F32) for _ in range(2)]
        RT_all = view(1024, F32)
        RT = [RT_all[:, 0:512], RT_all[:, 512:1024]]
        SS = view(1024, F32).rearrange("p (a n) -> p a n", a=2)
        PT = [view(512, F16).rearrange("p (a b n) -> p a b n", a=2, b=4) for _ in range(2)]
        AT = [view(1024, F16).rearrange("p (h t) -> p h t", h=4) for _ in range(2)]
        MK = view(1024, F32)
        M01 = MK[:, 0:512].bitcast(U8).rearrange("p (b k) -> p b k", b=NB)
        MNO = MK[:, 512:1024].bitcast(U8).rearrange("p (b k) -> p b k", b=NB)
        SQH = MK.bitcast(BF16)
        SQL = RT_all.bitcast(BF16)
        MASK1, WQK = KR[:, 0, 0:64], KR[:, 1, :]
        MXT, SMT, RCT, RSQ, KSS, RSK = sm(16), sm(16), sm(16), sm(16), sm(4), sm(4)
        HLF = sm(16)
        WSC = sm(24)
        CO = sm(16)
        c_hlf = fill(HLF, -0.5, S("one"))
        

        def rows_of(t, pair, b):
            return t[:, (pair * BC + b) * 128:(pair * BC + b + 1) * 128]

        def head_of(t, h):
            return t.rearrange("p (a b h q) -> p a b h q", a=2, b=BC, h=2)[:, h // 2, :, h % 2, :]

        def by_batch(t):
            return t.rearrange("p (b s) -> p b s", s=SQ)

        class G:
            w_used = [[], [], [], [], [], []]
            qt_used, kt_used, v_used = [], [], [[], []]
            kf_free, m1_free, rt_free = [], [[], []], [[], []]
            ss_free, pt_used, at_used = [], [], []
            sml_free, sq_used = [], []
            late, late_lo = [], []

        def flush():
            todo, G.late = G.late, []
            for f in todo:
                f()

        def flush_lo():
            todo, G.late_lo = G.late_lo, []
            for f in todo:
                f()

        W_ready = {}

        def prep_steps(L, g, kind):
            par = (g + L) % 2
            q, kv, o = WSET[par]
            i, st = stage()
            s4 = st.rearrange("p (k n) -> p k n", k=4)
            if kind == 0:
                m = dma(s4, din[f"wq{L}"].rearrange("(k p) n -> p k n", p=128)[:, :, g * 512:(g + 1) * 512], S(f"stg{i}"))
                n, dst = 512, q
            elif kind == 1:
                s4 = st[:, 0:1024].rearrange("p (k n) -> p k n", k=4)
                for j, nm in enumerate(("wk", "wv")):
                    m = dma(s4[:, :, j * 128:(j + 1) * 128],
                            din[f"{nm}{L}"].rearrange("(k p) n -> p k n", p=128)[:, :, g * 128:(g + 1) * 128],
                            S(f"stg{i}"))
                n, dst = 256, kv
            else:
                m = dma(s4, din[f"wo{L}"].rearrange("(h p) n -> p h n", p=128)[:, 4 * g:4 * g + 4, :], S(f"stg{i}"))
                n, dst = 512, o
            yield
            a = red(AMX[:, 0:1], st[:, 0:4 * n], ALU.max, S("amx"), [m] + list(am_free[0]), absv=True)
            yield
            col = par * 12 + kind * 4
            b = norm_scale(WSC[:, col:col + 1], WSC[:, col + 1:col + 2], AMX[:, 0:1], a)
            am_free[0] = [b]
            r = WSC[:, col + 1:col + 2]
            used = G.w_used[par * 3 + kind]
            hs = [act(dst[0][:, k, :], s4[:, k, :], ACTF.Copy, S("w_hi"), [b] + used, scale=r) for k in range(4)]
            ls = []
            for half in range(2):
                yield
                ls += [stt(dst[1][:, k, :], s4[:, k, :], r, dst[0][:, k, :], ALU.mult, ALU.subtract, S("w_lo"), [hs[k]])
                       for k in (2 * half, 2 * half + 1)]
            Stage.free[i] = [ls[-1]]
            W_ready[(L, g, kind)] = [hs[-1], ls[-1]]
            if kind == 2:
                p_q, p_kv = [WSC[:, par * 12 + 4 * k:par * 12 + 4 * k + 1] for k in range(2)]
                r_q, r_kv = [WSC[:, par * 12 + 4 * k + 1:par * 12 + 4 * k + 2] for k in range(2)]
                e_q, e_kv = WSC[:, par * 12 + 2:par * 12 + 3], WSC[:, par * 12 + 3:par * 12 + 4]
                if L == 0:
                    a = ts(e_q, p_q, p_kv, ISQ, ALU.mult, ALU.mult, S("co"), [b] + G.co_used[par])
                else:
                    a = ts(e_q, r_q, r_q, LN_EPS, ALU.mult, ALU.mult, S("co"), [b] + G.co_used[par])
                    a = ts(e_kv, r_kv, r_kv, LN_EPS, ALU.mult, ALU.mult, S("co"), [b])
                W_ready[(L, g, 3)] = [a]

        def unit_scales(L, g, c):
            par = (g + L) % 2
            co, w = CO[:, par * 8:par * 8 + 8], [CT_scaled[c]] + W_ready[(L, g, 3)] + G.co_used[par]
            p_kv, p_o = [WSC[:, par * 12 + 4 * k:par * 12 + 4 * k + 1] for k in (1, 2)]
            a = ts(co[:, c:c + 1], CTP[:, c:c + 1], p_kv, p_o, ALU.mult, ALU.mult, S("co"), w)
            if L == 0:
                a = ts(co[:, 4 + c:5 + c], CTP[:, c:c + 1], WSC[:, par * 12 + 2:par * 12 + 3], None, ALU.mult, None, S("co"))
            else:
                a = ts(co[:, 4 + c:5 + c], CTR[:, c:c + 1], WSC[:, par * 12 + 3:par * 12 + 4], CTR[:, c:c + 1],
                       ALU.mult, ALU.mult, S("co"))
            G.co_ready = [a]

        def prep_weight(L, g, kind):
            for _ in prep_steps(L, g, kind):
                pass

        G.co_used = [[], []]
        PWN = sm(4)

        def kv_proj(L, g, c, uv, co_ready, between):
            par = (g + L) % 2
            wkv = WSET[par][1]
            ready = W_ready[(L, g, 1)] + CT_ready[c]
            vd, vmarks = V[uv], []
            banks = []
            for half in range(2):
                i, bank = ring.take()
                PE.wait(*ready)
                for t2 in range(2):
                    tok = slice((4 * c + 2 * half + t2) * 128, (4 * c + 2 * half + t2 + 1) * 128)
                    o = bank[:, t2 * 256:(t2 + 1) * 256]
                    n = 0
                    for k in range(KT):
                        for a, b in ((0, 0), (0, 1), (1, 0)):
                            m = mm(o, CT[a][:, k, tok], wkv[b][:, k, :], n == 0, n == 11,
                                   S("kv") if n == 11 else None)
                            n += 1
                src = bank[:, :].rearrange("p (t n) -> p t n", t=2)
                tsl = slice(2 * half, 2 * half + 2)
                h = act(vd[0][:, tsl, :], src[:, :, 128:256], ACTF.Copy, S("v_hi"), [m] + G.v_used[uv])
                if L == 0:
                    def bc(x):
                        return x.unsqueeze(1).to_broadcast([128, 2, x.shape[1]])
                    k1 = tt(KF[:, tsl, :], src[:, :, 0:128], bc(COSK), ALU.mult, S("k_e"), [h, c_cst] + G.kf_free)
                    tt(KR[:, tsl, 0:64], src[:, :, 64:128], bc(SINK[:, 0:64]), ALU.mult, S("k_e"), G.kf_free)
                    k2 = tt(KR[:, tsl, 64:128], src[:, :, 0:64], bc(SINK[:, 64:128]), ALU.mult, S("k_e"))
                else:
                    for t2 in range(2):
                        t = 2 * half + t2
                        k1 = act(M1[0][:, 0:128], src[:, t2, 0:128], ACTF.Square, S("k_sq"),
                                 [m] + G.m1_free[0] + G.kss_used, accum_out=KSS[:, t:t + 1])
                        G.m1_free[0] = [k1]
                    k2 = tt(KF[:, tsl, :], src[:, :, 0:128], WQK.unsqueeze(1).to_broadcast([128, 2, 128]), ALU.mult,
                            S("k_e"), [k1] + G.kf_free + G.wqk)
                l = tt(vd[1][:, tsl, :], src[:, :, 128:256], vd[0][:, tsl, :], ALU.subtract, S("v_lo"), [h])
                ring.release(i, h, l, k1, k2)
                vmarks = [h, l]
                if half == 0:
                    between()
            kk = [k1, k2]
            G.w_used[par * 3 + 1] = [m]
            if L == 0:
                k = tt(KF[:, :, :], KF[:, :, :], KR[:, :, :], ALU.add, S("k_add"), kk, q=POOL)
            else:
                a = ts(KSS[:, :], KSS[:, :], 1.0 / DH, CO[:, par * 8 + 4 + c:par * 8 + 5 + c], ALU.mult, ALU.add,
                       S("k_ms"), [k1] + co_ready)
                a = tt(RSK[:, :], KSS[:, :], HLF[:, 0:4], ALU.pow, S("k_pow"), [a, c_hlf] + G.kss_used, q=POOL)
                k = tt(KF[:, :, :], KF[:, :, :], RSK[:, :].unsqueeze(2).to_broadcast([128, 4, 128]), ALU.mult,
                       S("k_add"), [a, k2], q=POOL)
                G.kss_used = [k]
            return k, vmarks

        G.kss_used, G.wqk = [], []

        def k_turn(k):
            i, bank = ring.take()
            for t in range(4):
                m = tp(bank[:, t * 128:(t + 1) * 128], KF[:, t, :], IDN, S("k_t"), [k])
            G.kf_free = [m]
            h = act(KTT[0], bank[:, :], ACTF.Copy, S("kt_hi"), [m] + G.kt_used)
            l = tt(KTT[1], bank[:, :], KTT[0], ALU.subtract, S("kt_lo"), [h])
            ring.release(i, h, l)
            return [h, l]

        def q_proj(L, g, c, h, marks):
            par = (g + L) % 2
            wq = WSET[par][0]
            i, bank = ring.take()
            PE.wait(*W_ready[(L, g, 0)], *XT_ready[c])
            n = 0
            for k in range(KT):
                for a, b in ((0, 0), (0, 1), (1, 0)):
                    m = mm(bank[:, :], wq[a][:, k, h * 128:(h + 1) * 128], XT[b][:, k, c * TC:(c + 1) * TC],
                           n == 0, n == 11, S("q") if n == 11 else None)
                    n += 1
            if h == 3:
                G.w_used[par * 3] = [m]
                XT_used[c] = [m]
            m1, rt = M1[h % 2], RT[h % 2]
            v3 = bank[:, :].rearrange("p (b s) -> p b s", s=SQ)
            if L == 0:
                r1 = act(rt[0:64, :], bank[64:128, :], ACTF.Copy, S("q_rot"), [m] + G.rt_free[h % 2])
                r2 = act(rt[64:128, :], bank[0:64, :], ACTF.Copy, S("q_rot"))
                c1 = tt(m1.rearrange("p (b s) -> p b s", s=SQ), v3, COST.unsqueeze(1).to_broadcast([128, BC, SQ]),
                        ALU.mult, S("q_cos"), [r2, c_cst] + G.m1_free[h % 2])
                ring.release(i, r2, c1)
                r3v = rt.rearrange("p (b s) -> p b s", s=SQ)
                r3 = tt(r3v, r3v, SINT.unsqueeze(1).to_broadcast([128, BC, SQ]), ALU.mult, S("q_sin"), [r2], q=POOL)

                def finish():
                    a = tt(m1, m1, rt, ALU.add, S("q_add"), [c1, r3])
                    G.rt_free[h % 2] = [a]
                    hi = act(head_of(QT[0], h), by_batch(m1), ACTF.Copy, S("qt_hi"), [a] + G.qt_used)

                    def finish_lo():
                        lo = tt(head_of(QT[1], h), by_batch(m1), head_of(QT[0], h), ALU.subtract, S("qt_lo"), [hi])
                        G.m1_free[h % 2] = [lo]
                        marks.extend([hi, lo])
                    G.late_lo.append(finish_lo)
                G.late.append(finish)
            else:
                hi = act(head_of(QT[0], h), v3, ACTF.Copy, S("qt_hi"), [m] + G.qt_used)
                s1 = act(m1, bank[:, :], ACTF.Square, S("q_sq"), G.m1_free[h % 2])
                s2 = act(head_of(SQH, h), v3, ACTF.Square, S("q_sq"), G.sq_used)
                lo = tt(head_of(QT[1], h), v3, head_of(QT[0], h), ALU.subtract, S("qt_lo"), [s2])
                ring.release(i, s2, lo)
                s3 = tt(head_of(SQL, h), by_batch(m1), head_of(SQH, h), ALU.subtract, S("q_sql"), [s1, s2] + G.sq_used, q=POOL)
                G.m1_free[h % 2] = [s3]
                marks.extend([hi, lo])
                G.sq_ready = [s2, s3]

        def q_norm(L, g):
            par = (g + L) % 2
            i, bank = ring.take()
            PE.wait(*G.sq_ready, c_one)
            for pair in range(2):
                for b in range(BC):
                    o = bank[:, pair * BC + b:pair * BC + b + 1]
                    for n, s in enumerate((SQH, SQL)):
                        m = mm(o, rows_of(s, pair, b), ONEB[:, 0:1], n == 0, n == 1,
                               S("q_ss") if n else None)
            G.sq_used = [m]
            a = ts(RSQ[:, :], bank[:, 0:16], 1.0 / DH, WSC[:, par * 12 + 2:par * 12 + 3], ALU.mult, ALU.add,
                   S("q_ms"), [m] + G.rsq_used + W_ready[(L, g, 3)])
            ring.release(i, a)
            return tt(RSQ[:, :], RSQ[:, :], HLF, ALU.pow, S("q_pow"), [a, c_hlf], q=POOL)

        G.rsq_used = []

        def scores(ready, d):
            banks = []
            for pair in range(2):
                i, bank = ring.take()
                PE.wait(*ready)
                for b in range(BC):
                    o = bank[:, b * SQ:(b + 1) * SQ]
                    for n, (x, y) in enumerate(((0, 0), (0, 1), (1, 0))):
                        m = mm(o, rows_of(QT[x], pair, b), KTT[y][:, b * SQ:(b + 1) * SQ],
                               n == 0, n == 2, S("s") if n == 2 else None)
                banks.append((i, bank, m))
            G.qt_used = G.kt_used = [m]
            d["s"] = banks

        def soft_max(L, c, d):
            par, banks, rsq = d["par"], d["s"], d["rsq"]
            co = CO[:, par * 8:par * 8 + 8]
            bsl = slice(c * BC, (c + 1) * BC)
            v = [by_batch(SS[:, pair, :]) for pair in range(2)]
            mx = [MXT[:, pair * BC:(pair + 1) * BC] for pair in range(2)]
            a = [None, None]
            for pair, (i, bank, m) in enumerate(banks):
                b3 = by_batch(bank[:, :])
                if L == 0:
                    a[pair] = stt(v[pair], b3, co[:, 4 + c:5 + c], M01[:, bsl, :], ALU.mult, ALU.mult, S("sm"),
                                  [m] + G.ss_free + d["co"] + G.mask_ready)
                else:
                    a[pair] = tt(v[pair], b3, RSQ[:, pair * BC:(pair + 1) * BC].unsqueeze(2).to_broadcast([128, BC, SQ]),
                                 ALU.mult, S("sm"), [m, rsq] + G.ss_free)
                ring.release(i, a[pair])
            G.rsq_used = [a[1]]
            for pair in range(2):
                if L == 0:
                    a[pair] = stt(v[pair], MNO[:, bsl, :], -1e9, v[pair], ALU.mult, ALU.add, S("sm"), [a[pair]])
                else:
                    a[pair] = stt(v[pair], v[pair], PWN[:, 2:3], MASK1.unsqueeze(1).to_broadcast([128, BC, SQ]), ALU.mult,
                                  ALU.add, S("sm"), [a[pair]] + G.wqk)
            for pair in range(2):
                d["mx"] = a[pair] = red(mx[pair], v[pair], ALU.max, S("sm"), [a[pair]])

        def soft_exp(d):
            d["e"] = []
            for pair in range(2):
                s, mx = SS[:, pair, :], MXT[:, pair * BC:(pair + 1) * BC]
                a = tt(by_batch(s), by_batch(s), mx.unsqueeze(2).to_broadcast([128, BC, SQ]), ALU.subtract, S("sm"),
                       [d["mx"]])
                d["e"].append(act(s, s, ACTF.Exp, S("exp"), [a]))

        def soft_norm(d):
            cols = [slice(pair * BC, (pair + 1) * BC) for pair in range(2)]
            v = [by_batch(SS[:, pair, :]) for pair in range(2)]
            a = [red(SMT[:, cols[p]], v[p], ALU.add, S("sm"), [d["e"][p]]) for p in range(2)]
            a = [recip(RCT[:, cols[p]], SMT[:, cols[p]], S("sm"), [a[p]] + G.sml_free) for p in range(2)]
            ps = [tt(v[p], v[p], RCT[:, cols[p]].unsqueeze(2).to_broadcast([128, BC, SQ]), ALU.mult, S("p_n"),
                     [a[p]], q=POOL) for p in range(2)]
            G.sml_free = [ps[-1]]
            return ps

        def p_turn(ps):
            marks = []
            for pair in range(2):
                i, bank = ring.take()
                for b2 in range(4):
                    m = tp(bank[:, b2 * 128:(b2 + 1) * 128], SS[:, pair, b2 * 128:(b2 + 1) * 128], IDN, S("p_t"),
                           [ps[pair]])
                src = bank[:, :].rearrange("p (b n) -> p b n", b=4)
                h = act(PT[0][:, pair, :, :], src, ACTF.Copy, S("pt_hi"), [m] + G.pt_used)
                l = tt(PT[1][:, pair, :, :], src, PT[0][:, pair, :, :], ALU.subtract, S("pt_lo"), [h])
                ring.release(i, h, l)
                marks += [h, l]
            G.ss_free = [m]
            return marks

        def pv(uv, ready):
            vd = V[uv]
            halves = []
            for j in range(2):
                marks = []
                bk = [ring.take(), ring.take()]
                PE.wait(*ready)
                for jj in range(2):
                    b2 = 2 * j + jj
                    for n, (x, y) in enumerate(((0, 0), (0, 1), (1, 0))):
                        for odd in range(2):
                            rows = slice(64 * odd, 64 * odd + 64)
                            m = mm(bk[odd][1][:, jj * 256:(jj + 1) * 256], vd[x][rows, b2, :], PT[y][rows, :, b2, :],
                                   n == 0, n == 2, S("pv") if n == 2 else None)
                for odd in range(2):
                    i, bank = bk[odd]
                    src = bank[:, :].rearrange("p (b h q) -> p b h q", b=2, h=4)
                    hi, lo = [AT[n].rearrange("p h (b o q) -> p b o h q", o=2, q=SQ)[:, 2 * j:2 * j + 2, odd, :, :]
                              for n in range(2)]
                    h = act(hi, src, ACTF.Copy, S("at_hi"), [m] + G.at_used)
                    l = tt(lo, src, hi, ALU.subtract, S("at_lo"), [h])
                    ring.release(i, h, l)
                    marks += [h, l]
                halves.append(marks)
            G.pt_used = G.v_used[uv] = [m]
            return halves

        def wo_proj(L, g, c, halves, co_ready, between):
            par = (g + L) % 2
            wo = WSET[par][2]
            for t in range(4):
                i, bank = ring.take()
                PE.wait(*halves[t // 2], *W_ready[(L, g, 2)])
                n = 0
                for h in range(4):
                    for x, y in ((0, 0), (0, 1), (1, 0)):
                        m = mm(bank[:, :], AT[x][:, h, t * 128:(t + 1) * 128], wo[y][:, h, :], n == 0, n == 11,
                               S("wo") if n == 11 else None)
                        n += 1
                xs = X[:, 4 * c + t, :]
                a = stt(xs, bank[:, :], CO[:, par * 8 + c:par * 8 + c + 1], xs, ALU.mult, ALU.add, S("x_add"),
                        [m, XM[4 * c + t]] + co_ready)
                ring.release(i, a)
                XM[4 * c + t] = a
                between(t)
            G.at_used = [m]
            G.w_used[par * 3 + 2] = [m]
            G.co_used[par] = [a]

        def attention(L, before_unit, in_wo, after_unit):
            units = [(g, c) for g in range(NKV) for c in range(NC)]
            nxt = {}

            def front(u, part, between=lambda: None):
                g, c = units[u]
                d = nxt.setdefault(u, {"marks": [], "rsq": None, "par": (g + L) % 2})
                if part == "kv":
                    unit_scales(L, g, c)
                    d["co"] = G.co_ready
                    d["k"], d["v"] = kv_proj(L, g, c, u % 2, d["co"], between)
                elif part == "kt":
                    d["marks"] += k_turn(d["k"])
                elif part == "qn":
                    if L:
                        d["rsq"] = q_norm(L, g)
                else:
                    q_proj(L, g, c, part, d["marks"])

            before_unit(0)
            for p in ("kv", 0, 1, "kt", 2, 3, "qn"):
                front(0, p)
                flush()
                flush_lo()
            for u, (g, c) in enumerate(units):
                d = nxt.pop(u)
                more = u + 1 < len(units)
                if more:
                    before_unit(u + 1)
                scores(d["marks"], d)
                soft_max(L, c, d)
                if more:
                    front(u + 1, "kv", lambda: soft_exp(d))
                else:
                    soft_exp(d)
                ps = soft_norm(d)
                if more:
                    front(u + 1, 0)
                    front(u + 1, 1)
                    flush()
                    flush_lo()
                    front(u + 1, 2)
                pt = p_turn(ps)
                if more:
                    front(u + 1, 3)
                halves = pv(u % 2, pt + d["v"])
                if more:
                    front(u + 1, "kt")
                    front(u + 1, "qn")
                flush()
                steps = in_wo(u)

                def between(t):
                    if t == 0:
                        flush_lo()
                    next(steps, None)
                wo_proj(L, g, c, halves, d["co"], between)
                for _ in steps:
                    pass
                after_unit(u)

        def load_masks0():
            st0, st1 = STG[:, 0:2048], STG[:, 2048:4096]
            i, st = stage()
            src = din["mask0"].rearrange("b q k -> q b k")
            for half in range(2):
                m = dma(st[64 * half:64 * half + 64, :].rearrange("p (b k) -> p b k", b=NB), src, S(f"stg{i}"))
            v = st.rearrange("p (b k) -> p b k", b=NB)
            a = ts(M01, v, 0.0, None, ALU.not_equal, None, S("mask"), [m])
            b = ts(MNO, v, 0.0, None, ALU.is_equal, None, S("mask"), [a])
            Stage.free[i] = [b]
            G.mask_ready = [b]

        ln_chunk(0)
        load_ctx(0)
        for k in range(3):
            prep_weight(0, 0, k)
        load_masks0()

        TB = WB[0]
        SCT, ZPT = TB[0:64, 0:2752], TB[0:4, 2752:5504]
        OHG, OHD = TB[0:64, 5504:6016], TB[0:64, 6016:7392]
        SCD, ZPD = TB[0:64, 7392:7904], TB[0:10, 7904:8416]
        GUW = [[AR[:, o + n * 1024:o + (n + 1) * 1024].bitcast(F16).rearrange("p (k f) -> p k f", k=4)
                for n in range(2)] for o in (0, 7680)]
        DW = [[AR[:, o + n * 512:o + (n + 1) * 512].bitcast(F16).rearrange("p (j f) -> p j f", j=2)
               for n in range(2)] for o in (2048, 9728)]
        HB = [[AR[:, 5632 + 1024 * i + 512 * n:5632 + 1024 * i + 512 * n + 512].bitcast(F16)
               .rearrange("p (j t) -> p j t", j=2) for n in range(2)] for i in range(2)]
        SG = [AR[:, 10752 + 512 * i:11264 + 512 * i] for i in range(2)]
        PGU, RGU, PD, RD, CH, CY, AMF = sm(1), sm(1), sm(1), sm(1), sm(1), sm(1), sm(2)

        class F:
            tabs, gu_ready, d_ready = [], {}, {}
            gu_used, d_used, h_used, sg_free = [[], []], [[], []], [[], []], [[], []]
            last = []

        def tables_scales(kind):
            name, n, w, dst, p, r = (("scales_gu", 4, 2752, SCT, PGU, RGU), ("scales_d", 10, 512, SCD, PD, RD))[kind]
            SP.wait(*Stage.free[0], *Stage.free[1])
            sf = STG[0:n, 0:w]
            m = dma(sf, din[name], S(f"stg{kind}"))
            z = fill(AMF[:, kind:kind + 1], 0.0, S("tab"))
            a = red(AMF[0:n, kind:kind + 1], sf, ALU.max, S("tab"), [m, z], absv=True)
            b = norm_scale(p, r, AMF[:, kind:kind + 1], a, 16.0)
            z = fill(dst, 0.0, S("tab"), G.w_used[0] + G.w_used[1] + G.w_used[2])
            a = ts(sf, sf, r[0:n, :], None, ALU.mult, None, S("tab"), [b, z])
            h = ts(dst[0:n, :], sf, 1.0, None, ALU.mult, None, S("tab"), [a])
            l = tt(dst[32:32 + n, :], sf, dst[0:n, :], ALU.subtract, S("tab"), [h])
            Stage.free[0] = Stage.free[1] = [l]
            F.tabs.append(l)

        def tables_zeros(kind):
            name, n, w, dst = (("qzeros_gu", 4, 344, ZPT), ("qzeros_d", 10, 64, ZPD))[kind]
            SP.wait(*Stage.free[0], *Stage.free[1])
            qz = STG[0:n, 2752:2752 + w].bitcast(U32)
            uz = STG[0:n, 0:8 * w].bitcast(U32)
            m = dma(qz, din[name], S(f"stg{kind}"))
            for e in range(8):
                a = ts(uz.rearrange("p (c e) -> p e c", e=8)[:, e, :], qz, 4 * e, 15, ALU.logical_shift_right,
                       ALU.bitwise_and, S("tab"), [m])
            a = ts(dst, uz, 1.0, None, ALU.add, None, S("tab"), [a] + G.w_used[0] + G.w_used[1] + G.w_used[2])
            Stage.free[0] = Stage.free[1] = [a]
            F.tabs.append(a)

        def tables_groups(kind):
            name, n, w, dst, idx = (("gidx_gu", 4, 512, OHG, IDXG), ("gidx_d", 10, INTER, OHD, IDXD))[kind]
            SP.wait(*Stage.free[0], *Stage.free[1])
            gi, gf = STG[0:64, 0:w].bitcast(I32), STG[0:64, 2048:2048 + w]
            m = dma(gi, din[name].unsqueeze(0).to_broadcast([64, w]), S(f"stg{kind}"))
            a = ts(gf, gi, 0.0, float(n), ALU.is_lt, ALU.mult, S("tab"), [m])
            a = tt(gf, gf, gi, ALU.add, S("tab"), [a])
            a = ts(gf, gf, 0.0, float(n - 1), ALU.max, ALU.min, S("tab"), [a])
            a = ts(dst, gf, idx[0:64, :], None, ALU.is_equal, None, S("tab"),
                   [a, c_cst] + G.w_used[0] + G.w_used[1] + G.w_used[2])
            Stage.free[0] = Stage.free[1] = [a]
            F.tabs.append(a)

        def tables_factors():
            a = ts(CH, RGU, 1.0 / 32, None, ALU.mult, None, S("tab"), norm_scale.last)
            b = ts(CY, PGU, PGU, 32.0, ALU.mult, ALU.mult, S("tab"), [a])
            b = ts(CY, CY, PD, None, ALU.mult, None, S("tab"), [b])
            F.tabs.append(b)

        def unpack(q, w, n, zp, sc, hi, lo, free, marks):
            a = ts(q.bitcast(U32), q.bitcast(U32), SHC[0:w, :], 15, ALU.logical_shift_right, ALU.bitwise_and, S("uq"), marks)
            iz, bz = ring.take()
            PE.wait(*F.tabs)
            for o, l, r in zp:
                m = mm(bz[0:w, o:o + r.shape[1]], l, r, True, True, S("uq_z"))
            is_, bs = ring.take()
            for o, l, r in sc:
                m2 = mm(bs[0:w, o:o + r.shape[1]], l, r, True, True, S("uq_z"))
            a = tt(q, q.bitcast(U32), bz[0:w, 0:n], ALU.subtract, S("uq"), [a, m])
            ring.release(iz, a)
            a = tt(q, q, bs[0:w, 0:n], ALU.mult, S("uq"), [a, m2])
            ring.release(is_, a)
            h = act(hi, q, ACTF.Copy, S("uq_hi"), [a] + free)
            l = tt(lo, q, hi, ALU.subtract, S("uq_lo"), [h])
            return [h, l], m2

        def step_tiles(s):
            return [128, 128] if s < 5 else [96]

        class Dq:
            pass

        def dequant_load(s):
            n = sum(step_tiles(s))
            i, st = stage()
            q = st[:, 0:8 * n].rearrange("p (k f) -> p k f", k=4)
            for k in range(KT):
                for j in range(2):
                    m = dma(q[:, k, j * n:(j + 1) * n].bitcast(U32),
                            din["qw_gu"][16 * k:16 * k + 16, j * INTER + 256 * s:j * INTER + 256 * s + n]
                            .unsqueeze(1).to_broadcast([16, 8, n]), S(f"stg{i}"))
            Dq.gu = (i, q, m)

        def dequant_load_d(s):
            i, st = stage()
            q = st[:, 0:1024].rearrange("p (j f) -> p j f", j=2)
            for j, w in enumerate(step_tiles(s)):
                m = dma(q[0:w, j, :].bitcast(U32), din["qw_d"][32 * s + 16 * j:32 * s + 16 * j + w // 8, :]
                        .unsqueeze(1).to_broadcast([w // 8, 8, D]), S(f"stg{i}"))
            Dq.d = (i, q, m)

        def dequant(s, k):
            n = sum(step_tiles(s))
            i, q, m = Dq.gu
            cols = [slice(j * INTER + 256 * s, j * INTER + 256 * s + n) for j in range(2)]
            oh = OHG[:, k * 128:(k + 1) * 128]
            marks, last = unpack(q[:, k, :], 128, 2 * n,
                                 [(j * n, oh[0:4, :], ZPT[:, cols[j]]) for j in range(2)],
                                 [(j * n, oh, SCT[:, cols[j]]) for j in range(2)],
                                 GUW[s % 2][0][:, k, 0:2 * n], GUW[s % 2][1][:, k, 0:2 * n], F.gu_used[s % 2], [m, c_sh])
            F.gu_ready[s] = F.gu_ready.get(s, []) + marks
            if k == KT - 1:
                Stage.free[i] = marks

        def dequant_d(s, j):
            i, q, m = Dq.d
            w = step_tiles(s)[j]
            f0 = 256 * s + 128 * j
            marks, last = unpack(q[0:w, j, :], w, 512, [(0, OHD[0:10, f0:f0 + w], ZPD)], [(0, OHD[:, f0:f0 + w], SCD)],
                                 DW[s % 2][0][0:w, j, :], DW[s % 2][1][0:w, j, :], F.d_used[s % 2], [m, c_sh])
            F.d_ready[s] = F.d_ready.get(s, []) + marks
            if j == len(step_tiles(s)) - 1:
                Stage.free[i] = marks
            F.tab_used = [last]

        def ffn_up(s, c):
            n, hb = sum(step_tiles(s)), (4 * s + c) % 2
            hm = []
            for j, w in enumerate(step_tiles(s)):
                bk = []
                for half in range(2):
                    i, bank = ring.take()
                    PE.wait(*F.gu_ready[s], *XT_ready[c])
                    cols = slice(half * n + j * 128, half * n + j * 128 + w)
                    e = 0
                    for k in range(KT):
                        for x, y in ((0, 0), (0, 1), (1, 0)):
                            m = mm(bank[0:w, :], GUW[s % 2][x][:, k, cols], XT[y][:, k, c * TC:(c + 1) * TC],
                                   e == 0, e == 11, S("gu") if e == 11 else None)
                            e += 1
                    bk.append((i, bank, m))
                (ig, bg, mg), (iu, bu, mu) = bk
                sg = SG[j]
                a = act(sg[0:w, :], bg[0:w, :], ACTF.Silu, S("silu"), [mg] + F.sg_free[j] + F.tabs, scale=PGU[0:w, :])
                ring.release(ig, a)
                b = stt(sg[0:w, :], sg[0:w, :], CH[0:w, :], bu[0:w, :], ALU.mult, ALU.mult, S("hf"), [a, mu])
                ring.release(iu, b)
                h = act(HB[hb][0][0:w, j, :], sg[0:w, :], ACTF.Copy, S("h_hi"), [b] + F.h_used[hb])
                l = tt(HB[hb][1][0:w, j, :], sg[0:w, :], HB[hb][0][0:w, j, :], ALU.subtract, S("h_lo"), [h])
                F.sg_free[j] = [l]
                hm += [h, l]
            F.gu_used[s % 2] = [mu]
            if s == 4:
                F.gu0_used = [mu]
            XT_used[c] = [mu]
            return hm

        def ffn_down(s, c, hm):
            hb = (4 * s + c) % 2
            tiles = step_tiles(s)
            for t in range(4):
                i, bank = ring.take()
                PE.wait(*F.d_ready[s], *hm)
                e, last = 0, 3 * len(tiles) - 1
                for j, w in enumerate(tiles):
                    for x, y in ((0, 0), (0, 1), (1, 0)):
                        m = mm(bank[:, :], HB[hb][x][0:w, j, t * 128:(t + 1) * 128], DW[s % 2][y][0:w, j, :],
                               e == 0, e == last, S("y") if e == last else None)
                        e += 1
                xs = X[:, 4 * c + t, :]
                a = stt(xs, bank[:, :], CY[:, :], xs, ALU.mult, ALU.add, S("x_add"), [m, XM[4 * c + t]] + F.tabs)
                ring.release(i, a)
                XM[4 * c + t] = a
            F.h_used[hb] = F.d_used[s % 2] = [m]
            if s == 4:
                F.gu0_used = F.gu0_used + [m]
            F.last = [m, a]

        def ffn(after_chunk):
            prev = None
            for s in range(6):
                for c in range(NC):
                    if s < 5:
                        if c == 0:
                            dequant_load(s + 1)
                            dequant_load_d(s + 1)
                    hm = ffn_up(s, c)
                    if prev:
                        ffn_down(*prev)
                    if s < 5:
                        dequant(s + 1, c)
                        if c < len(step_tiles(s + 1)):
                            dequant_d(s + 1, c)
                    prev = (s, c, hm)
                    after_chunk(s, c)
            ffn_down(*prev)

        def before0(u):
            if 0 < u < NC:
                load_ctx(u)
                ln_chunk(u)

        def in_wo(L):
            def steps(u):
                g, c = divmod(u, NC)
                return prep_steps(L, g + 1, c) if g + 1 < NKV and c < 3 else iter(())
            return steps

        def after0(u):
            g, c = divmod(u, NC)
            if STAGES >= 2 and g == NKV - 1:
                if c == 0:
                    tables_scales(0)
                    tables_scales(1)
                    tables_factors()
                if c == 1:
                    tables_zeros(0)
                    tables_zeros(1)
                    ln_chunk(0)
                if c == 2:
                    tables_groups(0)
                    tables_groups(1)
                    dequant_load(0)
                    dequant_load_d(0)
                    ln_chunk(1)

        if STAGES >= 1:
            attention(0, before0, in_wo(0), after0)

        if STAGES >= 2:
            ends = G.qt_used + G.kt_used + G.v_used[0] + G.v_used[1] + G.pt_used + G.at_used + G.ss_free + \
                G.m1_free[0] + G.m1_free[1] + G.rt_free[0] + G.rt_free[1] + G.kf_free
            for i in range(2):
                F.gu_used[i] = F.d_used[i] = F.h_used[i] = F.sg_free[i] = ends
            for k in range(KT):
                dequant(0, k)
            for j in range(2):
                dequant_d(0, j)
            ln_chunk(2)
            ln_chunk(3)

            def after_ffn(s, c):
                if STAGES >= 3 and s == 4 and c == 3:
                    for k in range(3):
                        prep_weight(1, 0, k)
                if STAGES >= 3 and s == 5 and c >= 2:
                    ln_chunk(c - 2)

            ffn(after_ffn)
            if STAGES >= 3:
                for k in range(3):
                    G.w_used[k] = F.tab_used
                ln_chunk(2)
                ln_chunk(3)

        TW = WB[1][:, :].bitcast(F32)
        wpos = [0]

        def tw(rows, words):
            o = wpos[0]
            wpos[0] += words
            assert wpos[0] <= 5120
            return TW[0:rows, o:o + words]

        WQM = tw(128, 256).rearrange("p (k n) -> p k n", k=4)
        WU1 = tw(128, 512).rearrange("p (k n) -> p k n", k=4)
        AVT = tw(128, 512).rearrange("p (k n) -> p k n", k=4)
        WVD = tw(128, 128).rearrange("p (k n) -> p k n", k=4)
        WRT, AKT = tw(64, 48), tw(64, 128)
        WVU, AV3 = tw(32, 512), tw(128, 512)
        T1T, RKT = tw(32, 128), tw(48, 128)
        WU2, BU1, LREL, BU2, GWT, GBT = tw(128, 2), tw(128, 1), tw(128, 128), tw(128, 1), tw(128, 1), tw(128, 1)
        ALL1 = tw(128, 128)
        VAR, LGT, GATE = sm(16), sm(16), sm(16)
        TOT = sm(4)

        class R4:
            ready = []

        def tail_loads():
            used = G.w_used[3] + G.w_used[4] + G.w_used[5]
            for dst, src in (
                (WQM, din["wqm"].rearrange("(k p) n -> p k n", p=128)),
                (WU1, din["wu1"].rearrange("(k p) n -> p k n", p=128)),
                (AVT, din["avT"].rearrange("(k p) n -> p k n", p=128)),
                (WVD, din["wvd"].rearrange("(k p) n -> p k n", p=128)),
                (WRT, din["wrT"]), (AKT, din["akT"]), (WVU, din["wvu"]),
                (WU2[:, 0:1], din["wu2"]), (BU1, din["bu1"]),
                (LREL, din["log_rel"].to_broadcast([128, NSLOT])),
                (BU2, din["bu2"].to_broadcast([128, 1])),
                (GWT, din["gate_w1"].to_broadcast([128, 1])),
                (GBT, din["gate_bias"].to_broadcast([128, 1])),
            ):
                R4.ready = [dma(dst, src, S("tail_w"), used)]
            R4.ones = fill(ALL1, 1.0, S("tail_one"), used)

        def tail_setup():
            i, bank = ring.take()
            PE.wait(*R4.ready)
            m = mm(bank[0:48, 0:128], WRT, AKT, True, True, S("t_pe"))
            a = act(RKT, bank[0:48, 0:128], ACTF.Copy, S("t_act"), [m])
            ring.release(i, a)
            i, bank = ring.take()
            for k in range(KT):
                m = mm(bank[0:32, 0:128], WVD[:, k, :], AVT[:, k, :], k == 0, k == 3, S("t_pe") if k == 3 else None)
            b = act(T1T, bank[0:32, 0:128], ACTF.Copy, S("t_act"), [m])
            ring.release(i, b)
            i, bank = ring.take()
            m = mm(bank[:, :], T1T, WVU, True, True, S("t_pe"), [b])
            b = act(AV3, bank[:, :], ACTF.Copy, S("t_act"), [m])
            ring.release(i, b)
            R4.setup = [a, b]

        def AO(t):
            return CT[t // 8][:, :, :].rearrange("p k t -> p (k t)")[:, (t % 8) * 1024:(t % 8) * 1024 + 1024].bitcast(F32)

        tv = [0]

        def tv_view(words):
            o = tv[0]
            tv[0] += words
            assert tv[0] <= 11776
            return AR[:, o:o + words]

        QY, RQ, UG = [[tv_view(512) for _ in range(2)] for _ in range(3)]
        RS_, AS_, SE_, R2_ = [[tv_view(512).rearrange("p (t n) -> p t n", t=4) for _ in range(2)] for _ in range(4)]
        WT = [tv_view(512) for _ in range(2)]
        M8, MX4, SM4, RC4 = tv_view(32), tv_view(4), tv_view(4), tv_view(4)
        LNS2, LNM2 = tv_view(24), tv_view(8)

        def tail_front(c, used):
            r = ln_stats(c)
            i0, ht = stage()
            ht = ht.rearrange("p (k t) -> p k t", k=4)
            for t in range(4):
                b = LNB[:, t % 2, :]
                n = ts(b, X[:, 4 * c + t, :], LNM[:, 2 * t:2 * t + 1], LNR[:, t:t + 1], ALU.subtract, ALU.mult,
                       S("ln_x"), [r] + ln_free[t % 2])
                lns_free[0] = [n]
                v = DVE_bn(LNS2[:, 6 * t:6 * t + 6], b, [n] + used)
                xs = X[:, 4 * c + t, :]
                XM[4 * c + t] = tt(xs, xs, b, ALU.add, S("x_add2"), [n], q=POOL)
                i, bank = ring.take()
                for k in range(KT):
                    m = tp(bank[:, k * 128:(k + 1) * 128], b[:, k * 128:(k + 1) * 128], IDN, S("ln_t"), [n])
                ln_free[t % 2] = [m, v, XM[4 * c + t]]
                h = act(ht[:, :, t * 128:(t + 1) * 128], bank[:, :].rearrange("p (k t) -> p k t", k=4), ACTF.Copy,
                        S("t_act"), [m] + list(Stage.free[i0]))
                ring.release(i, h)
            for t in range(4):
                v = DVE_agg(LNM2[:, 2 * t:2 * t + 2], LNS2[:, 6 * t:6 * t + 6], [v])
            v = ts(VAR[:, 4 * c:4 * c + 4], LNM2[:, 1:8:2], 1.0, None, ALU.mult, None, S("t_dve"), [v])
            i, bq = ring.take()
            PE.wait(*R4.ready, h)
            for k in range(KT):
                m = mm(bq[0:64, :], WQM[:, k, :], ht[:, k, :], k == 0, k == 3, S("t_pe") if k == 3 else None)
            q = act(QY[c % 2][0:64, :], bq[0:64, :], ACTF.Copy, S("t_act"), [m] + used)
            ring.release(i, q)
            i, bu = ring.take()
            for k in range(KT):
                m = mm(bu[:, :], WU1[:, k, :], ht[:, k, :], k == 0, k == 3, S("t_pe") if k == 3 else None)
            Stage.free[i0] = [m]
            u = act(UG[c % 2], bu[:, :], ACTF.Gelu_apprx_tanh, S("t_act"), [m], bias=BU1)
            ring.release(i, u)
            i, br_ = ring.take()
            m = mm(br_[0:48, :], WRT, QY[c % 2][0:64, :], True, True, S("t_pe"), [q])
            q2 = act(RQ[c % 2][0:48, :], br_[0:48, :], ACTF.Copy, S("t_act"), [m])
            ring.release(i, q2)
            return q, u, q2, v

        def tail_back(c, q, u, q2):
            p = c % 2
            r_, a_, s_, r2_ = RS_[p], AS_[p], SE_[p], R2_[p]
            ir, b_r = ring.take()
            ia, b_a = ring.take()
            PE.wait(q, q2, *R4.setup)
            for t in range(4):
                tok = slice(t * 128, (t + 1) * 128)
                m1 = mm(b_r[:, tok], RQ[p][0:48, tok], RKT, True, True, S("t_pe"))
            for t in range(4):
                tok = slice(t * 128, (t + 1) * 128)
                m2 = mm(b_a[:, tok], QY[p][0:64, tok], AKT, True, True, S("t_pe"))
            il, b_l = ring.take()
            PE.wait(u)
            for t in range(4):
                m3 = mm(b_l[:, t:t + 1], UG[p][:, t * 128:(t + 1) * 128], WU2[:, 0:1], True, True, S("t_pe"))
            lg = ts(LGT[:, 4 * c:4 * c + 4], b_l[:, 0:4], BU2, None, ALU.add, None, S("t_dve"), [m3])
            ring.release(il, lg)
            lrel = LREL.unsqueeze(1).to_broadcast([128, 4, NSLOT])
            a = stt(r_, b_r[:, :].rearrange("p (t n) -> p t n", t=4), float(1.0 / np.sqrt(np.float32(RDIM))), lrel,
                    ALU.mult, ALU.add, S("t_dve"), [m1])
            ring.release(ir, a)
            b = stt(a_, b_a[:, :].rearrange("p (t n) -> p t n", t=4), 0.125, lrel, ALU.mult, ALU.add, S("t_dve"), [m2])
            ring.release(ia, b)
            for t in range(4):
                x = top8(M8[:, 8 * t:8 * t + 8], r_[:, t, :], [a])
            for t in range(4):
                x = strike(r2_[:, t, :], M8[:, 8 * t:8 * t + 8], r_[:, t, :], [x])
            x = tt(s_, r2_, r_, ALU.not_equal, S("t_dve"), [x])
            y = ts(r2_, s_, 1.0, BIG, ALU.subtract, ALU.mult, S("t_dve"), [x])
            x = tt(a_, a_, s_, ALU.mult, S("t_dve"), [b, x])
            x = tt(a_, a_, r2_, ALU.add, S("t_dve"), [x, y])
            x = red(MX4, a_, ALU.max, S("t_dve"), [x])
            x = tt(a_, a_, MX4.unsqueeze(2).to_broadcast([128, 4, NSLOT]), ALU.subtract, S("t_dve"), [x])
            x = act(a_, a_, ACTF.Exp, S("t_act"), [x])
            x = red(SM4, a_, ALU.add, S("t_dve"), [x])
            x = recip(RC4, SM4, S("t_dve"), [x])
            x = tt(a_, a_, RC4.unsqueeze(2).to_broadcast([128, 4, NSLOT]), ALU.mult, S("t_dve"), [x])
            i, bank = ring.take()
            for t in range(4):
                m = tp(bank[:, t * 128:(t + 1) * 128], a_[:, t, :], IDN, S("t_pe"), [x])
            w = act(WT[p], bank[:, :], ACTF.Copy, S("t_act"), [m])
            ring.release(i, w)
            for t in range(4):
                i, bank = ring.take()
                m = mm(bank[:, :], WT[p][:, t * 128:(t + 1) * 128], AV3, True, True, S("t_pe"), [w])
                h = act(AO(4 * c + t), bank[:, :], ACTF.Copy, S("t_act"), [m] + R4.ct_used)
                ring.release(i, h)
                R4.ao.append(h)
            return m

        def top8(o, i, w):
            DVE.wait(*w)
            return DVE.put(lambda e: e.max(o, i), S("t_dve"))

        def strike(o, v, i, w):
            DVE.wait(*w)
            return DVE.put(lambda e: e.match_replace(o, v, i, -3e38), S("t_dve"))

        def gates(v):
            x = act(GATE, VAR[:, :], ACTF.Ln, S("t_act"), v, bias=1.0, accum_out=TOT[:, 0:1])
            i, bank = ring.take()
            m = mm(bank[:, 0:1], ALL1, TOT[:, 0:1], True, True, S("t_pe"), [x, R4.ones])
            y = ts(TOT[:, 1:2], bank[:, 0:1], 1.0 / T, 1e-6, ALU.mult, ALU.add, S("t_dve"), [m])
            ring.release(i, y)
            y = recip(TOT[:, 2:3], TOT[:, 1:2], S("t_dve"), [y])
            y = ts(GATE, GATE, TOT[:, 2:3], 0.5, ALU.mult, ALU.mult, S("t_dve"), [y, x])
            z = act(VAR, LGT, ACTF.Sigmoid, S("t_act"), [x] + R4.lg)
            y = stt(GATE, VAR, 2.5, GATE, ALU.mult, ALU.add, S("t_dve"), [y, z])
            y = ts(GATE, GATE, 0.0, 5.0, ALU.max, ALU.min, S("t_dve"), [y])
            y = ts(GATE, GATE, 0.5, 1.0 / 1.5, ALU.subtract, ALU.mult, S("t_dve"), [y])
            y = ts(GATE, GATE, 0.0, 1.0, ALU.max, ALU.min, S("t_dve"), [y])
            z = act(VAR, GATE, ACTF.Sigmoid, S("t_act"), [y], scale=GWT, bias=GBT)
            return stt(GATE, VAR, 0.05, VAR, ALU.is_ge, ALU.mult, S("t_dve"), [z])

        def setup_l1():
            i, st = stage()
            m = dma(st[:, 0:128], din["qnw"].to_broadcast([128, 128]), S(f"stg{i}"))
            m = dma(st[:, 128:256], din["knw"].to_broadcast([128, 128]), S(f"stg{i}"))
            for half in range(2):
                mk = dma(MASK1[64 * half:64 * half + 64, :], din["mask1"], S("mask1"), G.kf_free)
            w = st[:, 256:384]
            a = tt(w, st[:, 0:128], st[:, 128:256], ALU.mult, S("l1"), [m])
            a = red(AMX[:, 0:1], w, ALU.max, S("amx"), [a] + list(am_free[0]), absv=True)
            b = norm_scale(PWN[:, 0:1], PWN[:, 1:2], AMX[:, 0:1], a)
            am_free[0] = [b]
            a = ts(WQK, w, PWN[:, 1:2], None, ALU.mult, None, S("l1"), [b] + G.kf_free)
            a = ts(PWN[:, 2:3], PWN[:, 0:1], ISQ, None, ALU.mult, None, S("l1"), [a])
            Stage.free[i] = [a]
            G.wqk = [a, mk]

        if STAGES >= 3:
            setup_l1()
            G.qt_used = G.kt_used = G.v_used[0] = F.gu0_used
            G.rt_free[0] = G.rt_free[1] = G.ss_free = G.sq_used = G.pt_used = G.at_used = F.last

            def after1(u):
                g, c = divmod(u, NC)
                if STAGES >= 4 and g == NKV - 1 and c == 0:
                    tail_loads()

            attention(1, lambda u: None, in_wo(1), after1)

        ov = out.rearrange("(t p) d -> p t d", p=128)
        if STAGES >= 4:
            used = G.qt_used + G.kt_used + G.v_used[0] + G.v_used[1] + G.pt_used + G.at_used + G.ss_free + \
                G.m1_free[0] + G.m1_free[1] + G.sq_used + G.kf_free
            R4.ct_used, R4.ao = G.w_used[1], []
            tail_setup()
            R4.lg = []
            vs = []
            prev = None
            for c in range(NC):
                q, u, q2, v = tail_front(c, used)
                vs.append(v)
                if prev:
                    tail_back(*prev)
                prev = (c, q, u, q2)
            tail_back(*prev)
            R4.lg = [(S("t_dve"), S("t_dve").count)]
            gm = gates([vs[-1]])
            for t in range(16):
                xs = X[:, t, :]
                XM[t] = stt(xs, AO(t), GATE[:, t:t + 1], xs, ALU.mult, ALU.add, S("fin"), [gm, R4.ao[t], XM[t]])

        for t in range(16):
            dma(ov[:, t, :], X[:, t, :], S("out"), [XM[t]])
        SP.wait((S("out"), S("out").count))

        block = ctx.enter_context(nc.Block())
        block.sync(SP.run)
        block.tensor(PE.run)
        block.scalar(ACT.run)
        block.vector(DVE.run)
        block.gpsimd(POOL.run)


def _constants():
    f = np.float32
    inv = f(1.0) / np.power(f(10000.0), np.arange(0, DH, 2, dtype=f) / f(DH)).astype(f)
    ang = np.arange(SQ, dtype=f)[:, None] * inv[None, :]
    cos = np.concatenate([np.cos(ang), np.cos(ang)], axis=-1).astype(f)
    sin = np.concatenate([-np.sin(ang), np.sin(ang)], axis=-1).astype(f)
    c = np.zeros((128, 516), f)
    c[:, 0:128] = np.eye(128)
    c[:, 128:192] = cos.T
    c[:, 192:256] = sin.T
    c[:, 256:384] = np.concatenate([cos, cos], axis=0)
    c[:, 384:512] = np.concatenate([sin, sin], axis=0)
    p = np.arange(128)
    c[:, 512] = np.where((p % 32 < 4) & (p < 64), p % 32, -1)
    c[:, 513] = np.where((p % 32 < 10) & (p < 64), p % 32, -1)
    c[:, 514] = 1.0
    return c, (4 * (p % 8)).astype(np.uint32).reshape(128, 1)


def kernel(**inputs):
    import concourse.bacc as bacc
    from concourse.bass_utils import run_bass_kernel_spmd

    a = {k: np.asarray(v) for k, v in inputs.items()}
    cf, cu = _constants()
    arrays = {
        "const_f": cf,
        "const_u": cu,
        "x": a["x"].reshape(T, D),
        "ctxT": a["ctx_4096"].reshape(T, D).T,
        "mask0": a["mask_BxSxS2_ff1"],
        "mask1": a["mask_1x1xSxS2_ff0"].reshape(SQ, SQ),
        "scales_gu": a["L0_ffn_scales_gu"], "scales_d": a["L0_ffn_scales_down"],
        "qzeros_gu": a["L0_ffn_qzeros_gu"], "qzeros_d": a["L0_ffn_qzeros_down"],
        "qw_gu": a["L0_ffn_qweight_gu"], "qw_d": a["L0_ffn_qweight_down"],
        "gidx_gu": a["L0_ffn_g_idx_gu"], "gidx_d": a["L0_ffn_g_idx_down"],
        "wq0": a["L0_xattn_wq"], "wk0": a["L0_xattn_wk"], "wv0": a["L0_xattn_wv"], "wo0": a["L0_xattn_wo"],
        "wq1": a["L1_xattn_q_proj_w"].T, "wk1": a["L1_xattn_k_proj_w"].T, "wv1": a["L1_xattn_v_proj_w"].T,
        "wo1": a["L1_xattn_o_proj_w"].T, "qnw": a["L1_xattn_q_norm_w"].reshape(1, 128),
        "knw": a["L1_xattn_k_norm_w"].reshape(1, 128),
        "wqm": a["L1_ffn_Wq"].T, "wu1": a["L1_ffn_Wu1"].T, "avT": a["L1_ffn_aux_values"].T,
        "wvd": a["L1_ffn_Wvd"].T, "wrT": a["L1_ffn_Wr"].T, "akT": a["L1_ffn_aux_keys"].T,
        "wvu": a["L1_ffn_Wvu"].T, "wu2": a["L1_ffn_Wu2"].T, "bu1": a["L1_ffn_bu1"].reshape(128, 1),
        "log_rel": a["L1_ffn_log_rel"].reshape(1, NSLOT), "bu2": a["L1_ffn_bu2"].reshape(1, 1),
        "gate_w1": a["L1_ffn_gate_w1"].reshape(1, 1), "gate_bias": a["L1_ffn_gate_bias"].reshape(1, 1),
    }
    arrays = {k: np.ascontiguousarray(v) for k, v in arrays.items()}
    nc = bacc.Bacc("TRN2", target_bir_lowering=False, num_devices=1)
    din = {k: nc.dram_tensor("in_" + k, v.shape, mybir.dt.from_np(v.dtype), kind="ExternalInput").ap()
           for k, v in arrays.items()}
    out = nc.dram_tensor("out_x", (T, D), F32, kind="ExternalOutput").ap()
    build(nc, din, out)
    r = run_bass_kernel_spmd(nc, [{"in_" + k: v for k, v in arrays.items()}], core_ids=[0])
    return r.results[0]["out_x"].reshape(NB, SQ, D)
```

```python
from contextlib import ExitStack

import numpy as np

import concourse.bass as bass
from concourse import mybir

F32 = mybir.dt.float32
F16 = mybir.dt.float16
BF16 = mybir.dt.bfloat16
U32 = mybir.dt.uint32
I32 = mybir.dt.int32
U8 = mybir.dt.uint8
ALU = mybir.AluOpType
ACTF = mybir.ActivationFunctionType
AX = mybir.AxisListType.X
RMAX = bass.bass_isa.ReduceOp.max

NB, SQ, D = 32, 64, 512
T = NB * SQ
NH, NKV, DH = 32, 8, 128
KT = D // 128
TC = 512
NC = T // TC
BC = TC // SQ
INTER = 1376
FT = 11
NSLOT, BOT, RDIM, VB = 128, 64, 48, 32
LN_EPS = 1e-5
ISQ = float(1.0 / np.sqrt(np.float32(DH)))
BIG = 1e30
STAGES = 4


class Sem:

    def __init__(self, handle):
        self.handle, self.count = handle, 0


class Queue:

    def __init__(self):
        self.ops, self.seen = [], {}

    def wait(self, *marks):
        for sem, n in marks:
            if self.seen.get(id(sem), 0) < n:
                self.seen[id(sem)] = n
                self.ops.append((None, sem.handle, n))

    def put(self, fn, sem=None, n=1):
        self.ops.append((fn, sem.handle if sem else None, n))
        if sem:
            sem.count += n
            return (sem, sem.count)
        return None

    def run(self, eng):
        for fn, handle, n in self.ops:
            if fn is None:
                eng.wait_ge(handle, n)
            elif handle is None:
                fn(eng)
            else:
                fn(eng).then_inc(handle, n)


def build(nc, din, out):
    ctx = ExitStack()
    with ctx:
        def sb(name, shape, dt):
            return ctx.enter_context(nc.sbuf_tensor(name, shape, dt))

        sems = {}

        def S(name):
            if name not in sems:
                sems[name] = Sem(ctx.enter_context(nc.semaphore("s_" + name)))
            return sems[name]

        PE, ACT, DVE, POOL, SP = Queue(), Queue(), Queue(), Queue(), Queue()

        def mm(o, l, r, start, stop, sem=None, w=()):
            PE.wait(*w)
            return PE.put(lambda e: e.matmul(o, l, r, start=start, stop=stop), sem)

        def tp(o, i, ident, sem=None, w=()):
            PE.wait(*w)
            return PE.put(lambda e: e.transpose(o, i, ident), sem)

        def act(o, i, f, sem=None, w=(), **kw):
            ACT.wait(*w)
            return ACT.put(lambda e: e.activation(o, i, f, **kw), sem)

        def tt(o, a, b, op, sem=None, w=(), q=None):
            q = q or DVE
            q.wait(*w)
            return q.put(lambda e: e.tensor_tensor(o, a, b, op), sem)

        def ts(o, a, s1, s2, op0, op1, sem=None, w=(), q=None):
            q = q or DVE
            q.wait(*w)
            if op1 is None:
                return q.put(lambda e: e.tensor_scalar(o, a, s1, None, op0), sem)
            return q.put(lambda e: e.tensor_scalar(o, a, s1, s2, op0, op1), sem)

        def stt(o, a, s, b, op0, op1, sem=None, w=()):
            DVE.wait(*w)
            return DVE.put(lambda e: e.scalar_tensor_tensor(o, a, s, b, op0, op1), sem)

        def red(o, i, op, sem=None, w=(), absv=False):
            DVE.wait(*w)
            if absv:
                return DVE.put(lambda e: e.tensor_reduce(o, i, AX, op, apply_absolute_value=True), sem)
            return DVE.put(lambda e: e.tensor_reduce(o, i, AX, op), sem)

        def recip(o, i, sem=None, w=()):
            DVE.wait(*w)
            return DVE.put(lambda e: e.reciprocal(o, i), sem)

        def fill(o, v, sem=None, w=(), q=None):
            q = q or DVE
            q.wait(*w)
            return q.put(lambda e: e.memset(o, v), sem)

        def dma(o, i, sem, w=(), q=None):
            q = q or SP
            q.wait(*w)
            return q.put(lambda e: e.dma_start(o, i), sem, 16)

        def allmax(o, i, sem, w=()):
            POOL.wait(*w)
            return POOL.put(lambda e: e.partition_all_reduce(o, i, 128, RMAX), sem)

        X = sb("X", [128, T // 128, D], F32)
        CTB = sb("CTB", [128, 4096 * NC], F16)
        XTB = sb("XTB", [128, 4096 * NC], F16)
        WB = [sb(f"WB{i}", [128, 10240], F16) for i in range(2)]
        STG = sb("STG", [128, 4096], F32)
        AR = sb("AR", [128, 11776], F32)
        LNB = sb("LNB", [128, 2, D], F32)
        CST = sb("CST", [128, 260], F32)
        SHC = sb("SHC", [128, 1], U32)
        SML = sb("SML", [128, 256], F32)
        ONEB = sb("ONEB", [128, 2], BF16)
        PB = [ctx.enter_context(nc.psum_tensor(f"PB{i}", [128, 512], F32)) for i in range(8)]

        def parts(buf):
            return [[buf[:, (2 * c + n) * 2048:(2 * c + n + 1) * 2048].rearrange("p (k t) -> p k t", k=KT)
                     for c in range(NC)] for n in range(2)]

        CT, XT = parts(CTB), parts(XTB)

        IDN = CST[:, 0:128]
        COST, SINT = CST[:, 128:192], CST[:, 192:256]
        IDXG, IDXD = CST[:, 256:257], CST[:, 257:258]

        small = [0]

        def sm(n):
            a = small[0]
            small[0] += n
            assert small[0] <= 256
            return SML[:, a:a + n]

        arena = [0]

        def view(words, dt, **dims):
            a = arena[0]
            arena[0] += words
            assert arena[0] <= 11776, arena[0]
            v = AR[:, a:a + words]
            return v if dt == F32 else v.bitcast(dt)

        def wset(i):
            w = WB[i]
            q = [w[:, n * 2048:(n + 1) * 2048].rearrange("p (k n) -> p k n", k=4) for n in range(2)]
            kv = [w[:, 4096 + n * 1024:4096 + (n + 1) * 1024].rearrange("p (k n) -> p k n", k=4) for n in range(2)]
            o = [w[:, 6144 + n * 2048:6144 + (n + 1) * 2048].rearrange("p (k n) -> p k n", k=4) for n in range(2)]
            return q, kv, o

        WSET = [wset(0), wset(1)]

        bank_free = [()] * 8

        class Ring:

            def __init__(self, banks):
                self.banks, self.n = banks, 0

            def take(self):
                i = self.banks[self.n % len(self.banks)]
                self.n += 1
                PE.wait(*bank_free[i])
                bank_free[i] = None
                return i, PB[i]

            def release(self, i, *marks):
                bank_free[i] = marks

        ring = Ring(list(range(8)))

        c_cst = dma(CST[:, :], din["const_f"], S("cst"))
        c_sh = dma(SHC[:, :], din["const_u"], S("cst2"))
        XM = [None] * 16
        xv = din["x"].rearrange("(t p) d -> p t d", p=128)

        def load_x(c):
            m = dma(X[:, 4 * c:4 * c + 4, :], xv[:, 4 * c:4 * c + 4, :], S(f"x{c}"))
            for t in range(4):
                XM[4 * c + t] = m

        c_one = fill(ONEB[:, :], 1.0, S("one"))

        NRM = sm(8)
        nrm_free = [[], []]

        def norm_all(n, am, mark):
            return allmax(NRM[:, 4 * n:4 * n + 1], am, S("ns_all"), [mark] + nrm_free[n])

        def norm_scale(n, p, r, mark, mul=1.0):
            m = NRM[:, 4 * n:4 * n + 4]
            a = ts(m[:, 1:2], m[:, 0:1], 2.0 ** -100, 2.0 ** 100, ALU.max, ALU.min, S("ns"), [mark])
            a = ts(m[:, 2:3].bitcast(U32), m[:, 1:2].bitcast(U32), 0x7F800000, None, ALU.bitwise_and, None, S("ns"), [a])
            a = ts(p, m[:, 2:3], mul, None, ALU.mult, None, S("ns"), [a])
            b = recip(r, p, S("ns"), [a])
            nrm_free[n] = norm_scale.last = [b]
            return b

        norm_scale.last = []

        class Stage:
            free = [()] * 8
            n = 0
            area = [STG[:, 0:2048], STG[:, 2048:4096]] + \
                [b[:, 4096 * c:4096 * c + 4096].bitcast(F32) for c in (2, 3) for b in (XTB, CTB)] + \
                [AR[:, 3072:5120], AR[:, 8704:10752]]

        def stage(i=None):
            if i is None:
                i = Stage.n % 2
                Stage.n += 1
            SP.wait(*Stage.free[i])
            return i, Stage.area[i]

        def finish(steps):
            for _ in steps:
                pass

        def chain(*gens):
            for g in gens:
                yield from g

        CTP, CTR, AMX = sm(4), sm(4), sm(2)
        CT_ready = [None] * NC
        CT_used = [[] for _ in range(NC)]
        CT_scaled = [None] * NC
        am_free = [(), ()]

        def ctx_steps(c, q=None):
            i, st = stage()
            m = dma(st.rearrange("p (k t) -> p k t", k=4),
                    din["ctxT"].rearrange("(k p) t -> p k t", p=128)[:, :, c * TC:(c + 1) * TC], S(f"stg{i}"))
            yield
            a = red(AMX[:, 1:2], st, ALU.max, S("amx"), [m] + list(am_free[1]), absv=True)
            a = norm_all(1, AMX[:, 1:2], a)
            yield
            b = norm_scale(1, CTP[:, c:c + 1], CTR[:, c:c + 1], a)
            am_free[1] = [b]
            CT_scaled[c] = b
            hi, lo = [[CT[n][c][:, k, :] for k in range(KT)] for n in range(2)]
            src = [st[:, k * TC:(k + 1) * TC] for k in range(KT)]
            h = [act(hi[k], src[k], ACTF.Copy, S("ct_hi"), [b] + CT_used[c], scale=CTR[:, c:c + 1]) for k in range(KT)]
            if q is POOL:
                h = [act(src[k], src[k], ACTF.Copy, S("ct_hi"), [h[k]], scale=CTR[:, c:c + 1]) for k in range(KT)]
            for half in range(2):
                yield
                for k in (2 * half, 2 * half + 1):
                    if q is POOL:
                        l = tt(lo[k], src[k], hi[k], ALU.subtract, S("ct_lop"), [h[k]], q=POOL)
                    else:
                        l = stt(lo[k], src[k], CTR[:, c:c + 1], hi[k], ALU.mult, ALU.subtract, S("ct_lo"), [h[k], b])
            Stage.free[i] = CT_ready[c] = [h[-1], l]

        LNS, LNM, LNV, LNR, LNC = sm(24), sm(8), sm(4), sm(4), sm(4)
        ln_free = [[], []]
        XT_ready = [None] * NC
        XT_used = [[] for _ in range(NC)]
        c_half = fill(LNC[:, :], -0.5, S("one"))
        lns_free = [[]]

        def tile_stats(c, t):
            return DVE_bn(LNS[:, 6 * t:6 * t + 6], X[:, 4 * c + t, :], [XM[4 * c + t]] + lns_free[0])

        def ln_stats(c, todo=range(4)):
            for t in todo:
                a = tile_stats(c, t)
            a = (S("ln"), S("ln").count)
            for t in range(4):
                a = DVE_agg(LNM[:, 2 * t:2 * t + 2], LNS[:, 6 * t:6 * t + 6], [a])
            a = ts(LNV[:, :], LNM[:, 1:8:2], LN_EPS, None, ALU.add, None, S("ln"), [a])
            return tt(LNR[:, :], LNV[:, :], LNC[:, :], ALU.pow, S("ln_pow"), [a, c_half], q=POOL)

        def DVE_bn(o, i, w):
            DVE.wait(*w)
            return DVE.put(lambda e: e.bn_stats(o, i), S("ln"))

        def DVE_agg(o, i, w):
            DVE.wait(*w)
            return DVE.put(lambda e: e.bn_aggr(o, i), S("ln"))

        def ln_steps(c):
            r = ln_stats(c)
            yield
            late = []
            for half in range(2):
                tiles, ns = (2 * half, 2 * half + 1), []
                for t in tiles:
                    ns.append(ts(LNB[:, t % 2, :], X[:, 4 * c + t, :], LNM[:, 2 * t:2 * t + 1], LNR[:, t:t + 1],
                                 ALU.subtract, ALU.mult, S("ln_x"), [r] + ln_free[t % 2]))
                lns_free[0] = [ns[-1]]
                for f in late:
                    f()
                late = []
                yield
                for t, n in zip(tiles, ns):
                    i, bank = ring.take()
                    for k in range(KT):
                        m = tp(bank[:, k * 128:(k + 1) * 128], LNB[:, t % 2, k * 128:(k + 1) * 128], IDN, S("ln_t"),
                               [n, c_cst])
                    ln_free[t % 2] = [m]
                    src = bank[:, :].rearrange("p (k t) -> p k t", k=4)
                    hi, lo = [XT[n][c][:, :, t * 128:(t + 1) * 128] for n in range(2)]
                    h = act(hi, src, ACTF.Copy, S("xt_hi"), [m] + XT_used[c])

                    def low(i=i, src=src, hi=hi, lo=lo, h=h):
                        l = tt(lo, src, hi, ALU.subtract, S("xt_lo"), [h])
                        ring.release(i, l)
                        XT_ready[c] = [h, l]
                    late.append(low)
                yield
            for f in late:
                f()
            yield

        QT = [view(1024, F16) for _ in range(2)]
        KTT = [view(256, F16) for _ in range(2)]
        V = [[view(256, F16).rearrange("p (t d) -> p t d", t=4) for _ in range(2)] for _ in range(2)]
        KF, KR = view(512, F32), view(512, F32)
        M1 = [view(512, F32) for _ in range(2)]
        RT_all = view(1024, F32)
        RT = [RT_all[:, 0:512], RT_all[:, 512:1024]]
        SS = view(1024, F32).rearrange("p (a n) -> p a n", a=2)
        PT = [view(512, F16).rearrange("p (a b n) -> p a b n", a=2, b=4) for _ in range(2)]
        AT = [view(1024, F16).rearrange("p (h t) -> p h t", h=4) for _ in range(2)]
        MK = view(1024, F32)
        M01 = MK[:, 0:512].bitcast(U8).rearrange("p (b k) -> p b k", b=NB)
        MNO = MK[:, 512:1024].bitcast(U8).rearrange("p (b k) -> p b k", b=NB)
        SQH = MK.bitcast(BF16)
        SQL = RT_all.bitcast(BF16)
        MASK1, WQK = KR[:, 0:64], KR[:, 128:256]
        MXT, SMT, RCT, RSQ, KSS, RSK = sm(16), sm(16), sm(16), sm(16), sm(4), sm(4)
        HLF = sm(16)
        WSC = sm(24)
        CO = sm(16)
        c_hlf = fill(HLF, -0.5, S("one"))
        

        def rows_of(t, pair, b):
            return t[:, (pair * BC + b) * 128:(pair * BC + b + 1) * 128]

        def head_of(t, h):
            return t.rearrange("p (a b h q) -> p a b h q", a=2, b=BC, h=2)[:, h // 2, :, h % 2, :]

        def by_batch(t):
            return t.rearrange("p (b s) -> p b s", s=SQ)

        class G:
            w_used = [[], [], [], [], [], []]
            qt_used, kt_used, v_used = [], [], [[], []]
            kf_free, m1_free, rt_free = [], [[], []], [[], []]
            ss_free, pt_used, at_used = [], [], []
            sml_free, sq_used = [], []
            late, late_lo = [], []

        def flush():
            todo, G.late = G.late, []
            for f in todo:
                f()

        def flush_lo():
            todo, G.late_lo = G.late_lo, []
            for f in todo:
                f()

        W_ready, scaled = {}, set()

        def prep_steps(L, g, kind, place=None, q_lo=None):
            par = (g + L) % 2
            q, kv, o = WSET[par]
            i, st = stage(place)
            s4 = st.rearrange("p (k n) -> p k n", k=4)
            if kind == 0:
                m = dma(s4, din[f"wq{L}"].rearrange("(k p) n -> p k n", p=128)[:, :, g * 512:(g + 1) * 512], S(f"stg{i}"))
                n, dst = 512, q
            elif kind == 1:
                s4 = st[:, 0:1024].rearrange("p (k n) -> p k n", k=4)
                for j, nm in enumerate(("wk", "wv")):
                    m = dma(s4[:, :, j * 128:(j + 1) * 128],
                            din[f"{nm}{L}"].rearrange("(k p) n -> p k n", p=128)[:, :, g * 128:(g + 1) * 128],
                            S(f"stg{i}"))
                n, dst = 256, kv
            else:
                m = dma(s4, din[f"wo{L}"].rearrange("(h p) n -> p h n", p=128)[:, 4 * g:4 * g + 4, :], S(f"stg{i}"))
                n, dst = 512, o
            yield
            a = red(AMX[:, 0:1], st[:, 0:4 * n], ALU.max, S("amx"), [m] + list(am_free[0]), absv=True)
            a = norm_all(0, AMX[:, 0:1], a)
            yield
            col = par * 12 + kind * 4
            b = norm_scale(0, WSC[:, col:col + 1], WSC[:, col + 1:col + 2], a)
            am_free[0] = [b]
            r = WSC[:, col + 1:col + 2]
            scaled.add((L, g, kind))
            if kind < 2 and (L, g, 1 - kind) in scaled:
                p_q, p_kv = [WSC[:, par * 12 + 4 * k:par * 12 + 4 * k + 1] for k in range(2)]
                r_q, r_kv = [WSC[:, par * 12 + 4 * k + 1:par * 12 + 4 * k + 2] for k in range(2)]
                e_q, e_kv = WSC[:, par * 12 + 2:par * 12 + 3], WSC[:, par * 12 + 3:par * 12 + 4]
                if L == 0:
                    a = ts(e_q, p_q, p_kv, ISQ, ALU.mult, ALU.mult, S("co"), [b] + G.co_used[par])
                else:
                    a = ts(e_q, r_q, r_q, LN_EPS, ALU.mult, ALU.mult, S("co"), [b] + G.co_used[par])
                    a = ts(e_kv, r_kv, r_kv, LN_EPS, ALU.mult, ALU.mult, S("co"), [b])
                W_ready[(L, g, 3)] = [a]
            used = G.w_used[par * 3 + kind]
            hs = [act(dst[0][:, k, :], s4[:, k, :], ACTF.Copy, S("w_hi"), [b] + used, scale=r) for k in range(4)]
            if q_lo is POOL:
                hs = [act(s4[:, k, :], s4[:, k, :], ACTF.Copy, S("w_hi"), [hs[k]], scale=r) for k in range(4)]
            ls = []
            for half in range(2):
                yield
                ls += [tt(dst[1][:, k, :], s4[:, k, :], dst[0][:, k, :], ALU.subtract, S("w_lop"), [hs[k]], q=POOL)
                       if q_lo is POOL else
                       stt(dst[1][:, k, :], s4[:, k, :], r, dst[0][:, k, :], ALU.mult, ALU.subtract, S("w_lo"), [hs[k]])
                       for k in (2 * half, 2 * half + 1)]
            Stage.free[i] = [ls[-1]]
            W_ready[(L, g, kind)] = [hs[-1], ls[-1]]

        def unit_scales(L, g, c):
            par = (g + L) % 2
            co, w = CO[:, par * 8:par * 8 + 8], [CT_scaled[c]] + W_ready[(L, g, 3)] + G.co_used[par]
            p_kv = WSC[:, par * 12 + 4:par * 12 + 5]
            a = ts(co[:, c:c + 1], CTP[:, c:c + 1], p_kv, None, ALU.mult, None, S("co"), w)
            if L == 0:
                a = ts(co[:, 4 + c:5 + c], CTP[:, c:c + 1], WSC[:, par * 12 + 2:par * 12 + 3], None, ALU.mult, None, S("co"))
            else:
                a = ts(co[:, 4 + c:5 + c], CTR[:, c:c + 1], WSC[:, par * 12 + 3:par * 12 + 4], CTR[:, c:c + 1],
                       ALU.mult, ALU.mult, S("co"))
            G.co_ready = [a]

        G.co_used = [[], []]
        PWN = sm(4)

        def kv_rope(L, g, c, uv, co_ready, between):
            par = (g + L) % 2
            wkv = WSET[par][1]
            i, bank = ring.take()
            PE.wait(*W_ready[(L, g, 1)], *CT_ready[c])
            n = 0
            for k in range(KT):
                for a, b in ((0, 0), (0, 1), (1, 0)):
                    m = mm(bank[:, :], wkv[a][:, k, 0:128], CT[b][c][:, k, :], n == 0, n == 11,
                           S("kv") if n == 11 else None)
                    n += 1
            r1 = act(KR[0:64, :], bank[64:128, :], ACTF.Copy, S("k_rot"), [m] + G.kf_free)
            r2 = act(KR[64:128, :], bank[0:64, :], ACTF.Copy, S("k_rot"))
            k1 = tt(by_batch(KF), by_batch(bank[:, :]), COST.unsqueeze(1).to_broadcast([128, BC, SQ]), ALU.mult,
                    S("k_e"), [r2, c_cst] + G.kf_free)
            ring.release(i, r2, k1)
            k2 = tt(by_batch(KR), by_batch(KR), SINT.unsqueeze(1).to_broadcast([128, BC, SQ]), ALU.mult, S("k_sin"), [r2],
                    q=POOL)
            k = tt(KF, KF, KR, ALU.add, S("k_add"), [k1, k2], q=POOL)
            between()
            i, bank = ring.take()
            for t in range(4):
                n = 0
                for k_ in range(KT):
                    for a, b in ((0, 0), (0, 1), (1, 0)):
                        m = mm(bank[:, t * 128:(t + 1) * 128], CT[a][c][:, k_, t * 128:(t + 1) * 128],
                               wkv[b][:, k_, 128:256], n == 0, n == 11, S("kv") if n == 11 else None)
                        n += 1
            src = bank[:, :].rearrange("p (t n) -> p t n", t=4)
            h = act(V[uv][0], src, ACTF.Copy, S("v_hi"), [m] + G.v_used[uv])
            l = tt(V[uv][1], src, V[uv][0], ALU.subtract, S("v_lo"), [h])
            ring.release(i, h, l)
            G.w_used[par * 3 + 1] = CT_used[c] = [m]
            return k, [h, l]

        def k_parts(k):
            h = act(KTT[0], KF, ACTF.Copy, S("kt_hi"), [k] + G.kt_used)
            l = tt(KTT[1], KF, KTT[0], ALU.subtract, S("kt_lo"), [h], q=POOL)
            G.kf_free = [h, l]
            return [h, l]

        def kv_norm(L, g, c, uv, co_ready, between):
            par = (g + L) % 2
            wkv = WSET[par][1]
            ready = W_ready[(L, g, 1)] + CT_ready[c]
            vd, vmarks = V[uv], []
            KF3 = KF.rearrange("p (t d) -> p t d", t=4)
            for half in range(2):
                i, bank = ring.take()
                PE.wait(*ready)
                for t2 in range(2):
                    tok = slice((2 * half + t2) * 128, (2 * half + t2 + 1) * 128)
                    o = bank[:, t2 * 256:(t2 + 1) * 256]
                    n = 0
                    for k in range(KT):
                        for a, b in ((0, 0), (0, 1), (1, 0)):
                            m = mm(o, CT[a][c][:, k, tok], wkv[b][:, k, :], n == 0, n == 11,
                                   S("kv") if n == 11 else None)
                            n += 1
                src = bank[:, :].rearrange("p (t n) -> p t n", t=2)
                tsl = slice(2 * half, 2 * half + 2)
                h = act(vd[0][:, tsl, :], src[:, :, 128:256], ACTF.Copy, S("v_hi"), [m] + G.v_used[uv])
                for t2 in range(2):
                    t = 2 * half + t2
                    k1 = act(M1[0][:, 0:128], src[:, t2, 0:128], ACTF.Square, S("k_sq"),
                             [m] + G.m1_free[0] + G.kss_used, accum_out=KSS[:, t:t + 1])
                    G.m1_free[0] = [k1]
                k2 = tt(KF3[:, tsl, :], src[:, :, 0:128], WQK.unsqueeze(1).to_broadcast([128, 2, 128]), ALU.mult,
                        S("k_e"), [k1] + G.kf_free + G.wqk)
                l = tt(vd[1][:, tsl, :], src[:, :, 128:256], vd[0][:, tsl, :], ALU.subtract, S("v_lo"), [h])
                ring.release(i, h, l, k1, k2)
                vmarks = [h, l]
                if half == 0:
                    between()
            G.w_used[par * 3 + 1] = CT_used[c] = [m]
            a = ts(KSS[:, :], KSS[:, :], 1.0 / DH, CO[:, par * 8 + 4 + c:par * 8 + 5 + c], ALU.mult, ALU.add,
                   S("k_ms"), [k1] + co_ready)
            a = tt(RSK[:, :], KSS[:, :], HLF[:, 0:4], ALU.pow, S("k_pow"), [a, c_hlf] + G.kss_used, q=POOL)
            k = tt(KF3, KF3, RSK[:, :].unsqueeze(2).to_broadcast([128, 4, 128]), ALU.mult,
                   S("k_add"), [a, k2], q=POOL)
            G.kss_used = [k]
            return k, vmarks

        G.kss_used, G.wqk = [], []

        def k_turn(k):
            i, bank = ring.take()
            for t in range(4):
                m = tp(bank[:, t * 128:(t + 1) * 128], KF[:, t * 128:(t + 1) * 128], IDN, S("k_t"), [k])
            G.kf_free = [m]
            h = act(KTT[0], bank[:, :], ACTF.Copy, S("kt_hi"), [m] + G.kt_used)
            l = tt(KTT[1], bank[:, :], KTT[0], ALU.subtract, S("kt_lo"), [h])
            ring.release(i, h, l)
            return [h, l]

        def q_proj(L, g, c, h, marks):
            par = (g + L) % 2
            wq = WSET[par][0]
            i, bank = ring.take()
            PE.wait(*W_ready[(L, g, 0)], *XT_ready[c])
            n = 0
            for k in range(KT):
                for a, b in ((0, 0), (0, 1), (1, 0)):
                    m = mm(bank[:, :], wq[a][:, k, h * 128:(h + 1) * 128], XT[b][c][:, k, :],
                           n == 0, n == 11, S("q") if n == 11 else None)
                    n += 1
            if h == 3:
                G.w_used[par * 3] = [m]
                XT_used[c] = [m]
            m1, rt = M1[h % 2], RT[h % 2]
            v3 = bank[:, :].rearrange("p (b s) -> p b s", s=SQ)
            if L == 0:
                r1 = act(rt[0:64, :], bank[64:128, :], ACTF.Copy, S("q_rot"), [m] + G.rt_free[h % 2])
                r2 = act(rt[64:128, :], bank[0:64, :], ACTF.Copy, S("q_rot"))
                c1 = tt(m1.rearrange("p (b s) -> p b s", s=SQ), v3, COST.unsqueeze(1).to_broadcast([128, BC, SQ]),
                        ALU.mult, S("q_cos"), [r2, c_cst] + G.m1_free[h % 2])
                ring.release(i, r2, c1)
                r3v = rt.rearrange("p (b s) -> p b s", s=SQ)
                r3 = tt(r3v, r3v, SINT.unsqueeze(1).to_broadcast([128, BC, SQ]), ALU.mult, S("q_sin"), [r2], q=POOL)

                def finish():
                    a = tt(m1, m1, rt, ALU.add, S("q_add"), [c1, r3], q=POOL if h > 1 else DVE)
                    G.rt_free[h % 2] = [a]
                    hi = act(head_of(QT[0], h), by_batch(m1), ACTF.Copy, S("qt_hi"), [a] + G.qt_used)

                    def finish_lo():
                        lo = tt(head_of(QT[1], h), by_batch(m1), head_of(QT[0], h), ALU.subtract, S("qt_lop" if h > 1 else "qt_lo"), [hi],
                                q=POOL if h > 1 else DVE)
                        G.m1_free[h % 2] = [lo]
                        marks.extend([hi, lo])
                    G.late_lo.append(finish_lo)
                G.late.append(finish)
            else:
                hi = act(head_of(QT[0], h), v3, ACTF.Copy, S("qt_hi"), [m] + G.qt_used)
                s1 = act(m1, bank[:, :], ACTF.Square, S("q_sq"), G.m1_free[h % 2])
                s2 = act(head_of(SQH, h), v3, ACTF.Square, S("q_sq"), G.sq_used)
                lo = tt(head_of(QT[1], h), v3, head_of(QT[0], h), ALU.subtract, S("qt_lo"), [s2])
                ring.release(i, s2, lo)
                s3 = tt(head_of(SQL, h), by_batch(m1), head_of(SQH, h), ALU.subtract, S("q_sql"), [s1, s2] + G.sq_used, q=POOL)
                G.m1_free[h % 2] = [s3]
                marks.extend([hi, lo])
                G.sq_ready = [s2, s3]

        def q_norm(L, g):
            par = (g + L) % 2
            i, bank = ring.take()
            PE.wait(*G.sq_ready, c_one)
            for pair in range(2):
                for b in range(BC):
                    o = bank[:, pair * BC + b:pair * BC + b + 1]
                    for n, s in enumerate((SQH, SQL)):
                        m = mm(o, rows_of(s, pair, b), ONEB[:, 0:1], n == 0, n == 1,
                               S("q_ss") if n else None)
            G.sq_used = [m]
            a = ts(RSQ[:, :], bank[:, 0:16], 1.0 / DH, WSC[:, par * 12 + 2:par * 12 + 3], ALU.mult, ALU.add,
                   S("q_ms"), [m] + G.rsq_used + W_ready[(L, g, 3)])
            ring.release(i, a)
            return tt(RSQ[:, :], RSQ[:, :], HLF, ALU.pow, S("q_pow"), [a, c_hlf], q=POOL)

        G.rsq_used = []

        def scores(ready, d):
            banks = []
            for pair in range(2):
                i, bank = ring.take()
                PE.wait(*ready)
                for b in range(BC):
                    o = bank[:, b * SQ:(b + 1) * SQ]
                    for n, (x, y) in enumerate(((0, 0), (0, 1), (1, 0))):
                        m = mm(o, rows_of(QT[x], pair, b), KTT[y][:, b * SQ:(b + 1) * SQ],
                               n == 0, n == 2, S("s") if n == 2 else None)
                banks.append((i, bank, m))
            G.qt_used = G.kt_used = [m]
            d["s"] = banks

        def soft_max(L, c, d):
            par, banks, rsq = d["par"], d["s"], d["rsq"]
            co = CO[:, par * 8:par * 8 + 8]
            bsl = slice(c * BC, (c + 1) * BC)
            v = [by_batch(SS[:, pair, :]) for pair in range(2)]
            mx = [MXT[:, pair * BC:(pair + 1) * BC] for pair in range(2)]
            a = [None, None]
            for pair, (i, bank, m) in enumerate(banks):
                b3 = by_batch(bank[:, :])
                if L == 0:
                    a[pair] = stt(v[pair], b3, co[:, 4 + c:5 + c], M01[:, bsl, :], ALU.mult, ALU.mult, S("sm"),
                                  [m] + G.ss_free + d["co"] + G.mask_ready)
                else:
                    a[pair] = tt(v[pair], b3, RSQ[:, pair * BC:(pair + 1) * BC].unsqueeze(2).to_broadcast([128, BC, SQ]),
                                 ALU.mult, S("sm"), [m, rsq] + G.ss_free)
                ring.release(i, a[pair])
            G.rsq_used = [a[1]]
            for pair in range(2):
                if L == 0:
                    a[pair] = stt(v[pair], MNO[:, bsl, :], -1e9, v[pair], ALU.mult, ALU.add, S("sm"), [a[pair]])
                else:
                    a[pair] = stt(v[pair], v[pair], PWN[:, 2:3], MASK1.unsqueeze(1).to_broadcast([128, BC, SQ]), ALU.mult,
                                  ALU.add, S("sm"), [a[pair]] + G.wqk)
            for pair in range(2):
                d["mx"] = a[pair] = red(mx[pair], v[pair], ALU.max, S("sm"), [a[pair]])

        def soft_exp(d):
            d["e"] = []
            for pair in range(2):
                s, mx = SS[:, pair, :], MXT[:, pair * BC:(pair + 1) * BC]
                a = tt(by_batch(s), by_batch(s), mx.unsqueeze(2).to_broadcast([128, BC, SQ]), ALU.subtract, S("sm"),
                       [d["mx"]])
                d["e"].append(act(s, s, ACTF.Exp, S("exp"), [a]))

        def soft_norm(d):
            cols = [slice(pair * BC, (pair + 1) * BC) for pair in range(2)]
            v = [by_batch(SS[:, pair, :]) for pair in range(2)]
            a = [red(SMT[:, cols[p]], v[p], ALU.add, S("sm"), [d["e"][p]]) for p in range(2)]
            a = [recip(RCT[:, cols[p]], SMT[:, cols[p]], S("sm"), [a[p]] + G.sml_free) for p in range(2)]
            ps = [tt(v[p], v[p], RCT[:, cols[p]].unsqueeze(2).to_broadcast([128, BC, SQ]), ALU.mult, S("p_n"),
                     [a[p]], q=POOL) for p in range(2)]
            G.sml_free = [ps[-1]]
            return ps

        def p_turn(ps):
            marks = []
            for pair in range(2):
                i, bank = ring.take()
                for b2 in range(4):
                    m = tp(bank[:, b2 * 128:(b2 + 1) * 128], SS[:, pair, b2 * 128:(b2 + 1) * 128], IDN, S("p_t"),
                           [ps[pair]])
                src = bank[:, :].rearrange("p (b n) -> p b n", b=4)
                h = act(PT[0][:, pair, :, :], src, ACTF.Copy, S("pt_hi"), [m] + G.pt_used)
                l = tt(PT[1][:, pair, :, :], src, PT[0][:, pair, :, :], ALU.subtract, S("pt_lo"), [h])
                ring.release(i, h, l)
                marks += [h, l]
            G.ss_free = [m]
            return marks

        def pv(uv, ready):
            vd = V[uv]
            halves = []
            for j in range(2):
                marks = []
                bk = [ring.take(), ring.take()]
                PE.wait(*ready)
                for jj in range(2):
                    b2 = 2 * j + jj
                    for n, (x, y) in enumerate(((0, 0), (0, 1), (1, 0))):
                        for odd in range(2):
                            rows = slice(64 * odd, 64 * odd + 64)
                            m = mm(bk[odd][1][:, jj * 256:(jj + 1) * 256], vd[x][rows, b2, :], PT[y][rows, :, b2, :],
                                   n == 0, n == 2, S("pv") if n == 2 else None)
                for odd in range(2):
                    i, bank = bk[odd]
                    src = bank[:, :].rearrange("p (b h q) -> p b h q", b=2, h=4)
                    hi, lo = [AT[n].rearrange("p h (b o q) -> p b o h q", o=2, q=SQ)[:, 2 * j:2 * j + 2, odd, :, :]
                              for n in range(2)]
                    h = act(hi, src, ACTF.Copy, S("at_hi"), [m] + G.at_used)
                    l = tt(lo, src, hi, ALU.subtract, S("at_lo"), [h])
                    ring.release(i, h, l)
                    marks += [h, l]
                halves.append(marks)
            G.pt_used = G.v_used[uv] = [m]
            return halves

        def wo_proj(L, g, c, halves, co_ready, between):
            par = (g + L) % 2
            wo = WSET[par][2]
            cs = CO[:, par * 8 + c:par * 8 + c + 1]
            cm = ts(cs, cs, WSC[:, par * 12 + 8:par * 12 + 9], None, ALU.mult, None, S("co"),
                    co_ready + W_ready[(L, g, 2)])
            for t in range(4):
                i, bank = ring.take()
                PE.wait(*halves[t // 2], *W_ready[(L, g, 2)])
                n = 0
                for h in range(4):
                    for x, y in ((0, 0), (0, 1), (1, 0)):
                        m = mm(bank[:, :], AT[x][:, h, t * 128:(t + 1) * 128], wo[y][:, h, :], n == 0, n == 11,
                               S("wo") if n == 11 else None)
                        n += 1
                xs = X[:, 4 * c + t, :]
                a = stt(xs, bank[:, :], cs, xs, ALU.mult, ALU.add, S("x_add"), [m, XM[4 * c + t], cm])
                ring.release(i, a)
                XM[4 * c + t] = a
                between(t)
            G.at_used = [m]
            G.w_used[par * 3 + 2] = [m]
            G.co_used[par] = [a]

        def attention(L, units, during, early=lambda u: False, after_last=lambda t: None, in_first=lambda: None):
            nxt = {}

            def front(u, part, between=lambda: None):
                g, c = units[u]
                d = nxt.setdefault(u, {"marks": [], "rsq": None, "par": (g + L) % 2})
                if part == (0 if L == 0 else "kv"):
                    unit_scales(L, g, c)
                    d["co"] = G.co_ready
                if part == "kv":
                    d["k"], d["v"] = (kv_norm if L else kv_rope)(L, g, c, u % 2, d.get("co"), between)
                elif part == "kt":
                    d["marks"] += k_turn(d["k"]) if L else k_parts(d["k"])
                elif part == "qn":
                    if L:
                        d["rsq"] = q_norm(L, g)
                else:
                    q_proj(L, g, c, part, d["marks"])

            front(0, "kv", in_first)
            yield
            for parts in ((0,), (1, "kt"), (2,), (3, "qn")):
                for p in parts:
                    front(0, p)
                yield
                if parts[0] in (1, 3):
                    flush()
                    yield
                    flush_lo()
                    yield
            waiting = None
            for u, (g, c) in enumerate(units):
                d = nxt.pop(u)
                more = u + 1 < len(units)
                scores(d["marks"], d)
                soft_max(L, c, d)
                if u == 0:
                    yield
                if more:
                    front(u + 1, "kv", lambda: soft_exp(d))
                else:
                    soft_exp(d)
                ps = soft_norm(d)
                steps = during(u)
                q_steps = steps if early(u) else iter(())
                if more:
                    for h in range(4):
                        if h == 2:
                            flush()
                            flush_lo()
                        front(u + 1, h)
                        next(q_steps, None)
                else:
                    wo_proj(L, *waiting, lambda t: next(steps, None))
                    waiting = None
                pt = p_turn(ps)
                if not more:
                    next(steps, None)

                def between(t):
                    if t == 0:
                        flush()
                    if t == 1:
                        flush_lo()
                    if t == 2 and more:
                        front(u + 1, "kt")
                    next(steps, None)
                if waiting:
                    wo_proj(L, *waiting, between)
                elif more:
                    for t in range(4):
                        between(t)
                if more:
                    next(steps, None)
                    front(u + 1, "qn")
                waiting = (g, c, pv(u % 2, pt + d["v"]), d["co"])
                finish(steps)
            wo_proj(L, *waiting, after_last)

        def mask_steps(place):
            i, st = stage(place)
            src = din["mask0"].rearrange("b q k -> q b k")
            for half in range(2):
                m = dma(st[64 * half:64 * half + 64, :].rearrange("p (b k) -> p b k", b=NB), src, S(f"stg{i}"))
            yield
            v = st.rearrange("p (b k) -> p b k", b=NB)
            a = ts(M01, v, 0.0, None, ALU.not_equal, None, S("mask"), [m])
            b = ts(MNO, v, 0.0, None, ALU.is_equal, None, S("mask"), [a])
            Stage.free[i] = [b]
            G.mask_ready = [b]

        TB = WB[0]
        SCT, ZPT = TB[0:64, 0:2752], TB[0:4, 2752:5504]
        OHG, OHD = TB[0:64, 5504:6016], TB[0:64, 6016:7392]
        SCD, ZPD = TB[0:64, 7392:7904], TB[0:10, 7904:8416]
        GUW = [[AR[:, o + n * 1024:o + (n + 1) * 1024].bitcast(F16).rearrange("p (k f) -> p k f", k=4)
                for n in range(2)] for o in (0, 7680)] + [WSET[1][0]]
        DW = [[AR[:, o + n * 512:o + (n + 1) * 512].bitcast(F16).rearrange("p (j f) -> p j f", j=2)
               for n in range(2)] for o in (2048, 9728)] + \
            [[WB[1][:, 4096 + n * 1024:5120 + n * 1024].rearrange("p (j f) -> p j f", j=2) for n in range(2)]]
        HB = [[AR[:, 5632 + 1024 * i + 512 * n:5632 + 1024 * i + 512 * n + 512].bitcast(F16)
               .rearrange("p (j t) -> p j t", j=2) for n in range(2)] for i in range(2)]
        SG = [AR[:, 10752 + 512 * i:11264 + 512 * i] for i in range(2)]
        PGU, RGU, PD, RD, CH, CY, AMF = sm(1), sm(1), sm(1), sm(1), sm(1), sm(1), sm(2)

        class F:
            tabs, gu_ready, d_ready = [], {}, {}
            gu_used, d_used, h_used, sg_free = [[], [], []], [[], [], []], [[], []], [[], []]
            last = []

        def tables_scales(kind):
            name, n, w, dst, p, r = (("scales_gu", 4, 2752, SCT, PGU, RGU), ("scales_d", 10, 512, SCD, PD, RD))[kind]
            SP.wait(*Stage.free[0], *Stage.free[1])
            sf = STG[0:n, 0:w]
            m = dma(sf, din[name], S(f"stg{kind}"))
            z = fill(AMF[:, kind:kind + 1], 0.0, S("tab"))
            f = fill(dst, 0.0, S("tab_z"), tab_used[kind](), q=POOL)
            yield
            a = red(AMF[0:n, kind:kind + 1], sf, ALU.max, S("tab"), [m, z], absv=True)
            a = norm_all(0, AMF[:, kind:kind + 1], a)
            yield
            b = norm_scale(0, p, r, a, 16.0)
            h = act(dst[0:n, :], sf, ACTF.Copy, S("tab_hi"), [b, f], scale=r[0:n, :])
            yield
            l = stt(dst[32:32 + n, :], sf, r[0:n, :], dst[0:n, :], ALU.mult, ALU.subtract, S("tab"), [h])
            Stage.free[0] = Stage.free[1] = [l]
            F.tabs.append(l)
            yield

        def tables_zeros(kind):
            name, n, w, dst = (("qzeros_gu", 4, 344, ZPT), ("qzeros_d", 10, 64, ZPD))[kind]
            SP.wait(*Stage.free[0], *Stage.free[1])
            qz = STG[0:n, 2752:2752 + w].bitcast(U32)
            uz = STG[0:n, 0:8 * w].bitcast(U32)
            m = dma(qz, din[name], S(f"stg{kind}"))
            yield
            for e in range(8):
                a = ts(uz.rearrange("p (c e) -> p e c", e=8)[:, e, :], qz, 4 * e, 15, ALU.logical_shift_right,
                       ALU.bitwise_and, S("tab"), [m])
            yield
            a = ts(dst, uz, 1.0, None, ALU.add, None, S("tab"), [a] + tab_used[kind]())
            Stage.free[0] = Stage.free[1] = [a]
            F.tabs.append(a)
            yield

        def tables_groups(kind):
            name, n, w, dst, idx = (("gidx_gu", 4, 512, OHG, IDXG), ("gidx_d", 10, INTER, OHD, IDXD))[kind]
            SP.wait(*Stage.free[0], *Stage.free[1])
            gi, gf = STG[0:64, 0:w].bitcast(I32), STG[0:64, 2048:2048 + w]
            m = dma(gi, din[name].unsqueeze(0).to_broadcast([64, w]), S(f"stg{kind}"))
            yield
            a = ts(gf, gi, 0.0, float(n), ALU.is_lt, ALU.mult, S("tab"), [m])
            a = tt(gf, gf, gi, ALU.add, S("tab"), [a])
            yield
            a = ts(gf, gf, 0.0, float(n - 1), ALU.max, ALU.min, S("tab"), [a])
            a = ts(dst, gf, idx[0:64, :], None, ALU.is_equal, None, S("tab"), [a, c_cst] + tab_used[kind]())
            Stage.free[0] = Stage.free[1] = [a]
            F.tabs.append(a)
            yield

        def tables_factors():
            a = ts(CH, RGU, 1.0 / 32, None, ALU.mult, None, S("tab"), norm_scale.last)
            b = ts(CY, PGU, PGU, 32.0, ALU.mult, ALU.mult, S("tab"), [a])
            b = ts(CY, CY, PD, None, ALU.mult, None, S("tab"), [b])
            F.tabs.append(b)
            yield

        tab_used = [lambda: G.w_used[0] + G.w_used[1], lambda: G.w_used[0] + G.w_used[1] + G.w_used[2]]

        def unpack(q, w, n, zp, sc, hi, lo, free, marks):
            a = ts(q.bitcast(U32), q.bitcast(U32), SHC[0:w, :], 15, ALU.logical_shift_right, ALU.bitwise_and, S("uq"), marks)
            iz, bz = ring.take()
            PE.wait(*F.tabs)
            for o, l, r in zp:
                m = mm(bz[0:w, o:o + r.shape[1]], l, r, True, True, S("uq_z"))
            is_, bs = ring.take()
            for o, l, r in sc:
                m2 = mm(bs[0:w, o:o + r.shape[1]], l, r, True, True, S("uq_z"))
            a = tt(q, q.bitcast(U32), bz[0:w, 0:n], ALU.subtract, S("uq"), [a, m])
            ring.release(iz, a)
            a = tt(q, q, bs[0:w, 0:n], ALU.mult, S("uq"), [a, m2])
            ring.release(is_, a)
            h = act(hi, q, ACTF.Copy, S("uq_hi"), [a] + free)
            l = tt(lo, q, hi, ALU.subtract, S("uq_lo"), [h], q=POOL)
            return [h, l], m2

        def place(s):
            return s % 2 if s else 2

        def step_tiles(s):
            return [128, 128] if s < 5 else [96]

        class Dq:
            pass

        def dequant_load(s):
            n = sum(step_tiles(s))
            i, st = stage()
            q = st[:, 0:8 * n].rearrange("p (k f) -> p k f", k=4)
            for k in range(KT):
                for j in range(2):
                    m = dma(q[:, k, j * n:(j + 1) * n].bitcast(U32),
                            din["qw_gu"][16 * k:16 * k + 16, j * INTER + 256 * s:j * INTER + 256 * s + n]
                            .unsqueeze(1).to_broadcast([16, 8, n]), S(f"stg{i}"))
            Dq.gu = (i, q, m)

        def dequant_load_d(s):
            i, st = stage()
            q = st[:, 0:1024].rearrange("p (j f) -> p j f", j=2)
            for j, w in enumerate(step_tiles(s)):
                m = dma(q[0:w, j, :].bitcast(U32), din["qw_d"][32 * s + 16 * j:32 * s + 16 * j + w // 8, :]
                        .unsqueeze(1).to_broadcast([w // 8, 8, D]), S(f"stg{i}"))
            Dq.d = (i, q, m)

        def dequant(s, k):
            n = sum(step_tiles(s))
            i, q, m = Dq.gu
            cols = [slice(j * INTER + 256 * s, j * INTER + 256 * s + n) for j in range(2)]
            oh = OHG[:, k * 128:(k + 1) * 128]
            marks, last = unpack(q[:, k, :], 128, 2 * n,
                                 [(j * n, oh[0:4, :], ZPT[:, cols[j]]) for j in range(2)],
                                 [(j * n, oh, SCT[:, cols[j]]) for j in range(2)],
                                 GUW[place(s)][0][:, k, 0:2 * n], GUW[place(s)][1][:, k, 0:2 * n], F.gu_used[place(s)], [m, c_sh])
            F.gu_ready[s] = F.gu_ready.get(s, []) + marks
            if k == KT - 1:
                Stage.free[i] = marks

        def dequant_d(s, j):
            i, q, m = Dq.d
            w = step_tiles(s)[j]
            f0 = 256 * s + 128 * j
            marks, last = unpack(q[0:w, j, :], w, 512, [(0, OHD[0:10, f0:f0 + w], ZPD)], [(0, OHD[:, f0:f0 + w], SCD)],
                                 DW[place(s)][0][0:w, j, :], DW[place(s)][1][0:w, j, :], F.d_used[place(s)], [m, c_sh])
            F.d_ready[s] = F.d_ready.get(s, []) + marks
            if j == len(step_tiles(s)) - 1:
                Stage.free[i] = marks
            F.tab_used = [last]

        def ffn_up(s, c):
            n, hb = sum(step_tiles(s)), (4 * s + c) % 2
            hm = []
            for j, w in enumerate(step_tiles(s)):
                bk = []
                for half in range(2):
                    i, bank = ring.take()
                    PE.wait(*F.gu_ready[s], *XT_ready[c])
                    cols = slice(half * n + j * 128, half * n + j * 128 + w)
                    e = 0
                    for k in range(KT):
                        for x, y in ((0, 0), (0, 1), (1, 0)):
                            m = mm(bank[0:w, :], GUW[place(s)][x][:, k, cols], XT[y][c][:, k, :],
                                   e == 0, e == 11, S("gu") if e == 11 else None)
                            e += 1
                    bk.append((i, bank, m))
                (ig, bg, mg), (iu, bu, mu) = bk
                sg = SG[j]
                a = act(sg[0:w, :], bg[0:w, :], ACTF.Silu, S("silu"), [mg] + F.sg_free[j] + F.tabs, scale=PGU[0:w, :])
                ring.release(ig, a)
                b = stt(sg[0:w, :], sg[0:w, :], CH[0:w, :], bu[0:w, :], ALU.mult, ALU.mult, S("hf"), [a, mu])
                ring.release(iu, b)
                h = act(HB[hb][0][0:w, j, :], sg[0:w, :], ACTF.Copy, S("h_hi"), [b] + F.h_used[hb])
                l = tt(HB[hb][1][0:w, j, :], sg[0:w, :], HB[hb][0][0:w, j, :], ALU.subtract, S("h_lo"), [h], q=POOL)
                F.sg_free[j] = [l]
                hm += [h, l]
            F.gu_used[place(s)] = [mu]
            if s == 4:
                F.gu0_used = [mu]
            XT_used[c] = [mu]
            return hm

        def ffn_down(s, c, hm):
            hb = (4 * s + c) % 2
            tiles = step_tiles(s)
            for t in range(4):
                i, bank = ring.take()
                PE.wait(*F.d_ready[s], *hm)
                e, last = 0, 3 * len(tiles) - 1
                for j, w in enumerate(tiles):
                    for x, y in ((0, 0), (0, 1), (1, 0)):
                        m = mm(bank[:, :], HB[hb][x][0:w, j, t * 128:(t + 1) * 128], DW[place(s)][y][0:w, j, :],
                               e == 0, e == last, S("y") if e == last else None)
                        e += 1
                xs = X[:, 4 * c + t, :]
                a = stt(xs, bank[:, :], CY[:, :], xs, ALU.mult, ALU.add, S("x_add"), [m, XM[4 * c + t]] + F.tabs)
                ring.release(i, a)
                XM[4 * c + t] = a
            F.h_used[hb] = F.d_used[place(s)] = [m]
            if s == 4:
                F.gu0_used = F.gu0_used + [m]
            F.last = [m, a]

        def ffn(during):
            prev = None
            for s in range(6):
                for c in range(NC):
                    steps = during(s, c)
                    if s < 5 and c == 0:
                        dequant_load(s + 1)
                        dequant_load_d(s + 1)
                    next(steps, None)
                    hm = ffn_up(s, c)
                    next(steps, None)
                    if (s, c) == (5, 3):
                        yield
                    if prev:
                        ffn_down(*prev)
                    next(steps, None)
                    if s < 5:
                        if c < 2:
                            dequant(s + 1, 2 * c)
                            dequant(s + 1, 2 * c + 1)
                        elif c == 2:
                            for j in range(len(step_tiles(s + 1))):
                                dequant_d(s + 1, j)
                    prev = (s, c, hm)
                    finish(steps)
            ffn_down(*prev)

        def setup_l1():
            i, st = stage()
            m = dma(st[:, 0:128], din["qnw"].to_broadcast([128, 128]), S(f"stg{i}"))
            m = dma(st[:, 128:256], din["knw"].to_broadcast([128, 128]), S(f"stg{i}"))
            for half in range(2):
                mk = dma(MASK1[64 * half:64 * half + 64, :], din["mask1"], S("mask1"), G.kf_free)
            w = st[:, 256:384]
            a = tt(w, st[:, 0:128], st[:, 128:256], ALU.mult, S("l1"), [m])
            a = red(AMX[:, 0:1], w, ALU.max, S("amx"), [a] + list(am_free[0]), absv=True)
            a = norm_all(0, AMX[:, 0:1], a)
            b = norm_scale(0, PWN[:, 0:1], PWN[:, 1:2], a)
            am_free[0] = [b]
            a = ts(WQK, w, PWN[:, 1:2], None, ALU.mult, None, S("l1"), [b] + G.kf_free)
            a = ts(PWN[:, 2:3], PWN[:, 0:1], ISQ, None, ALU.mult, None, S("l1"), [a])
            Stage.free[i] = [a]
            G.wqk = [a, mk]

        def some(steps, n):
            for _ in range(n):
                next(steps, None)
                yield

        def call(f, *a):
            f(*a)
            yield

        def in_turn(*gens):
            gens = list(gens)
            while gens:
                for g in list(gens):
                    try:
                        next(g)
                    except StopIteration:
                        gens.remove(g)
                        continue
                    yield

        def after_output(steps):
            return chain(some(steps, 2), empty(2), steps)

        def apart(steps):
            return chain(some(steps, 2), empty(2), some(steps, 2), empty(1), steps)

        def half_norm(steps, first):
            return chain(some(steps, 2), empty(1), some(steps, 2)) if first else steps

        def empty(n=4):
            for _ in range(n):
                yield

        units0 = [(g, c) for c in range(NC) for g in range(2)] + [(g, c) for g in range(2, NKV) for c in range(NC)]
        wq0, wkv0, wo0 = [prep_steps(0, 0, k, pl, q) for k, pl, q in ((0, 2, None), (1, None, None), (2, 4, POOL))]
        wq1, wkv1, wo1 = [prep_steps(0, 1, k, pl) for k, pl in ((0, 7), (1, 5), (2, None))]
        wq2, wkv2, wo2 = [prep_steps(0, 2, k) for k in range(3)]

        def start0():
            ctx0, ln0, mask = ctx_steps(0), ln_steps(0), mask_steps(3)
            next(ctx0)
            next(wkv0)
            load_x(0)
            for steps in (wq0, wkv1, wq1, mask, wo0):
                next(steps, None)
            for c in range(1, NC):
                load_x(c)
            for steps in (ctx0, wkv0, ctx0, wkv0, ctx0):
                next(steps, None)
            finish(ctx0)
            finish(wkv0)

            def in_first():
                for steps in (ln0, wq0, ln0, wq0, ln0, wq0):
                    next(steps, None)
                finish(wq0)
                finish(ln0)

            first = attention(0, units0, during0, lambda u: u < 5 or u == 6 or u >= 28, after_last0, in_first)
            for steps in (ln0, wq0, first, wkv1, first, wkv1, first, wkv1, first, wkv1, first, mask, first, first, first, first,
                          wq1, first, wq1):
                next(steps, None)
            finish(wkv1)
            finish(mask)
            finish(wq1)
            G.at_used = Stage.free[7]
            finish(first)

        def during0(u):
            g, c = units0[u]
            if u < 8:
                if 1 <= u <= 4:
                    used, i = ((CT_used, 3), (XT_used, 2), (CT_used, 5), (XT_used, 4))[u - 1]
                    used[2 + (u > 2)] = list(Stage.free[i])
                return (lambda: chain(ctx_steps(1), ln_steps(1), wo0), lambda: in_turn(wo1, ctx_steps(2)),
                        lambda: apart(ln_steps(2)), lambda: ctx_steps(3), lambda: apart(ln_steps(3)), lambda: iter(()),
                        lambda: chain(wkv2, wq2), lambda: after_output(wo2))[u]()
            if g + 1 < NKV and c < 3:
                return prep_steps(0, g + 1, c)
            if STAGES >= 2:
                if u == 27:
                    return tables_scales(0)
                if u == 28:
                    return chain(tables_zeros(0), tables_groups(0))
                if u == 29:
                    return chain(tables_scales(1), tables_factors(), tables_groups(1), tables_zeros(1),
                                 call(dequant_load, 0), call(dequant_load_d, 0))
                if u == 30:
                    return chain(some(ln0, 2), empty(2), ln0, *[call(dequant0, k) for k in range(KT)])
                if u == 31:
                    return chain(empty(5), some(ln1, 2))
            return iter(())

        def dequant0(k):
            if k == 0:
                F.gu_used[2], F.d_used[2] = G.w_used[3], G.w_used[4]
            dequant(0, k)

        down0 = [call(dequant_d, 0, j) for j in range(2)]
        ln0, ln1, ln2, ln3 = [ln_steps(c) for c in range(NC)]

        def after_last0(t):
            if STAGES >= 2:
                for steps in ((ln1, down0[0]), (ln1, down0[1]), (ln1,), (ln1, ln2))[t]:
                    next(steps, None)

        units1 = [(g, c) for c in range(NC) for g in range(2)] + [(g, c) for g in range(2, NKV - 2) for c in range(NC)] + \
            [(g, c) for c in range(NC) for g in (NKV - 2, NKV - 1)]
        wq_b, wkv_b, wo_b = [prep_steps(1, 1, k, None, POOL) for k in range(3)]
        wq_c, wkv_c, wo_c = [prep_steps(1, 2, k) for k in range(3)]
        ln_b = [ln_steps(c) for c in range(NC)]

        def during_ffn(s, c):
            if s == 0 and c < 2:
                return (chain(ln2, some(ln3, 1)), ln3)[c]
            if STAGES >= 3:
                if s in (1, 2, 3) and c == 0:
                    for k in range(3):
                        G.w_used[3 + k] = F.gu_used[2] + F.d_used[2]
                    return prep_steps(1, 0, s - 1, 6, POOL)
                if s == 4 and c == 3:
                    for k in range(3):
                        G.w_used[k] = F.tab_used
                    return chain(call(setup_l1), some(wkv_b, 2))
                if s == 5:
                    if c == 0:
                        return chain(wkv_b, some(wq_b, 2))
                    if c == 1:
                        return chain(wq_b, some(ln_b[0], 1))
                    if c == 2:
                        return chain(some(ln_b[0], 1), empty(1), some(ln_b[0], 2))
                    return chain(empty(1), ln_b[0], some(ln_b[1], 2))
            return iter(())

        wpos = [0]

        def tw(rows, words):
            o = wpos[0]
            wpos[0] += words
            assert wpos[0] <= 4096
            return STG[0:rows, o:o + words]

        WQM = tw(128, 256).rearrange("p (k n) -> p k n", k=4)
        WU1 = tw(128, 512).rearrange("p (k n) -> p k n", k=4)
        AVT = tw(128, 512).rearrange("p (k n) -> p k n", k=4)
        WVD = tw(128, 128).rearrange("p (k n) -> p k n", k=4)
        WRT, AKT = tw(64, 48), tw(64, 128)
        WVU, AV3 = tw(32, 512), tw(128, 512)
        T1T, RKT = tw(32, 128), tw(48, 128)
        WU2, BU1, LREL, BU2, GWT, GBT = tw(128, 2), tw(128, 1), tw(128, 128), tw(128, 1), tw(128, 1), tw(128, 1)
        ALL1 = tw(128, 128)
        M8, MX4, SM4, RC4 = tw(128, 32), tw(128, 4), tw(128, 4), tw(128, 4)
        LNS2, LNM2 = tw(128, 24), tw(128, 8)
        VAR, LGT, GATE = sm(16), sm(16), sm(16)
        TOT = sm(4)

        def tail_place(c):
            x, k = [b[:, c * 4096:(c + 1) * 4096].bitcast(F32) for b in (XTB, CTB)]
            return [x] + [k[:, n * 512:(n + 1) * 512] for n in range(4)] + [x[:, n * 512:(n + 1) * 512] for n in range(4)]

        class R4:
            ready = []
            q, u, rq, w = [None] * NC, [None] * NC, [None] * NC, [None] * NC

        def tail_loads():
            SP.wait(*Stage.free[0], *Stage.free[1])
            for dst, src in (
                (WQM, din["wqm"].rearrange("(k p) n -> p k n", p=128)),
                (WU1, din["wu1"].rearrange("(k p) n -> p k n", p=128)),
                (AVT, din["avT"].rearrange("(k p) n -> p k n", p=128)),
                (WVD, din["wvd"].rearrange("(k p) n -> p k n", p=128)),
                (WRT, din["wrT"]), (AKT, din["akT"]), (WVU, din["wvu"]),
                (WU2[:, 0:1], din["wu2"]), (BU1, din["bu1"]),
                (LREL, din["log_rel"].to_broadcast([128, NSLOT])),
                (BU2, din["bu2"].to_broadcast([128, 1])),
                (GWT, din["gate_w1"].to_broadcast([128, 1])),
                (GBT, din["gate_bias"].to_broadcast([128, 1])),
            ):
                R4.ready = [dma(dst, src, S("tail_w"))]
            R4.ones = fill(ALL1, 1.0, S("tail_one"), list(Stage.free[0]) + list(Stage.free[1]))

        def tail_setup():
            i, bank = ring.take()
            PE.wait(*R4.ready)
            m = mm(bank[0:48, 0:128], WRT, AKT, True, True, S("t_pe"))
            a = act(RKT, bank[0:48, 0:128], ACTF.Copy, S("t_act"), [m] + list(Stage.free[0]) + list(Stage.free[1]))
            ring.release(i, a)
            i, bank = ring.take()
            for k in range(KT):
                m = mm(bank[0:32, 0:128], WVD[:, k, :], AVT[:, k, :], k == 0, k == 3, S("t_pe") if k == 3 else None)
            b = act(T1T, bank[0:32, 0:128], ACTF.Copy, S("t_act"), [m])
            ring.release(i, b)
            yield
            i, bank = ring.take()
            m = mm(bank[:, :], T1T, WVU, True, True, S("t_pe"), [b])
            b = act(AV3, bank[:, :], ACTF.Copy, S("t_act"), [m])
            ring.release(i, b)
            R4.setup = [a, b]

        def tail_front(c, todo=range(4)):
            ht, qy, rq, ug = tail_place(c)[0:4]
            ht = ht.rearrange("p (k t) -> p k t", k=4)
            r = ln_stats(c, todo)
            yield
            for half in range(2):
                tiles, ns = (2 * half, 2 * half + 1), []
                for t in tiles:
                    ns.append(ts(LNB[:, t % 2, :], X[:, 4 * c + t, :], LNM[:, 2 * t:2 * t + 1], LNR[:, t:t + 1],
                                 ALU.subtract, ALU.mult, S("ln_x"), [r] + ln_free[t % 2]))
                lns_free[0] = [ns[-1]]
                vs = []
                for t, n in zip(tiles, ns):
                    b = LNB[:, t % 2, :]
                    vs.append(DVE_bn(LNS2[:, 6 * t:6 * t + 6], b, [n, R4.ones]))
                    xs = X[:, 4 * c + t, :]
                    XM[4 * c + t] = tt(xs, xs, b, ALU.add, S("x_add2"), [n], q=POOL)
                yield
                if half == 0:
                    yield
                for t, n, v in zip(tiles, ns, vs):
                    b = LNB[:, t % 2, :]
                    i, bank = ring.take()
                    for k in range(KT):
                        m = tp(bank[:, k * 128:(k + 1) * 128], b[:, k * 128:(k + 1) * 128], IDN, S("ln_t"), [n])
                    ln_free[t % 2] = [m, v, XM[4 * c + t]]
                    h = act(ht[:, :, t * 128:(t + 1) * 128], bank[:, :].rearrange("p (k t) -> p k t", k=4), ACTF.Copy,
                            S("t_act"), [m] + XT_used[c])
                    ring.release(i, h)
                yield
            for t in range(4):
                v = DVE_agg(LNM2[:, 2 * t:2 * t + 2], LNS2[:, 6 * t:6 * t + 6], [v])
            v = ts(VAR[:, 4 * c:4 * c + 4], LNM2[:, 1:8:2], 1.0, None, ALU.mult, None, S("t_dve"), [v])
            if c == NC - 1:
                R4.log = act(GATE, VAR[:, :], ACTF.Ln, S("t_act"), [v], bias=1.0, accum_out=TOT[:, 0:1])
            i, bq = ring.take()
            PE.wait(*R4.ready, h)
            for k in range(KT):
                m = mm(bq[0:64, :], WQM[:, k, :], ht[:, k, :], k == 0, k == 3, S("t_pe") if k == 3 else None)
            R4.q[c] = act(qy[0:64, :], bq[0:64, :], ACTF.Copy, S("t_act"), [m] + CT_used[c])
            ring.release(i, R4.q[c])
            yield
            i, bu = ring.take()
            for k in range(KT):
                m = mm(bu[:, :], WU1[:, k, :], ht[:, k, :], k == 0, k == 3, S("t_pe") if k == 3 else None)
            XT_used[c] = [m]
            R4.u[c] = act(ug, bu[:, :], ACTF.Gelu_apprx_tanh, S("t_act"), [m], bias=BU1)
            ring.release(i, R4.u[c])
            i, br_ = ring.take()
            m = mm(br_[0:48, :], WRT, qy[0:64, :], True, True, S("t_pe"), [R4.q[c]])
            R4.rq[c] = act(rq[0:48, :], br_[0:48, :], ACTF.Copy, S("t_act"), [m])
            ring.release(i, R4.rq[c])
            yield

        def tail_back(c):
            _, qy, rq, ug, a_, r_, s_, r2_, w_ = tail_place(c)
            a_, r_, s_, r2_ = [v.rearrange("p (t n) -> p t n", t=4) for v in (a_, r_, s_, r2_)]
            ir, b_r = ring.take()
            PE.wait(R4.q[c], R4.rq[c], *R4.setup)
            for t in range(4):
                tok = slice(t * 128, (t + 1) * 128)
                m1 = mm(b_r[:, tok], rq[0:48, tok], RKT, True, True, S("t_pe"))
            ia, b_a = ring.take()
            for t in range(4):
                tok = slice(t * 128, (t + 1) * 128)
                m2 = mm(b_a[:, tok], qy[0:64, tok], AKT, True, True, S("t_pe"))
            il, b_l = ring.take()
            PE.wait(R4.u[c])
            for t in range(4):
                m3 = mm(b_l[:, t:t + 1], ug[:, t * 128:(t + 1) * 128], WU2[:, 0:1], True, True, S("t_pe"))
            lrel = LREL.unsqueeze(1).to_broadcast([128, 4, NSLOT])
            a = stt(r_, b_r[:, :].rearrange("p (t n) -> p t n", t=4), float(1.0 / np.sqrt(np.float32(RDIM))), lrel,
                    ALU.mult, ALU.add, S("t_dve"), [m1] + XT_used[c])
            ring.release(ir, a)
            b = stt(a_, b_a[:, :].rearrange("p (t n) -> p t n", t=4), 0.125, lrel, ALU.mult, ALU.add, S("t_dve"), [m2])
            ring.release(ia, b)
            lg = ts(LGT[:, 4 * c:4 * c + 4], b_l[:, 0:4], BU2, None, ALU.add, None, S("t_dve"), [m3] + R4.ready)
            R4.lg = [lg]
            ring.release(il, lg)
            yield
            for t in range(4):
                x = top8(M8[:, 8 * t:8 * t + 8], r_[:, t, :], [a])
            for t in range(4):
                x = strike(r2_[:, t, :], M8[:, 8 * t:8 * t + 8], r_[:, t, :], [x])
            yield
            x = tt(s_, r2_, r_, ALU.not_equal, S("t_dve"), [x])
            y = ts(r2_, s_, 1.0, BIG, ALU.subtract, ALU.mult, S("t_dve"), [x])
            x = tt(a_, a_, s_, ALU.mult, S("t_dve"), [b, x])
            x = tt(a_, a_, r2_, ALU.add, S("t_dve"), [x, y])
            yield
            x = red(MX4, a_, ALU.max, S("t_dve"), [x])
            x = tt(a_, a_, MX4.unsqueeze(2).to_broadcast([128, 4, NSLOT]), ALU.subtract, S("t_dve"), [x])
            x = act(a_, a_, ACTF.Exp, S("t_act"), [x])
            yield
            x = red(SM4, a_, ALU.add, S("t_dve"), [x])
            x = recip(RC4, SM4, S("t_dve"), [x])
            x = tt(a_, a_, RC4.unsqueeze(2).to_broadcast([128, 4, NSLOT]), ALU.mult, S("t_dve"), [x])
            yield
            yield
            i, bank = ring.take()
            for t in range(4):
                m = tp(bank[:, t * 128:(t + 1) * 128], a_[:, t, :], IDN, S("t_pe"), [x])
            R4.w[c] = act(w_, bank[:, :], ACTF.Copy, S("t_act"), [m])
            ring.release(i, R4.w[c])
            yield

        def tail_values(t):
            i, bank = ring.take()
            c = t // 4
            w_ = tail_place(c)[8]
            m = mm(bank[:, :], w_[:, (t % 4) * 128:(t % 4 + 1) * 128], AV3, True, True, S("t_pe"), [R4.w[c]])
            return t, i, bank, m

        def tail_out(gm, t, i, bank, m):
            xs = X[:, t, :]
            XM[t] = stt(xs, bank[:, :], GATE[:, t:t + 1], xs, ALU.mult, ALU.add, S("fin"), [gm, m, XM[t]])
            ring.release(i, XM[t])

        def top8(o, i, w):
            DVE.wait(*w)
            return DVE.put(lambda e: e.max(o, i), S("t_dve"))

        def strike(o, v, i, w):
            DVE.wait(*w)
            return DVE.put(lambda e: e.match_replace(o, v, i, -3e38), S("t_dve"))

        def gates():
            i, bank = ring.take()
            x = R4.log
            m = mm(bank[:, 0:1], ALL1, TOT[:, 0:1], True, True, S("t_pe"), [x, R4.ones])
            y = ts(TOT[:, 1:2], bank[:, 0:1], 1.0 / T, 1e-6, ALU.mult, ALU.add, S("t_dve"), [m])
            ring.release(i, y)
            y = recip(TOT[:, 2:3], TOT[:, 1:2], S("t_dve"), [y])
            y = ts(GATE, GATE, TOT[:, 2:3], 0.5, ALU.mult, ALU.mult, S("t_dve"), [y, x])
            z = act(VAR, LGT, ACTF.Sigmoid, S("t_act"), [x] + R4.lg)
            y = stt(GATE, VAR, 2.5, GATE, ALU.mult, ALU.add, S("t_dve"), [y, z])
            y = ts(GATE, GATE, 0.0, 5.0, ALU.max, ALU.min, S("t_dve"), [y])
            y = ts(GATE, GATE, 0.5, 1.0 / 1.5, ALU.subtract, ALU.mult, S("t_dve"), [y])
            y = ts(GATE, GATE, 0.0, 1.0, ALU.max, ALU.min, S("t_dve"), [y])
            z = act(VAR, GATE, ACTF.Sigmoid, S("t_act"), [y], scale=GWT, bias=GBT)
            return stt(GATE, VAR, 0.05, VAR, ALU.is_ge, ALU.mult, S("t_dve"), [z])

        late_prep = [prep_steps(1, NKV - 1, k) for k in range(3)]
        front2, back2 = tail_front(2), tail_back(2)
        front3, back3 = tail_front(3, ()), tail_back(3)

        def during1(u):
            g, c = units1[u]
            if u < 8:
                return (lambda: chain(ln_b[1], wo_b), lambda: half_norm(ln_b[2], True), lambda: half_norm(ln_b[2], False),
                        lambda: half_norm(ln_b[3], True), lambda: half_norm(ln_b[3], False), lambda: iter(()), lambda: chain(wkv_c, wq_c),
                        lambda: after_output(wo_c))[u]()
            if g + 1 < NKV - 1 and c < 3:
                return prep_steps(1, g + 1, c)
            if u == 23:
                return chain(late_prep[0], late_prep[1])
            if STAGES >= 4:
                if u == 24:
                    return chain(after_output(late_prep[2]), call(tail_loads))
                if u == 25:
                    return tail_setup()
                if u in (27, 29):
                    return tail_front((u - 27) // 2)
                if u in (28, 30):
                    return tail_back((u - 28) // 2)
                if u == 31:
                    return chain(empty(), some(front2, 2))
            elif u == 24:
                return after_output(late_prep[2])
            return iter(())

        def after_last1(t):
            if STAGES >= 4:
                if t > 0:
                    next(front2)
                tile_stats(NC - 1, t)

        if STAGES >= 1:
            start0()

        if STAGES >= 2:
            ends = G.qt_used + G.kt_used + G.v_used[0] + G.v_used[1] + G.pt_used + G.at_used + G.ss_free + \
                G.m1_free[0] + G.m1_free[1] + G.rt_free[0] + G.rt_free[1] + G.kf_free
            Stage.free[6] = ends
            for i in range(2):
                F.gu_used[i] = F.d_used[i] = F.h_used[i] = F.sg_free[i] = ends
            feed = ffn(during_ffn)
            next(feed)
            if STAGES >= 3:
                G.qt_used = G.kt_used = G.v_used[0] = F.gu0_used
                second = attention(1, units1, during1, lambda u: u in (0, 6, 23) or 27 <= u <= 30, after_last1)
                next(second)
            finish(feed)
            if STAGES >= 3:
                G.rt_free[0] = G.rt_free[1] = G.ss_free = G.sq_used = G.pt_used = G.at_used = F.last
                finish(second)

        ov = out.rearrange("(t p) d -> p t d", p=128)
        if STAGES >= 4:
            for steps in (front2, front3, front2, front3, front3, front3, front3, front3, front2, back2, front3,
                          back2, back2, back2, front3, back2, back2, back3, back2):
                next(steps, None)
            gm = gates()
            ready = [tail_values(t) for t in range(6)]
            finish(back3)
            for t in range(6, 16):
                tail_out(gm, *ready.pop(0))
                ready.append(tail_values(t))
            for r in ready:
                tail_out(gm, *r)

        for t in range(16):
            dma(ov[:, t, :], X[:, t, :], S("out"), [XM[t]])
        SP.wait((S("out"), S("out").count))

        block = ctx.enter_context(nc.Block())
        block.sync(SP.run)
        block.tensor(PE.run)
        block.scalar(ACT.run)
        block.vector(DVE.run)
        block.gpsimd(POOL.run)


def _constants():
    f = np.float32
    inv = f(1.0) / np.power(f(10000.0), np.arange(0, DH, 2, dtype=f) / f(DH)).astype(f)
    ang = np.arange(SQ, dtype=f)[:, None] * inv[None, :]
    cos = np.concatenate([np.cos(ang), np.cos(ang)], axis=-1).astype(f)
    sin = np.concatenate([-np.sin(ang), np.sin(ang)], axis=-1).astype(f)
    c = np.zeros((128, 260), f)
    c[:, 0:128] = np.eye(128)
    c[:, 128:192] = cos.T
    c[:, 192:256] = sin.T
    p = np.arange(128)
    c[:, 256] = np.where((p % 32 < 4) & (p < 64), p % 32, -1)
    c[:, 257] = np.where((p % 32 < 10) & (p < 64), p % 32, -1)
    return c, (4 * (p % 8)).astype(np.uint32).reshape(128, 1)


def kernel(**inputs):
    import concourse.bacc as bacc
    from concourse.bass_utils import run_bass_kernel_spmd

    a = {k: np.asarray(v) for k, v in inputs.items()}
    cf, cu = _constants()
    arrays = {
        "const_f": cf,
        "const_u": cu,
        "x": a["x"].reshape(T, D),
        "ctxT": a["ctx_4096"].reshape(T, D).T,
        "mask0": a["mask_BxSxS2_ff1"],
        "mask1": a["mask_1x1xSxS2_ff0"].reshape(SQ, SQ),
        "scales_gu": a["L0_ffn_scales_gu"], "scales_d": a["L0_ffn_scales_down"],
        "qzeros_gu": a["L0_ffn_qzeros_gu"], "qzeros_d": a["L0_ffn_qzeros_down"],
        "qw_gu": a["L0_ffn_qweight_gu"], "qw_d": a["L0_ffn_qweight_down"],
        "gidx_gu": a["L0_ffn_g_idx_gu"], "gidx_d": a["L0_ffn_g_idx_down"],
        "wq0": a["L0_xattn_wq"], "wk0": a["L0_xattn_wk"], "wv0": a["L0_xattn_wv"], "wo0": a["L0_xattn_wo"],
        "wq1": a["L1_xattn_q_proj_w"].T, "wk1": a["L1_xattn_k_proj_w"].T, "wv1": a["L1_xattn_v_proj_w"].T,
        "wo1": a["L1_xattn_o_proj_w"].T, "qnw": a["L1_xattn_q_norm_w"].reshape(1, 128),
        "knw": a["L1_xattn_k_norm_w"].reshape(1, 128),
        "wqm": a["L1_ffn_Wq"].T, "wu1": a["L1_ffn_Wu1"].T, "avT": a["L1_ffn_aux_values"].T,
        "wvd": a["L1_ffn_Wvd"].T, "wrT": a["L1_ffn_Wr"].T, "akT": a["L1_ffn_aux_keys"].T,
        "wvu": a["L1_ffn_Wvu"].T, "wu2": a["L1_ffn_Wu2"].T, "bu1": a["L1_ffn_bu1"].reshape(128, 1),
        "log_rel": a["L1_ffn_log_rel"].reshape(1, NSLOT), "bu2": a["L1_ffn_bu2"].reshape(1, 1),
        "gate_w1": a["L1_ffn_gate_w1"].reshape(1, 1), "gate_bias": a["L1_ffn_gate_bias"].reshape(1, 1),
    }
    arrays = {k: np.ascontiguousarray(v) for k, v in arrays.items()}
    nc = bacc.Bacc("TRN2", target_bir_lowering=False, num_devices=1)
    din = {k: nc.dram_tensor("in_" + k, v.shape, mybir.dt.from_np(v.dtype), kind="ExternalInput").ap()
           for k, v in arrays.items()}
    out = nc.dram_tensor("out_x", (T, D), F32, kind="ExternalOutput").ap()
    build(nc, din, out)
    r = run_bass_kernel_spmd(nc, [{"in_" + k: v for k, v in arrays.items()}], core_ids=[0])
    return r.results[0]["out_x"].reshape(NB, SQ, D)
```
